# Optimizing a Trainium2 kernel written in Bass

```python
import numpy as np
import jax
import jax.numpy as jnp

def _softmax(x, axis=-1):
    return jax.nn.softmax(x, axis=axis)

def _gelu(x):
    return jax.nn.gelu(x, approximate=True)

def _silu(x):
    return jax.nn.silu(x)

def _sigmoid(x):
    return jax.nn.sigmoid(x)

def _layernorm(x, axis=-1, eps=1e-05):
    m = jnp.mean(x, axis=axis, keepdims=True)
    v = jnp.var(x, axis=axis, keepdims=True)
    return (x - m) / jnp.sqrt(v + eps)

def _scatter_add(tgt, idx, src, axis=0):
    return tgt.at[idx].add(src)

def _segment_sum(src, seg, n):
    return jax.ops.segment_sum(src, seg, n)
kernel_name = 'mk_flamingo_gated_d2_seqx_r8_884562'

def setup_inputs(seed: int=0):
    np.random.seed(seed)
    _w = jnp.asarray

    def _rec_inputs():
        import jax
        import jax.numpy as jnp
        _rk = jax.random.key(seed)
        x = 7.22e-05 + 1 * jax.random.normal(jax.random.fold_in(_rk, 1), (16, 128, 256), jnp.float32)
        _lenS = 128 - jax.random.randint(jax.random.fold_in(_rk, 7), (16,), 0, max(1, 128 // 4) + 1, jnp.int32)
        _lenS2 = 128 - jax.random.randint(jax.random.fold_in(_rk, 8), (16,), 0, max(1, 128 // 4) + 1, jnp.int32)
        _ctx_2048P = jax.random.normal(jax.random.fold_in(_rk, 11), (16, 16, 256), jnp.float32)
        _ctx_2048c = jax.random.dirichlet(jax.random.fold_in(_rk, 511), 0.3 * jnp.ones((16,), jnp.float32), (16, 128))
        _ctx_2048t = jnp.einsum('bsk,bkd->bsd', _ctx_2048c, _ctx_2048P)
        _ctx_2048t = _ctx_2048t * jax.lax.rsqrt(jnp.mean(jnp.square(_ctx_2048t)) + 1e-12) * 0.953939
        ctx_2048 = 4.13588e-05 + 0.999923 * (_ctx_2048t + 0.3 * jax.random.normal(jax.random.fold_in(_rk, 611), (16, 128, 256), jnp.float32))
        _g = jax.random.normal(jax.random.fold_in(_rk, 9001), (2, 2), jnp.float32)
        _g = jnp.sign(_g) * jnp.maximum(jnp.abs(_g), 1.0) + (_g == 0) * 1.0
        g_xattn = _g[0]
        g_ffn = _g[1]
        return (x, ctx_2048, g_xattn, g_ffn)
    x, ctx_2048, g_xattn, g_ffn = _rec_inputs()

    def _L0_xattn_setup():
        import jax, jax.numpy as jnp
        import numpy as np
        N_HEADS = 16
        K_CH = 128 // N_HEADS
        SCALE = 1.0 / np.sqrt(K_CH)
        key = jax.random.key(seed)
        ks = jax.random.split(key, 10)
        B, C, T = (4, 128, 256)
        Cout = 128
        xavier = lambda k, o, i: jax.random.uniform(k, (o, i), jnp.float32, -1.0, 1.0) * np.sqrt(6.0 / (o + i))
        return {'x': jax.random.normal(ks[0], (B, C, T), jnp.float32), 'c': jax.random.normal(ks[1], (B, C, T), jnp.float32), 'Wq': xavier(ks[2], C, C), 'bq': jnp.zeros((C,), jnp.float32), 'Wk': xavier(ks[3], C, C), 'bk': jnp.zeros((C,), jnp.float32), 'Wv': xavier(ks[4], C, C), 'bv': jnp.zeros((C,), jnp.float32), 'Wo': xavier(ks[5], Cout, C), 'bo': jnp.zeros((Cout,), jnp.float32)}
    _L0_xattn_all = _L0_xattn_setup()
    _L0_xattn_in = {k: v for k, v in _L0_xattn_all.items() if k in ('Wq', 'bq', 'Wk', 'bk', 'Wv', 'bv', 'Wo', 'bo')}
    del _L0_xattn_all

    def _L0_ffn_setup():
        import jax, jax.numpy as jnp
        import numpy as np
        E = 32
        G = 8
        TKG = 4
        K = 4
        D = 256
        H = 128
        HS = 512
        SCALE = 2.5
        CAP = 128

        def relu2(x):
            r = jnp.maximum(x, 0.0)
            return r * r

        def route_tokens(scores, bias_corr):
            T = scores.shape[0]
            scores_c = scores + bias_corr
            group_scores = jax.lax.top_k(scores_c.reshape(T, G, E // G), 2)[0].sum(-1)
            _, group_idx = jax.lax.top_k(group_scores, TKG)
            group_mask = jnp.zeros((T, G), scores.dtype).at[jnp.arange(T)[:, None], group_idx].set(1.0)
            score_mask = jnp.repeat(group_mask, E // G, axis=1)
            masked = jnp.where(score_mask > 0, scores_c, 0.0)
            _, topk_idx = jax.lax.top_k(masked, K)
            topk_w = jnp.take_along_axis(scores, topk_idx, axis=1)
            topk_w = topk_w / (topk_w.sum(-1, keepdims=True) + 1e-20)
            return (topk_idx, topk_w * SCALE)
        key = jax.random.key(seed)
        ks = jax.random.split(key, 6)
        B, S = (2, 256)
        return dict(hidden_states=jax.random.normal(ks[0], (B, S, D), jnp.float32), gate_w=jax.random.normal(ks[1], (E, D), jnp.float32) * 0.02, bias_corr=jnp.zeros((E,), jnp.float32), up_w=jax.random.normal(ks[2], (E, H, D), jnp.float32) * 0.02, down_w=jax.random.normal(ks[3], (E, D, H), jnp.float32) * 0.02, shared_up_w=jax.random.normal(ks[4], (HS, D), jnp.float32) * 0.02, shared_down_w=jax.random.normal(ks[5], (D, HS), jnp.float32) * 0.02)
    _L0_ffn_all = _L0_ffn_setup()
    _L0_ffn_in = {k: v for k, v in _L0_ffn_all.items() if k in ('gate_w', 'bias_corr', 'up_w', 'down_w', 'shared_up_w', 'shared_down_w')}
    del _L0_ffn_all

    def _L1_xattn_setup():
        import jax, jax.numpy as jnp
        import numpy as np
        N_HEAD = 8
        key = jax.random.key(seed)
        k1, k2, k3 = jax.random.split(key, 3)
        B, D, L = (4, 128, 256)
        q = jax.random.normal(k1, (B, D, L), dtype=jnp.float32)
        k = jax.random.normal(k2, (B, D, L), dtype=jnp.float32)
        v = jax.random.normal(k3, (B, D, L), dtype=jnp.float32)
        gamma = jnp.ones((), dtype=jnp.float32)
        return {'q': q, 'k': k, 'v': v, 'gamma': gamma}
    _L1_xattn_all = _L1_xattn_setup()
    _L1_xattn_in = {k: v for k, v in _L1_xattn_all.items() if k in ('gamma',)}
    del _L1_xattn_all

    def _L1_ffn_setup():
        import jax, jax.numpy as jnp
        import numpy as np
        H = 256
        I = 176
        E = 8
        TOP_K = 2
        N_SHARED = 2
        I_SH = I * N_SHARED
        NORM_TOPK = True

        def _moe_forward(hidden_states, gate_w, expert_gate, expert_up, expert_down, shared_gate, shared_up, shared_down):
            bsz, seq_len, hdim = hidden_states.shape
            x = hidden_states.reshape(-1, hdim)
            logits = x @ gate_w.T
            probs = jax.nn.softmax(logits, axis=-1)
            routing_weights, selected = jax.lax.top_k(probs, TOP_K)
            if NORM_TOPK:
                routing_weights = routing_weights / (routing_weights.sum(axis=-1, keepdims=True) + 1e-20)
            combine = jnp.sum(jax.nn.one_hot(selected, E, dtype=routing_weights.dtype) * routing_weights[..., None], axis=1)
            g_sh = x @ shared_gate.T
            u_sh = x @ shared_up.T
            out = jax.nn.silu(g_sh) * u_sh @ shared_down.T
            g = jnp.einsum('nh,eih->nei', x, expert_gate)
            u = jnp.einsum('nh,eih->nei', x, expert_up)
            y = jnp.einsum('nei,ehi->neh', jax.nn.silu(g) * u, expert_down)
            out = out + jnp.einsum('neh,ne->nh', y, combine)
            return out.reshape(bsz, seq_len, hdim)
        key = jax.random.key(seed)
        ks = jax.random.split(key, 8)
        s = 0.02
        return {'hidden_states': jax.random.normal(ks[0], (1, 128, H), dtype=jnp.float32), 'gate_w': jax.random.normal(ks[1], (E, H), dtype=jnp.float32) * s, 'expert_gate': jax.random.normal(ks[2], (E, I, H), dtype=jnp.float32) * s, 'expert_up': jax.random.normal(ks[3], (E, I, H), dtype=jnp.float32) * s, 'expert_down': jax.random.normal(ks[4], (E, H, I), dtype=jnp.float32) * s, 'shared_gate': jax.random.normal(ks[5], (I_SH, H), dtype=jnp.float32) * s, 'shared_up': jax.random.normal(ks[6], (I_SH, H), dtype=jnp.float32) * s, 'shared_down': jax.random.normal(ks[7], (H, I_SH), dtype=jnp.float32) * s}
    _L1_ffn_all = _L1_ffn_setup()
    _L1_ffn_in = {k: v for k, v in _L1_ffn_all.items() if k in ('gate_w', 'expert_gate', 'expert_up', 'expert_down', 'shared_gate', 'shared_up', 'shared_down')}
    del _L1_ffn_all
    return {'x': x, 'ctx_2048': ctx_2048, 'g_xattn': g_xattn, 'g_ffn': g_ffn, 'L0_xattn_Wq': _L0_xattn_in['Wq'], 'L0_xattn_bq': _L0_xattn_in['bq'], 'L0_xattn_Wk': _L0_xattn_in['Wk'], 'L0_xattn_bk': _L0_xattn_in['bk'], 'L0_xattn_Wv': _L0_xattn_in['Wv'], 'L0_xattn_bv': _L0_xattn_in['bv'], 'L0_xattn_Wo': _L0_xattn_in['Wo'], 'L0_xattn_bo': _L0_xattn_in['bo'], 'L0_ffn_gate_w': _L0_ffn_in['gate_w'], 'L0_ffn_bias_corr': _L0_ffn_in['bias_corr'], 'L0_ffn_up_w': _L0_ffn_in['up_w'], 'L0_ffn_down_w': _L0_ffn_in['down_w'], 'L0_ffn_shared_up_w': _L0_ffn_in['shared_up_w'], 'L0_ffn_shared_down_w': _L0_ffn_in['shared_down_w'], 'L1_xattn_gamma': _L1_xattn_in['gamma'], 'L1_ffn_gate_w': _L1_ffn_in['gate_w'], 'L1_ffn_expert_gate': _L1_ffn_in['expert_gate'], 'L1_ffn_expert_up': _L1_ffn_in['expert_up'], 'L1_ffn_expert_down': _L1_ffn_in['expert_down'], 'L1_ffn_shared_gate': _L1_ffn_in['shared_gate'], 'L1_ffn_shared_up': _L1_ffn_in['shared_up'], 'L1_ffn_shared_down': _L1_ffn_in['shared_down']}

def reference(x, ctx_2048, g_xattn, g_ffn, L0_xattn_Wq, L0_xattn_bq, L0_xattn_Wk, L0_xattn_bk, L0_xattn_Wv, L0_xattn_bv, L0_xattn_Wo, L0_xattn_bo, L0_ffn_gate_w, L0_ffn_bias_corr, L0_ffn_up_w, L0_ffn_down_w, L0_ffn_shared_up_w, L0_ffn_shared_down_w, L1_xattn_gamma, L1_ffn_gate_w, L1_ffn_expert_gate, L1_ffn_expert_up, L1_ffn_expert_down, L1_ffn_shared_gate, L1_ffn_shared_up, L1_ffn_shared_down):
    import jax
    import jax.numpy as jnp

    def _L0_xattn_ref(x, c, Wq, bq, Wk, bk, Wv, bv, Wo, bo):
        import jax, jax.numpy as jnp
        import numpy as np
        N_HEADS = 16
        K_CH = 128 // N_HEADS
        SCALE = 1.0 / np.sqrt(K_CH)
        B, C, T = x.shape
        H, K = (N_HEADS, K_CH)
        q = jnp.einsum('oc,bct->bot', Wq, x) + bq[None, :, None]
        k = jnp.einsum('oc,bct->bot', Wk, c) + bk[None, :, None]
        v = jnp.einsum('oc,bct->bot', Wv, c) + bv[None, :, None]
        q = q.reshape(B, H, K, T)
        k = k.reshape(B, H, K, -1)
        v = v.reshape(B, H, K, -1)
        scores = jnp.einsum('bhkt,bhks->bhts', q, k) * SCALE
        p = jax.nn.softmax(scores, axis=-1)
        out = jnp.einsum('bhts,bhks->bhkt', p, v)
        out = out.reshape(B, H * K, T)
        return jnp.einsum('oc,bct->bot', Wo, out) + bo[None, :, None]

    def _L0_ffn_ref(hidden_states, gate_w, bias_corr, up_w, down_w, shared_up_w, shared_down_w):
        import jax, jax.numpy as jnp
        import numpy as np
        E = 32
        G = 8
        TKG = 4
        K = 4
        D = 256
        H = 128
        HS = 512
        SCALE = 2.5
        CAP = 128

        def relu2(x):
            r = jnp.maximum(x, 0.0)
            return r * r

        def route_tokens(scores, bias_corr):
            T = scores.shape[0]
            scores_c = scores + bias_corr
            group_scores = jax.lax.top_k(scores_c.reshape(T, G, E // G), 2)[0].sum(-1)
            _, group_idx = jax.lax.top_k(group_scores, TKG)
            group_mask = jnp.zeros((T, G), scores.dtype).at[jnp.arange(T)[:, None], group_idx].set(1.0)
            score_mask = jnp.repeat(group_mask, E // G, axis=1)
            masked = jnp.where(score_mask > 0, scores_c, 0.0)
            _, topk_idx = jax.lax.top_k(masked, K)
            topk_w = jnp.take_along_axis(scores, topk_idx, axis=1)
            topk_w = topk_w / (topk_w.sum(-1, keepdims=True) + 1e-20)
            return (topk_idx, topk_w * SCALE)
        B, S, _ = hidden_states.shape
        T = B * S
        flat = hidden_states.reshape(T, D)
        logits = flat @ gate_w.T
        scores = jax.nn.sigmoid(logits)
        topk_idx, topk_w = route_tokens(scores, bias_corr)
        e_flat = topk_idx.reshape(-1)
        oh = jax.nn.one_hot(e_flat, E, dtype=jnp.int32)
        pos = jnp.take_along_axis(jnp.cumsum(oh, axis=0) - 1, e_flat[:, None], axis=1)[:, 0]
        tok = jnp.repeat(jnp.arange(T), K)
        valid = pos < CAP
        xe = jnp.zeros((E, CAP, D), flat.dtype).at[e_flat, pos].set(flat[tok], mode='drop')
        h = relu2(jnp.einsum('ecd,ehd->ech', xe, up_w))
        ye = jnp.einsum('ech,edh->ecd', h, down_w)
        gathered = ye[e_flat, jnp.minimum(pos, CAP - 1)]
        gathered = jnp.where(valid[:, None], gathered, 0.0) * topk_w.reshape(-1)[:, None]
        routed = gathered.reshape(T, K, D).sum(axis=1).reshape(B, S, D)
        shared = relu2(hidden_states @ shared_up_w.T) @ shared_down_w.T
        return routed + shared

    def _L1_xattn_ref(q, k, v, gamma):
        import jax, jax.numpy as jnp
        import numpy as np
        N_HEAD = 8
        B, Dq, Lq = q.shape
        Dv, Lk = (v.shape[-2], v.shape[-1])
        h = N_HEAD
        dq = Dq // h
        dv = Dv // h
        qh = q.reshape(B, h, dq, Lq)
        kh = k.reshape(B, h, dq, Lk)
        vh = v.reshape(B, h, dv, Lk)
        scale = 1.0 / jnp.sqrt(jnp.asarray(dq, dtype=q.dtype))
        qk = jnp.einsum('bhdq,bhdl->bhql', qh, kh) * scale
        sm = jax.nn.softmax(qk, axis=-1)
        ret = jnp.einsum('bhql,bhdl->bhdq', sm, vh)
        ret = ret.reshape(B, Dv, Lq)
        return gamma * ret

    def _L1_ffn_ref(hidden_states, gate_w, expert_gate, expert_up, expert_down, shared_gate, shared_up, shared_down):
        import jax, jax.numpy as jnp
        import numpy as np
        H = 256
        I = 176
        E = 8
        TOP_K = 2
        N_SHARED = 2
        I_SH = I * N_SHARED
        NORM_TOPK = True

        def _moe_forward(hidden_states, gate_w, expert_gate, expert_up, expert_down, shared_gate, shared_up, shared_down):
            bsz, seq_len, hdim = hidden_states.shape
            x = hidden_states.reshape(-1, hdim)
            logits = x @ gate_w.T
            probs = jax.nn.softmax(logits, axis=-1)
            routing_weights, selected = jax.lax.top_k(probs, TOP_K)
            if NORM_TOPK:
                routing_weights = routing_weights / (routing_weights.sum(axis=-1, keepdims=True) + 1e-20)
            combine = jnp.sum(jax.nn.one_hot(selected, E, dtype=routing_weights.dtype) * routing_weights[..., None], axis=1)
            g_sh = x @ shared_gate.T
            u_sh = x @ shared_up.T
            out = jax.nn.silu(g_sh) * u_sh @ shared_down.T
            g = jnp.einsum('nh,eih->nei', x, expert_gate)
            u = jnp.einsum('nh,eih->nei', x, expert_up)
            y = jnp.einsum('nei,ehi->neh', jax.nn.silu(g) * u, expert_down)
            out = out + jnp.einsum('neh,ne->nh', y, combine)
            return out.reshape(bsz, seq_len, hdim)
        return _moe_forward(hidden_states, gate_w, expert_gate, expert_up, expert_down, shared_gate, shared_up, shared_down)
    x = x + jnp.tanh(g_xattn[0]) * _L0_xattn_ref(_layernorm(x, axis=-1), ctx_2048, L0_xattn_Wq, L0_xattn_bq, L0_xattn_Wk, L0_xattn_bk, L0_xattn_Wv, L0_xattn_bv, L0_xattn_Wo, L0_xattn_bo)
    x = x + jnp.tanh(g_ffn[0]) * _L0_ffn_ref(_layernorm(x, axis=-1), L0_ffn_gate_w, L0_ffn_bias_corr, L0_ffn_up_w, L0_ffn_down_w, L0_ffn_shared_up_w, L0_ffn_shared_down_w)
    x = x + jnp.tanh(g_xattn[1]) * _L1_xattn_ref(_layernorm(x, axis=-1), ctx_2048, ctx_2048, L1_xattn_gamma)
    x = x + jnp.tanh(g_ffn[1]) * _L1_ffn_ref(_layernorm(x, axis=-1), L1_ffn_gate_w, L1_ffn_expert_gate, L1_ffn_expert_up, L1_ffn_expert_down, L1_ffn_shared_gate, L1_ffn_shared_up, L1_ffn_shared_down)
    return x

_drawn_inputs = setup_inputs


def setup_inputs(seed=0):
    import zlib

    import numpy as np

    out = dict(_drawn_inputs(seed))
    spreads = {'g_ffn': (-1.0, 0.6),
     'L0_xattn_bq': (0.0, 0.313),
     'L0_xattn_bk': (0.0, 2.0),
     'L0_xattn_bv': (0.0, 0.329),
     'L0_xattn_bo': (0.0, 0.319),
     'L0_ffn_bias_corr': (0.0, 0.439)}
    factors = {'L0_ffn_gate_w': 4.441,
     'L0_ffn_up_w': 4.356,
     'L0_ffn_down_w': 4.02,
     'L1_ffn_gate_w': 6.779,
     'L1_ffn_expert_gate': 5.969,
     'L1_ffn_expert_up': 5.887,
     'L1_ffn_expert_down': 5.883,
     'L1_ffn_shared_gate': 2.998,
     'L1_ffn_shared_up': 2.967,
     'L1_ffn_shared_down': 2.973}
    for name, (base, spread) in spreads.items():
        noise = np.random.default_rng([zlib.crc32(name.encode()), seed]).standard_normal(out[name].shape)
        drawn = base * np.exp(spread * noise) if base else spread * noise
        out[name] = jnp.asarray(drawn.astype(out[name].dtype))
    for name, factor in factors.items():
        out[name] = (out[name] * factor).astype(out[name].dtype)
    return out
```

```python
from contextlib import ExitStack

import numpy as np
import concourse.bass as bass
from concourse import mybir

F32 = mybir.dt.float32
BF16 = mybir.dt.bfloat16
U32 = mybir.dt.uint32
I32 = mybir.dt.int32
ALU = mybir.AluOpType
ACT = mybir.ActivationFunctionType
AX = mybir.AxisListType
P = 128
ENGINES = ("pe", "dve", "act", "pool", "sp")


class Queue:

    def __init__(self, nc, ctx):
        self.nc, self.ctx = nc, ctx
        self.sem = {}
        self.phases = []
        self.sem["pad"] = ctx.enter_context(nc.semaphore("s_pad"))

    def channel(self, name):
        if name not in self.sem:
            self.sem[name] = self.ctx.enter_context(self.nc.semaphore("s_" + name))
        return name

    def phase(self, n=1):
        self.phases.append(dict(n=n, lags={0}, ops={e: [] for e in ENGINES}, at={}, count={}))

    def op(self, engine, name, fn, after=(), lag=0, channel=None, apart=False):
        ph = self.phases[-1]
        ch = self.channel(channel or engine)
        k = ph["count"].get(ch, 0)
        ph["count"][ch] = k + 1
        ph["lags"].add(lag)
        assert name not in ph["at"], name
        ph["at"][name] = (ch, k)
        ph["ops"][engine].append((name, ch, k, fn, [(a, 0) if isinstance(a, str) else a for a in after], lag, apart))

    def emit(self):
        total = {c: 0 for c in self.sem if c != "pad"}
        step = {c: 1 if c in ENGINES else 16 for c in total}
        plans = []
        for ph in self.phases:
            runs = ph["n"] + max(ph["lags"]) - min(ph["lags"])
            start = dict(total)
            for c, m in ph["count"].items():
                total[c] += m * runs
            plans.append((ph, runs, start, dict(total)))
        programs = {}
        for e in ENGINES:
            programs[e] = self._program(e, plans, step)
        with self.nc.Block() as block:
            for e in ("sp", "pool", "act", "pe", "dve"):
                of_block(block, e)(programs[e])

    def _program(self, e, plans, step):
        q = self

        def program(eng):
            seen = {}

            def wait(sem, value):
                if isinstance(value, int):
                    if value <= 0 or seen.get(sem, 0) >= value:
                        return
                    seen[sem] = value
                eng.wait_ge(q.sem[sem], value)
                if e == "sp" and not isinstance(value, int):
                    eng.sem_inc(q.sem["pad"], 1)

            for n_ph, (ph, runs, start, end) in enumerate(plans):
                if n_ph and ph["ops"][e]:
                    for c, v in start.items():
                        if v and not c.startswith("w_"):
                            wait(c, v * step[c])

                def iteration(r, i):
                    skipped = {}
                    inside = {}

                    def flush(c):
                        if skipped.get(c):
                            base = start[c] + ph["count"][c] * r
                            k0, m = skipped.pop(c)
                            wait(c, (base + k0) * step[c])
                            eng.sem_inc(q.sem[c], m * step[c])

                    issued = set()
                    for name, ch, k, fn, after, lag, apart in ph["ops"][e]:
                        if isinstance(i, int) and not 0 <= i - lag < ph["n"]:
                            k0, m = skipped.get(ch, (k, 0))
                            skipped[ch] = (k0, m + 1)
                            continue
                        for c in list(skipped):
                            flush(c)
                        need = {}
                        for a, d in after:
                            if a.startswith("w_"):
                                need[a] = max(need.get(a, 0), d) if d else end[a] * step[a]
                                continue
                            c, ka = ph["at"][a]
                            off = start[c] + ka + 1 - d * ph["count"][c]
                            need[c] = max(need.get(c, -10**9), off)
                        for c, off in need.items():
                            if c.startswith("w_"):
                                wait(c, off)
                                continue
                            if isinstance(r, int):
                                v = off + ph["count"][c] * r
                                if off + ph["count"][c] * r > start[c]:
                                    wait(c, v * step[c])
                            elif off > inside.get(c, -10**9):
                                inside[c] = off
                                wait(c, (r * ph["count"][c] + off) * step[c])
                        if apart and e != "sp" and not isinstance(r, int) and need:
                            eng.sem_inc(q.sem["pad"], 1)
                        made = fn(eng, i)
                        made.then_inc(q.sem[ch], step[ch])
                    for c in list(skipped):
                        flush(c)

                if not ph["ops"][e]:
                    continue
                lo, hi = min(ph["lags"]), ph["n"] + max(ph["lags"])
                full = (max(ph["lags"]), ph["n"] + min(ph["lags"]))
                if full[0] == lo:
                    full = (lo + 1, full[1])
                for i in range(lo, min(full[0], hi)):
                    iteration(i - lo, i)
                if full[1] > full[0]:
                    with eng.Fori(full[0], full[1]) as i:
                        iteration(i - lo, i)
                    seen.clear()
                for i in range(max(full), hi):
                    iteration(i - lo, i)
            if e == "sp":
                for c, v in plans[-1][3].items():
                    wait(c, v * step[c])

        return program


def of_block(block, engine):
    return {"sp": block.sync, "pool": block.gpsimd, "act": block.scalar, "pe": block.tensor, "dve": block.vector}[engine]



NB, C, T = 16, 128, 256
E0, H0, CAP, K0 = 32, 128, 128, 4
HS = 512
E1, I1, ISH = 8, 176, 352
EPS = 1e-5
TERMS = ((0, 0), (1, 0), (2, 0), (0, 1), (1, 1), (0, 2))


class Attention:
    def __init__(self, name, H, R):
        self.name, self.H, self.R = name, H, R
        self.K = len(TERMS) * R
        self.J = 2 if self.K <= 64 else 1
        self.NG = H // self.J
        self.NQ = H // 4
        self.scale = float(R) ** -0.5

    def at(self, h, extra=0):
        j, g = divmod(h, self.NG)
        return slice(64 * j, 64 * j + self.K + extra), g

    def order(self, quad):
        c = (0, 2, 1, 3)
        return [(k, self.NQ * k + quad) for k in c]


def attention_half(q, A, M, hb):
    R, H, NQ, L0 = A.R, A.H, A.NQ, A.name == "L0"
    skew = {0: 3, 1: 2, 2: 1, 3: 0, 4: -1}
    B = {s: hb + k for s, k in skew.items()}
    lag = {s: -(b // 2) for s, b in B.items()}
    n0, n1, n2, n3, n4 = (B[s] % 2 for s in range(5))
    QS, QKc, QKs, VA, M1, PX = M["QS"], M["QKc"], M["QKs"], M["VA"], M["M1"], M["PX"]
    at = q.phases[-1]["at"]

    def of(kind, stage, batch, end=""):
        return (f"{kind}{batch % 2}{end}", -((batch - skew[stage]) // 2))

    def x_at(i, batch):
        return M["X"][:, bass.ds(i * 2 + batch, 1), :][:, 0, :]

    def back(kind, n, per):
        return (f"{kind}{n % (2 * per)}", 0 if n >= 0 else 1)

    def score(k):
        h = A.order(k // 4)[k % 4][1]
        n = hb * H + k
        rows, g = A.at(h)
        for a in range(2):
            q.op("pe", f"s{n}.{a}", lambda e, i, a=a: e.matmul(
                M["S"][n % 2][:, 256 * a:256 * a + 256], QS[n2][rows, g, 0, 128 * a:128 * a + 128],
                QS[n2][rows, g, 1, :], start=True, stop=True), after=[of("sp", 1, B[2]), back("max", n - 2, H)], lag=lag[2])
        q.op("dve", f"max{n}", lambda e, i: e.tensor_reduce(
            M["mx"][n2][:, :, h], M["S"][n % 2][:, :].rearrange("p (a s) -> p a s", a=2), AX.X, ALU.max, negate=True),
            after=[f"s{n}.1", of("mtT", 2, B[2] - 2, ".1")], lag=lag[2])

    def score_t(m):
        pair = hb * (H // 2) + m
        bank = M["ST"][pair % 2]
        for u in range(2):
            h = A.order(m // 2)[2 * (m % 2) + u][1]
            rows, g = A.at(h, 1)
            for a in range(2):
                q.op("pe", f"st{pair}.{u}{a}", lambda e, i, a=a, u=u, g=g, rows=rows: e.matmul(
                    bank[:, 512 * u + 256 * a:512 * u + 256 * a + 256], QS[n3][rows, g, 1, 128 * a:128 * a + 128],
                    QS[n3][rows, g, 0, :], start=True, stop=True),
                    after=[of("mrow", 2, B[3]), of("sp", 1, B[3]), back("exp", pair - 2, H // 2)])
        q.op("act", f"exp{pair}", lambda e, i: e.activation(PX[pair % 4][:, :], bank[:, :], ACT.Exp, scale=A.scale),
             after=[f"st{pair}.11", back("pv", hb * NQ + m // 2 - 2, NQ)])

    def values(quad):
        n = hb * NQ + quad
        O = M["O"]
        for a in range(2):
            for u in range(4):
                c, h = A.order(quad)[u]
                pair = hb * (H // 2) + 2 * quad + u // 2
                q.op("pe", f"pv{n}" if (a, u) == (1, 3) else f"pv{n}.{a}.{u}", lambda e, i, a=a, u=u, c=c, h=h, pair=pair: e.matmul(
                    O[32 * c:32 * c + 32, 256 * (quad % 2):256 * (quad % 2) + 256], VA[n3][:, a, h, :],
                    PX[pair % 4][:, 512 * (u % 2) + 256 * a:512 * (u % 2) + 256 * a + 256], start=(a == 0), stop=(a == 1)),
                    after=[f"exp{pair}", of("va", 2, B[3]), back("oe", (n - 2) // 2, NQ // 2)])
        if quad % 2 == 1:
            k = n // 2
            q.op("act", f"oe{k}", lambda e, i: e.activation(
                M["OS"][:, quad - 1:quad + 1, :], O[:, :].rearrange("p (g t) -> p g t", g=2), ACT.Copy),
                after=[f"pv{n}", of("num", 3, B[3] - 1, ".3"), of("den", 3, B[3] - 1)])

    def norm():
        n, g = n0, lag[0]
        Xb = lambda i: x_at(i, B[0])
        q.op("dve", f"bn{n}", lambda e, i: e.bn_stats(M["st6"][n][:, :], Xb(i)), after=["w_x"], lag=g)
        q.op("dve", f"bna{n}", lambda e, i: e.bn_aggr(M["mv"][n][:, :], M["st6"][n][:, :]), after=[f"bn{n}", of("xn", 0, B[0] - 2)], lag=g, apart=True)
        q.op("dve", f"ve{n}", lambda e, i: e.tensor_scalar(M["ve"][n][:, :], M["mv"][n][:, 1:2], EPS, None, ALU.add), after=[f"bna{n}"], lag=g)
        q.op("pool", f"rs{n}", lambda e, i: e.tensor_tensor(M["rs"][n][:, :], M["ve"][n][:, :], M["mhalf"][:, :], ALU.pow),
             after=[f"ve{n}", of("xn", 0, B[0] - 2)], lag=g)
        q.op("dve", f"xn{n}", lambda e, i: e.tensor_scalar(
            M["Xn"][:, :] if L0 else QKc[n][:, 0, :], Xb(i), M["mv"][n][:, 0:1], M["rs"][n][:, 0:1], ALU.subtract, ALU.mult),
            after=[f"rs{n}", of("qp", 0, B[0] - 1) if L0 else of("res2.", 0, B[0] - 2)], lag=g)

    def keys_in():
        n = n0
        q.op("sp", f"ldc{n}", lambda e, i: e.dma_start(
            M["Cb"][n][:, :], M["ctx_d"][:, bass.ds(i * 2 + B[0], 1), :][:, 0, :]),
             after=[of("vt", 2, B[0] - 2), of("kp" if L0 else "kc", 0, B[0] - 2)], lag=lag[0], channel=f"ldc{n}", apart=True)

    def project():
        n, g = n0, lag[0]
        free = [of("res2.", 0, B[0] - 2)]
        if L0:
            q.op("pe", f"qp{n}", lambda e, i: e.matmul(M1[:, 0:256], M["Wq"][:, :], M["Xn"][:, :], start=True, stop=True),
                 after=[f"xn{n}", "w_w", of("x", 4, B[4])], lag=g)
            q.op("pe", f"kp{n}", lambda e, i: e.matmul(M1[:, 256:512], M["Wk"][:, :], M["Cb"][n][:, :], start=True, stop=True),
                 after=[f"ldc{n}"], lag=g)
            q.op("act", f"qc{n}", lambda e, i: e.activation(QKc[n][:, 0, :], M1[:, 0:256], ACT.Identity, bias=M["bq"][:, 0:1]),
                 after=[f"kp{n}"] + free, lag=g)
            q.op("act", f"kc{n}", lambda e, i: e.activation(QKc[n][:, 1, :], M1[:, 256:512], ACT.Identity, bias=M["bk"][:, 0:1]),
                 after=[f"kp{n}"] + free, lag=g)
        else:
            q.op("act", f"kc{n}", lambda e, i: e.activation(QKc[n][:, 1, :], M["Cb"][n][:, :], ACT.Copy), after=[f"ldc{n}"] + free, lag=g)
            at[f"qc{n}"] = at[f"xn{n}"]
        part = lambda k: QKs[n][:, k, :, :]
        q.op("pool", f"cut0.{n}", lambda e, i: e.tensor_copy(part(0), QKc[n][:, :, :]),
             after=[f"qc{n}", f"kc{n}", of("sp", 1, B[0] - 2)], lag=g, apart=True)
        q.op("pool", f"res1.{n}", lambda e, i: e.tensor_tensor(QKc[n][:, :, :], QKc[n][:, :, :], part(0), ALU.subtract), after=[f"cut0.{n}"], lag=g)
        q.op("pool", f"cut1.{n}", lambda e, i: e.tensor_copy(part(1), QKc[n][:, :, :]), after=[f"res1.{n}"], lag=g, apart=True)
        q.op("pool", f"res2.{n}", lambda e, i: e.tensor_tensor(part(2), QKc[n][:, :, :], part(1), ALU.subtract), after=[f"cut1.{n}"], lag=g)

    def spread():
        n = n1
        w = 128 // A.J
        for k, (a, b) in enumerate(TERMS):
            for j in range(A.J):
                def f(e, i, k=k, j=j, a=a, b=b):
                    parts = QKs[n][w * j:w * j + w, :, :, :].rearrange("p k s t -> p (k s) t")
                    x, y = 2 * a, 2 * b + 1
                    pair = parts[:, x:y + 1:y - x, :] if y > x else parts[:, x:y - 1 if y else None:y - x, :]
                    return e.dma_start(QS[n][64 * j + R * k:64 * j + R * k + R, :, :, :], pair)
                end = (k, j) == (len(TERMS) - 1, A.J - 1)
                q.op("sp", f"sp{n}" if end else f"sp{n}.{k}{j}", f,
                     after=[of("res2.", 0, B[1]), of("st.done", 3, B[1] - 2)], lag=lag[1], channel=f"sp{n}")

    def values_in():
        n, g = n2, lag[2]
        for a in range(2):
            if L0:
                f = lambda e, i, a=a: e.matmul(M1[:, 128 * a:128 * a + 128], M["Cb"][n][:, 128 * a:128 * a + 128], M["Wv"][:, :], start=True, stop=True)
            else:
                f = lambda e, i, a=a: e.transpose(M1[:, 128 * a:128 * a + 128], M["Cb"][n][:, 128 * a:128 * a + 128], M["ident"][:, :])
            q.op("pe", f"vt{n}" if a else f"vt{n}.0", f, after=[of("ldc", 0, B[2]), of("mt", 2, B[2] - 1), "w_w"], lag=g)
        for a in range(2):
            def f(e, i, a=a):
                cols = M1[:, 128 * a:128 * a + 128]
                if L0:
                    v = lambda ap: ap.rearrange("p (c r g) -> p c g r", c=4, g=NQ)
                    o = VA[n][:, a, 0:H, 0:R].rearrange("p (c g) r -> p c g r", g=NQ)
                    return e.tensor_tensor(o, v(cols), v(M["bv"][:, :]), ALU.add)
                return e.tensor_copy(VA[n][:, a, 0:H, 0:R], cols.rearrange("p (r h) -> p h r", h=H))
            q.op("dve", f"va{n}" if a else f"va{n}.0", f, after=[f"vt{n}", of("pvl", 3, B[2] - 2)], lag=g)

    def maxima():
        n, g = n2, lag[2]
        for a in range(2):
            q.op("pe", f"mtT{n}.{a}", lambda e, i, a=a: e.transpose(
                M1[0:H, 256 + 128 * a:384 + 128 * a], M["mx"][n][:, a, 0:H], M["ident"][:, :]),
                after=[f"max{hb * H + H - 1}", of("on", 4, B[4])] + ([of("kc", 0, B[0])] if L0 else []), lag=g)
        q.op("act", f"mt{n}", lambda e, i: e.activation(M["mxT"][n][0:H, :], M1[0:H, 256:512], ACT.Copy),
             after=[f"mtT{n}.1", of("mrow", 2, B[2] - 2)], lag=g)
        rows = slice(A.K, 64 + A.K + 1, 64) if A.J == 2 else slice(A.K, A.K + 1)
        q.op("sp", f"mrow{n}", lambda e, i: e.dma_start(QS[n][rows, :, 0, :], M["mxT"][n][0:H, :]),
             after=[f"mt{n}", of("st.done", 3, B[2] - 2)], lag=g, channel=f"mrow{n}")

    W = 2 * H

    def heads_out():
        oe = f"oe{(hb * NQ + NQ - 1) // 2}"
        q.op("sp", f"den{hb}", lambda e, i: e.dma_start(M["dn"][:, 0:W], M["OS"][R:97 + R:32, 0:NQ, :]),
             after=[oe, of("rr", 4, B[3] - 1)], channel=f"den{hb}")
        for c in range(4):
            q.op("sp", f"num{hb}.{c}", lambda e, i, c=c: e.dma_start(
                M["on"][32 * c:32 * c + 32, :], M["OS"][32 * c:32 * c + R, 0:NQ, :]), after=[oe, of("pm", 4, B[3] - 1)], channel=f"num{hb}")

    def residual():
        n, g = n4, lag[4]
        dn, rdn, rd, on = M["dn"], M["rdn"], M["rd"], M["on"]
        q.op("dve", f"rr{n}", lambda e, i: e.reciprocal(rdn[:, 0:W], dn[:, 0:W]), after=[of("den", 3, B[4]), of("rT", 4, B[4] - 1)], lag=g)
        q.op("sp", f"rT{n}", lambda e, i: e.dma_start(M["rT"][0:H, :], rdn[:, 0:W]), after=[f"rr{n}", of("rb", 4, B[4] - 1)], channel=f"rT{n}", lag=g)

    def residual2():
        n, g = n4, lag[4]
        rd, on = M["rd"], M["on"]
        q.op("pe", f"rb{n}", lambda e, i: e.matmul(M1[:, 256:512], M["hb" + A.name][0:H, :], M["rT"][0:H, :], start=True, stop=True),
             after=[f"rT{n}", of("mt", 2, B[2] - 1), "w_w"], lag=g)
        q.op("dve", f"on{n}", lambda e, i: e.tensor_tensor(on[:, :], M1[:, 256:512], on[:, :], ALU.mult),
             after=[of("num", 3, B[4], ".3"), f"rb{n}"], lag=g)
        q.op("pe", f"pm{n}", lambda e, i: e.matmul(M1[:, 0:256], M["Wo" if L0 else "perm"][:, :], on[:, :], start=True, stop=True),
             after=[f"on{n}", of("va", 2, B[2])], lag=g)
        if L0:
            q.op("act", f"yb{n}", lambda e, i: e.activation(rd[:, :], M1[:, 0:256], ACT.Identity, bias=M["bog"][:, 0:1], scale=M["tg"][:, 0:1]),
                 after=[f"pm{n}", of("x", 4, B[4] - 1)], lag=g)
            q.op("dve", f"x{n}", lambda e, i: e.tensor_tensor(x_at(i, B[4]), x_at(i, B[4]), rd[:, :], ALU.add), after=[f"yb{n}"], lag=g)
        else:
            q.op("dve", f"x{n}", lambda e, i: e.scalar_tensor_tensor(
                out=x_at(i, B[4]), in0=M1[:, 0:256], scalar=M["tg"][:, 2:3], in1=x_at(i, B[4]), op0=ALU.mult, op1=ALU.add), after=[f"pm{n}"], lag=g)

    n_pairs, made = H // 2, 0
    for m in range(n_pairs):
        while made < 2 + (H - 2) * m // n_pairs:
            score(made)
            made += 1
        score_t(m)
        if m == 0:
            norm()
            values_in()
            keys_in()
            residual()
        if m == 1:
            residual2()
        if m == 2:
            project()
        if m % 2 == 1 and m >= 3:
            values(m // 2 - 1)
    at[f"st.done{n3}"] = at[f"st{hb * n_pairs + n_pairs - 1}.11"]
    spread()
    values(NQ - 1)
    at[f"pvl{n3}"] = at[f"pv{hb * NQ + NQ - 1}"]
    while made < H:
        score(made)
        made += 1
    heads_out()
    maxima()



GB = 4
NGRP = NB // GB


def layer_norm_batches(q, M, BK, pre):
    Xb = lambda i, b: M["X"][:, bass.ds(i * GB + b, 1), :][:, 0, :]
    Nb = lambda i, b: M["XN"][:, bass.ds(i * GB + b, 1), :][:, 0, :]
    st, mv = M["st4"], M["mv4"]
    for b in range(GB):
        q.op("dve", f"bn{b}", lambda e, i, b=b: e.bn_stats(st[:, b, :], Xb(i, b)), after=[("xn3", 1)])
    for b in range(GB):
        q.op("dve", f"bna{b}", lambda e, i, b=b: e.bn_aggr(mv[:, b, :], st[:, b, :]), after=[f"bn{b}"], apart=True)
    q.op("dve", "ve", lambda e, i: e.tensor_scalar(M["ve4"][:, :], mv[:, :, 1], EPS, None, ALU.add), after=["bna3"])
    q.op("pool", "rs", lambda e, i: e.tensor_tensor(M["rs4"][:, :], M["ve4"][:, :], M["mhalf4"][:, :], ALU.pow), after=["ve", ("xn3", 1)])
    for b in range(GB):
        q.op("dve", f"xn{b}", lambda e, i, b=b: e.tensor_scalar(
            Nb(i, b), Xb(i, b), mv[:, b, 0:1], M["rs4"][:, b:b + 1], ALU.subtract, ALU.mult), after=["rs"] + (["w_z"] if pre == "L0" else []))
    for b in range(GB):
        q.op("act", f"xc{b}", lambda e, i, b=b: e.activation(M["XC"][b % 2][:, :], Nb(i, b), ACT.Copy),
             after=[f"xn{b}", (f"tp{b - 2}.1", 0) if b >= 2 else (f"tp{b + 2}.1", 1)])
        for a in range(2):
            q.op("pe", f"tp{b}.{a}", lambda e, i, b=b, a=a: e.transpose(
                BK[a][:, 128 * b:128 * b + 128], M["XC"][b % 2][:, 128 * a:128 * a + 128], M["ident"][:, :]),
                after=[f"xc{b}", (f"xt{a}", 1), "w_w"])
    q.op("act", "xt0", lambda e, i: e.activation(M["XT"][:, 0, :], BK[0][:, :], ACT.Copy), after=["tp3.0", ("xt.read", 1)])
    q.op("dve", "xt1", lambda e, i: e.tensor_copy(M["XT"][:, 1, :], BK[1][:, :]), after=["tp3.1", ("xt.read", 1)])


def tokens(M, b, a):
    return M["XT"][:, a, 128 * b:128 * b + 128]


def shared0(q, M, BK):
    layer_norm_batches(q, M, BK, "L0")
    at = q.phases[-1]["at"]
    L = BK[2]
    for b in range(GB):
        for a in range(2):
            q.op("pe", f"lg{b}.{a}", lambda e, i, b=b, a=a: e.matmul(
                L[:, E0 * b:E0 * b + E0], tokens(M, b, a), M["GW"][:, a, :], start=(a == 0), stop=(a == 1)),
                after=["xt0", "xt1", ("lgc", 1), "w_w"])
    q.op("dve", "lgc", lambda e, i: e.tensor_copy(
        M["LG"][:, bass.ds(i * GB, GB), :], L[:, 0:GB * E0].rearrange("p (b e) -> p b e", b=GB)), after=["lg3.1"])
    for c in range(4):
        U = BK[3 + c % 2]
        for a in range(2):
            q.op("pe", f"up{c}.{a}", lambda e, i, c=c, a=a, U=U: e.matmul(
                U[:, :], M["SU"][:, a, 128 * c:128 * c + 128], M["XT"][:, a, :], start=(a == 0), stop=(a == 1)),
                after=["xt0", "xt1", (f"relu{c - 2}", 0) if c >= 2 else (f"relu{c + 2}", 1), "w_s0"])
        q.op("act", f"relu{c}", lambda e, i, c=c, U=U: e.activation(M["RL"][:, c, :], U[:, :], ACT.Relu), after=[f"up{c}.1", ("dn3.3", 1)])
        q.op("dve", f"sq{c}", lambda e, i, c=c: e.tensor_tensor(M["RL"][:, c, :], M["RL"][:, c, :], M["RL"][:, c, :], ALU.mult), after=[f"relu{c}"])
    at["xt.read"] = at["up3.1"]
    for b in range(GB):
        D = BK[5 + b % 2]
        for c in range(4):
            q.op("pe", f"dn{b}.{c}", lambda e, i, b=b, c=c, D=D: e.matmul(
                D[:, 0:256], M["RL"][:, c, 128 * b:128 * b + 128], M["SD"][:, c, :], start=(c == 0), stop=(c == 3)),
                after=["sq3", (f"xs{b - 2}", 0) if b >= 2 else (f"xs{b + 2}", 1), "w_s0"])
        X = lambda i, b=b: M["X"][:, bass.ds(i * GB + b, 1), :][:, 0, :]
        q.op("dve", f"xs{b}", lambda e, i, X=X, D=D: e.scalar_tensor_tensor(
            out=X(i), in0=D[:, 0:256], scalar=M["tg"][:, 1:2], in1=X(i), op0=ALU.mult, op1=ALU.add), after=[f"dn{b}.3"])


def chain(q, engine, steps, first=()):
    prev = list(first)
    for name, fn in steps:
        q.op(engine, name, lambda e, i, fn=fn: fn(e), after=prev)
        prev = [name]


def route0(q, M, BK):
    G, K = 8, K0
    LG = M["LG"]
    sc, sb, t = M["sc"], M["scb"], M["rt"]
    flat = lambda ap: ap[:, :, :].rearrange("p b e -> p (b e)")
    q.op("act", "sig", lambda e, i: e.activation(flat(sc), flat(LG), ACT.Sigmoid))
    bias = M["bc"][:, :].unsqueeze(1).to_broadcast([P, NB, E0])
    v4 = sb[:, :, :].rearrange("p b (g m) -> p (b g) m", m=4)
    hi1, lo1, hi2, lo2, gs = (t[k] for k in range(5))
    g3 = lambda ap: ap[:, :].rearrange("p (b g) -> p b g", g=G)
    other = g3(gs).unsqueeze(2).to_broadcast([P, NB, G, G])
    own = g3(gs).unsqueeze(3).to_broadcast([P, NB, G, G])
    lt = M["lt"][:, :, :].unsqueeze(1).to_broadcast([P, NB, G, G])
    big0, big1, oh = M["big0"], M["big1"], M["oh"]
    gg = lambda m: m[:, 0:NB * G * G].rearrange("p (b g h) -> p b g h", g=G, h=G)
    gg3 = lambda m: m[:, 0:NB * G * G].rearrange("p (x h) -> p x h", h=G)
    ke = lambda m: m[:, :].rearrange("p (b k e) -> p b k e", k=K, e=E0)
    TT = lambda o, a, b, op: (lambda e: e.tensor_tensor(o, a, b, op))
    chain(q, "dve", [
        ("bias", TT(sb[:, :, :], sc[:, :, :], bias, ALU.add)),
        ("hi1", TT(hi1[:, :], v4[:, :, 0], v4[:, :, 1], ALU.max)),
        ("lo1", TT(lo1[:, :], v4[:, :, 0], v4[:, :, 1], ALU.min)),
        ("hi2", TT(hi2[:, :], v4[:, :, 2], v4[:, :, 3], ALU.max)),
        ("lo2", TT(lo2[:, :], v4[:, :, 2], v4[:, :, 3], ALU.min)),
        ("lo", TT(lo1[:, :], lo1[:, :], lo2[:, :], ALU.max)),
        ("mid", TT(lo2[:, :], hi1[:, :], hi2[:, :], ALU.min)),
        ("second", TT(lo1[:, :], lo1[:, :], lo2[:, :], ALU.max)),
        ("first", TT(hi1[:, :], hi1[:, :], hi2[:, :], ALU.max)),
        ("gs", TT(gs[:, :], hi1[:, :], lo1[:, :], ALU.add)),
        ("eq", TT(gg(big0), other, own, ALU.is_equal)),
        ("eqlt", TT(gg(big0), gg(big0), lt, ALU.mult)),
        ("gt", TT(gg(big1), other, own, ALU.is_gt)),
        ("ahead", TT(gg(big0), gg(big0), gg(big1), ALU.add)),
        ("rank", lambda e: e.tensor_reduce(hi1[:, :], gg3(big0), AX.X, ALU.add)),
        ("gm", lambda e: e.tensor_scalar(hi1[:, :], hi1[:, :], 4.0, None, ALU.is_lt)),
        ("masked", TT(v4, v4, hi1[:, :].unsqueeze(2).to_broadcast([P, NB * G, 4]), ALU.mult)),
        ("masked0", lambda e: e.tensor_scalar(flat(sb), flat(sb), 0.0, None, ALU.add)),
    ], ["sig", "w_w"])
    for b in range(NB):
        q.op("dve", f"top{b}", lambda e, i, b=b: e.max(M["MV"][:, b, :], sb[:, b, :]), after=["masked0"])
    for b in range(NB):
        q.op("dve", f"idx{b}", lambda e, i, b=b: e.max_index(M["MI"][:, b, :], M["MV"][:, b, :], sb[:, b, :]), after=[f"top{b}"])
    idxf, w, pk, val, f0, f1 = (M["tk"][k] for k in range(6))
    io = M["iota"][:, :].unsqueeze(1).unsqueeze(1).to_broadcast([P, NB, K, E0])
    x4 = lambda m: m[:, :, :].unsqueeze(3).to_broadcast([P, NB, K, E0])
    xe = lambda m: m[:, :, :].unsqueeze(2).to_broadcast([P, NB, K, E0])
    red = lambda o, m: (lambda e: e.tensor_reduce(o[:, :, :], ke(m), AX.X, ALU.add))
    chain(q, "dve", [
        ("idxf", lambda e: e.tensor_copy(idxf[:, :, :], M["MI"][:, :, 0:K])),
        ("oh", TT(ke(oh), x4(idxf), io, ALU.is_equal)),
        ("A", lambda e: e.tensor_reduce(M["A"][:, :, :], oh[:, :].rearrange("p (b k e) -> p b e k", k=K, e=E0), AX.X, ALU.add)),
        ("Ab", lambda e: e.tensor_copy(flat(M["Ab"]), flat(M["A"]))),
        ("C0", lambda e: e.memset(M["C"][:, 0, :], 0.0)),
    ] + [(f"C{b}", TT(M["C"][:, b, :], M["C"][:, b - 1, :], M["A"][:, b - 1, :], ALU.add)) for b in range(1, NB)]
      + [("Cb", lambda e: e.tensor_copy(flat(M["Ab2"]), flat(M["C"])))], [f"idx{NB - 1}", "w_w"])
    q.op("pe", "pos0", lambda e, i: e.matmul(BK[0][:, :], M["before"][:, :], flat(M["Ab"]), start=True, stop=False), after=["Ab", "w_w"])
    q.op("pe", "pos1", lambda e, i: e.matmul(BK[0][:, :], M["ones"][:, :], flat(M["Ab2"]), start=False, stop=True), after=["Cb"])
    pos = M["pos"]
    chain(q, "dve", [
        ("wp", TT(ke(big1), ke(oh), xe(sc), ALU.mult)),
        ("w", red(w, big1)),
        ("posc", lambda e: e.tensor_copy(flat(pos), BK[0][:, :])),
        ("pp", TT(ke(big1), ke(oh), xe(pos), ALU.mult)),
        ("pk", red(pk, big1)),
        ("val", lambda e: e.tensor_scalar(val[:, :, :], pk[:, :, :], float(CAP), None, ALU.is_lt)),
        ("e128", lambda e: e.tensor_scalar(idxf[:, :, :], idxf[:, :, :], float(CAP), None, ALU.mult)),
        ("out", lambda e: e.tensor_scalar(f0[:, :, :], val[:, :, :], -2.0 * E0 * CAP, 2.0 * E0 * CAP, ALU.mult, ALU.add)),
        ("s0", TT(f0[:, :, :], f0[:, :, :], idxf[:, :, :], ALU.add)),
        ("s1", TT(f0[:, :, :], f0[:, :, :], pk[:, :, :], ALU.add)),
        ("si", lambda e: e.tensor_copy(M["SI"][:, :, :], f0[:, :, :])),
        ("g0", lambda e: e.tensor_scalar(f1[:, :, :], pk[:, :, :], float(CAP - 1), None, ALU.min)),
        ("g1", TT(f1[:, :, :], f1[:, :, :], idxf[:, :, :], ALU.add)),
        ("gi", lambda e: e.tensor_copy(M["GI"][:, :, :], f1[:, :, :])),
        ("ws", lambda e: e.tensor_reduce(M["ws"][:, :], w[:, :, :], AX.X, ALU.add)),
        ("we", lambda e: e.tensor_scalar(M["ws"][:, :], M["ws"][:, :], 1e-20, None, ALU.add)),
        ("wr", lambda e: e.reciprocal(M["ws"][:, :], M["ws"][:, :])),
        ("wn", TT(w[:, :, :], w[:, :, :], M["ws"][:, :].unsqueeze(2).to_broadcast([P, NB, K]), ALU.mult)),
        ("wv", TT(w[:, :, :], w[:, :, :], val[:, :, :], ALU.mult)),
        ("wg", lambda e: e.tensor_scalar(M["wr"][:, :, :], w[:, :, :], M["tg"][:, 1:2], 2.5, ALU.mult, ALU.mult)),
    ], ["Cb", "pos1"])
    for b in range(NB):
        for k in range(K):
            q.op("pool", f"sc{b}.{k}", lambda e, i, b=b, k=k: e.indirect_dma_start(
                out=M["xe_d"], out_offset=bass.IndirectOffsetOnAxis(ap=M["SI"][:, b, k:k + 1], axis=0),
                in_=M["XN"][:, b, :], in_offset=None, bounds_check=E0 * CAP - 1, oob_is_err=False),
                after=["si", "w_z"], channel=f"scat{(b * K + k) % 8}")


def experts0(q, M, BK):
    U = 4
    at = q.phases[-1]["at"]
    for u in range(U):
        def w(e, i, u=u):
            return e.dma_start(M["EW"][u][:, :], M["ew_d"][bass.ds(i * U + u + U, 1), :, :].rearrange("o p c -> (o p) c"))
        def x(e, i, u=u):
            return e.dma_start(M["XE"][u][:, :], M["xe_d"][bass.ds((i * U + u + U) * CAP, CAP), :])
        q.op("sp", f"ldx{u}", x, after=[(f"et{u}.1", 0)], lag=-1, channel=f"ldx{u}", apart=True)
        q.op("sp", f"ldw{u}", w, after=[(f"ed{u}", 0)], lag=-1, channel=f"ldw{u}", apart=True)
        q.op("sp", f"sty{u}", lambda e, i, u=u: e.dma_start(M["ye_d"][bass.ds((i * U + u) * CAP, CAP), :], M["YE"][u][:, :]),
             after=[f"ey{u}"], channel=f"sty{u}", apart=True)
    for u in range(U):
        v = u % 2
        for a in range(2):
            q.op("pe", f"et{u}.{a}", lambda e, i, u=u, a=a, v=v: e.transpose(
                BK[v][:, 128 * a:128 * a + 128], M["XE"][u][:, 128 * a:128 * a + 128], M["ident"][:, :]),
                after=[(f"ldx{u}", 1), (f"ex{u - 2}", 0) if u >= 2 else (f"ex{u + 2}", 1)])
        q.op("act", f"ex{u}", lambda e, i, v=v: e.activation(M["XeT"][v][:, :], BK[v][:, 0:256], ACT.Copy),
             after=[f"et{u}.1", (f"eu{u - 2}.1", 0) if u >= 2 else (f"eu{u + 2}.1", 1)])
        for a in range(2):
            q.op("pe", f"eu{u}.{a}", lambda e, i, u=u, a=a, v=v: e.matmul(
                BK[2 + v][:, 0:128], M["EW"][u][:, 128 * a:128 * a + 128], M["XeT"][v][:, 128 * a:128 * a + 128],
                start=(a == 0), stop=(a == 1)),
                after=[f"ex{u}", (f"ldw{u}", 1), (f"er{u - 2}", 0) if u >= 2 else (f"er{u + 2}", 1)])
        q.op("act", f"er{u}", lambda e, i, v=v: e.activation(M["EH"][v][:, :], BK[2 + v][:, 0:128], ACT.Relu),
             after=[f"eu{u}.1", (f"ed{u - 2}", 0) if u >= 2 else (f"ed{u + 2}", 1)])
        q.op("dve", f"es{u}", lambda e, i, v=v: e.tensor_tensor(M["EH"][v][:, :], M["EH"][v][:, :], M["EH"][v][:, :], ALU.mult), after=[f"er{u}"])
        q.op("pe", f"ed{u}", lambda e, i, u=u, v=v: e.matmul(
            BK[4 + v][:, 0:256], M["EH"][v][:, :], M["EW"][u][:, 256:512], start=True, stop=True),
            after=[f"es{u}", (f"ey{u - 2}", 0) if u >= 2 else (f"ey{u + 2}", 1)])
        q.op("dve", f"ey{u}", lambda e, i, u=u, v=v: e.tensor_copy(M["YE"][u][:, :], BK[4 + v][:, 0:256]), after=[f"ed{u}", (f"sty{u}", 1)])


def combine0(q, M):
    D = 4
    for b in range(NB):
        for k in range(K0):
            n = b * K0 + k
            q.op("pool", f"ga{n}", lambda e, i, b=b, k=k, n=n: e.indirect_dma_start(
                out=M["GA"][n % 8][:, :], out_offset=None, in_=M["ye_d"],
                in_offset=bass.IndirectOffsetOnAxis(ap=M["GI"][:, b, k:k + 1], axis=0), bounds_check=E0 * CAP - 1, oob_is_err=False),
                after=[f"ca{n - 8}"] if n >= 8 else [], channel=f"scat{n % 8}")
            q.op("dve", f"ca{n}", lambda e, i, b=b, k=k, n=n: e.scalar_tensor_tensor(
                out=M["X"][:, b, :], in0=M["GA"][n % 8][:, :], scalar=M["wr"][:, b, k:k + 1], in1=M["X"][:, b, :],
                op0=ALU.mult, op1=ALU.add), after=[f"ga{n}"] + ([f"ca{n - 1}"] if k else []))


def ffn1(q, M, BK):
    layer_norm_batches(q, M, BK, "L1")
    at = q.phases[-1]["at"]
    L = BK[2]
    for b in range(GB):
        for a in range(2):
            q.op("pe", f"lg{b}.{a}", lambda e, i, b=b, a=a: e.matmul(
                L[:, E1 * b:E1 * b + E1], tokens(M, b, a), M["GW1"][:, a, :], start=(a == 0), stop=(a == 1)),
                after=["xt0", "xt1", ("fx34", 1), "w_w"])
    r = M["r1"]
    s = M["s1"]
    lc, p, m0, m1 = r[0], r[1], r[2], r[3]
    bc = lambda m: m[:, :].unsqueeze(2).to_broadcast([P, GB, E1])
    other = lambda m: m[:, :, :].unsqueeze(2).to_broadcast([P, GB, E1, E1])
    own = lambda m: m[:, :, :].unsqueeze(3).to_broadcast([P, GB, E1, E1])
    lt = M["lt"][:, :, :].unsqueeze(1).to_broadcast([P, GB, E1, E1])
    W = GB * E1 * E1
    gg = lambda m: m[:, 0:W].rearrange("p (b g h) -> p b g h", g=E1, h=E1)
    gg3 = lambda m: m[:, 0:W].rearrange("p (x h) -> p x h", h=E1)
    fl = lambda m: m[:, :, :].rearrange("p b e -> p (b e)")
    q.op("dve", "lc", lambda e, i: e.tensor_copy(fl(lc), L[:, 0:GB * E1]), after=["lg3.1"])
    q.op("dve", "mx", lambda e, i: e.tensor_reduce(s[0][:, :], lc[:, :, :], AX.X, ALU.max), after=["lc"])
    q.op("dve", "sm", lambda e, i: e.tensor_tensor(lc[:, :, :], lc[:, :, :], bc(s[0]), ALU.subtract), after=["mx"])
    q.op("act", "ex", lambda e, i: e.activation(fl(p), fl(lc), ACT.Exp), after=["sm", ("wc", 1)])
    steps = [
        ("su", lambda e: e.tensor_reduce(s[1][:, :], p[:, :, :], AX.X, ALU.add)),
        ("ri", lambda e: e.reciprocal(s[1][:, :], s[1][:, :])),
        ("pr", lambda e: e.tensor_tensor(p[:, :, :], p[:, :, :], bc(s[1]), ALU.mult)),
        ("eq", lambda e: e.tensor_tensor(gg(M["big0"]), other(p), own(p), ALU.is_equal)),
        ("el", lambda e: e.tensor_tensor(gg(M["big0"]), gg(M["big0"]), lt, ALU.mult)),
        ("gt", lambda e: e.tensor_tensor(gg(M["big1"]), other(p), own(p), ALU.is_gt)),
        ("ah", lambda e: e.tensor_tensor(gg(M["big0"]), gg(M["big0"]), gg(M["big1"]), ALU.add)),
        ("rk", lambda e: e.tensor_reduce(fl(m0), gg3(M["big0"]), AX.X, ALU.add)),
        ("se", lambda e: e.tensor_scalar(fl(m0), fl(m0), 2.0, None, ALU.is_lt)),
        ("ps", lambda e: e.tensor_tensor(m1[:, :, :], m0[:, :, :], p[:, :, :], ALU.mult)),
        ("sw", lambda e: e.tensor_reduce(s[2][:, :], m1[:, :, :], AX.X, ALU.add)),
        ("sa", lambda e: e.tensor_scalar(s[2][:, :], s[2][:, :], 1e-20, None, ALU.add)),
        ("sr", lambda e: e.reciprocal(s[2][:, :], s[2][:, :])),
        ("wn", lambda e: e.tensor_tensor(m1[:, :, :], m1[:, :, :], bc(s[2]), ALU.mult)),
        ("wc", lambda e: e.tensor_scalar(M["CW"][:, :, :], m1[:, :, :], M["tg"][:, 3:4], None, ALU.mult)),
    ]
    prev = ["ex"]
    for name, fn in steps:
        q.op("dve", name, lambda e, i, fn=fn: fn(e), after=prev + ([("lastx", 1)] if name == "wc" else []))
        prev = [name]
    work = [("S", 0, [(0, 128), (128, 128), (256, 96)])] + [("E", x, [(0, 88), (88, 88)]) for x in range(E1)]
    n_chunks = sum(len(c) for _, _, c in work)

    def back(kind, n, depth):
        return (f"{kind}{n - depth}", 0) if n >= depth else (f"{kind}{max(m for m in range(n_chunks) if m % depth == n)}", 1)

    n = ndn = 0
    for kind, x, chunks in work:
        first = n
        for lo, size in chunks:
            slot = n % 4
            for w, bk in (("g", 3), ("u", 4)):
                for a in range(2):
                    src = M["SG" if w == "g" else "SP"][:, a, lo:lo + size] if kind == "S" else M["EG" if w == "g" else "EP"][:, x, a, lo:lo + size]
                    q.op("pe", f"{w}{n}.{a}", lambda e, i, src=src, a=a, bk=bk, size=size, n=n: e.matmul(
                        BK[bk + 2 * (n % 2)][0:size, :], src, M["XT"][:, a, :], start=(a == 0), stop=(a == 1)),
                        after=["xt0", "xt1", back("hu", n, 2), "w_f1"])
            q.op("act", f"si{n}", lambda e, i, n=n, size=size, slot=slot: e.activation(
                M["RL"][0:size, slot, :], BK[3 + 2 * (n % 2)][0:size, :], ACT.Silu), after=[f"g{n}.1", back("dr", n, 4)])
            q.op("dve", f"hu{n}", lambda e, i, n=n, size=size, slot=slot: e.tensor_tensor(
                M["RL"][0:size, slot, :], BK[4 + 2 * (n % 2)][0:size, :], M["RL"][0:size, slot, :], ALU.mult), after=[f"si{n}", f"u{n}.1"])
            n += 1
        for b in range(GB):
            D = BK[7 if ndn % 2 else 2]
            for k, (lo, size) in enumerate(chunks):
                slot = (first + k) % 4
                src = M["SDn"][0:size, k, :] if kind == "S" else M["ED"][0:size, x, k, :]
                q.op("pe", f"fd{ndn}.{k}", lambda e, i, D=D, slot=slot, size=size, b=b, src=src, k=k, chunks=chunks: e.matmul(
                    D[:, 0:256], M["RL"][0:size, slot, 128 * b:128 * b + 128], src, start=(k == 0), stop=(k == len(chunks) - 1)),
                    after=[f"hu{first + len(chunks) - 1}", "lc", (f"fx{ndn - 2}", 0) if ndn >= 2 else (f"fx{34 + ndn}", 1), "w_f1"])
            sc = M["tg"][:, 3:4] if kind == "S" else M["CW"][:, b, x:x + 1]
            X = lambda i, b=b: M["X"][:, bass.ds(i * GB + b, 1), :][:, 0, :]
            q.op("dve", f"fx{ndn}", lambda e, i, D=D, sc=sc, X=X: e.scalar_tensor_tensor(
                out=X(i), in0=D[:, 0:256], scalar=sc, in1=X(i), op0=ALU.mult, op1=ALU.add),
                after=[f"fd{ndn}.{len(chunks) - 1}", "wc"] + ([f"fx{ndn - 4}"] if ndn >= 4 else []))
            for k in range(len(chunks)):
                if b == GB - 1:
                    at[f"dr{first + k}"] = at[f"fd{ndn}.{len(chunks) - 1}"]
            ndn += 1
    at["xt.read"] = at[f"u{n - 1}.1"]
    at["lastx"] = at[f"fx{ndn - 1}"]




def build(nc, d, out):
    ctx = ExitStack()
    with ctx:
        sb = lambda name, shape, dt=F32: ctx.enter_context(nc.sbuf_tensor(name, shape, dt))
        q = Queue(nc, ctx)
        for e in ENGINES[:4]:
            q.channel(e)
        M = {}
        X = M["X"] = sb("X", [P, NB, T])
        for nm in ("Wq", "Wk", "Wv", "Wo"):
            M[nm] = sb(nm, [P, P])
        for nm in ("bq", "bk", "bo"):
            M[nm] = sb(nm, [P, 1])
        M["bv"] = sb("bv", [P, P])
        M["ident"] = sb("ident", [P, P]); M["perm"] = sb("perm", [P, P])
        M["dn"] = sb("dn", [P, 32]); M["rdn"] = sb("rdn", [P, 32]); M["bog"] = sb("bog", [P, 1])
        M["tg"] = sb("tg", [P, 4]); M["graw"] = sb("graw", [P, 5])
        M["mhalf"] = sb("mhalf", [P, 1])
        for nm, shape, dt in (("QS", [P, 8, 2, T], BF16),
                              ("VA", [P, 2, 16, 32], F32), ("QKc", [P, 2, T], F32), ("QKs", [P, 3, 2, T], BF16),
                               ("Cb", [P, T], F32), ("st6", [P, 6], F32), ("mv", [P, 2], F32),
                              ("ve", [P, 1], F32), ("rs", [P, 1], F32), ("mx", [P, 2, 16], F32), ("mxT", [16, T], BF16)):
            M[nm] = [sb(f"{nm}{n}", shape, dt) for n in range(2)]
        M["Xn"] = sb("Xn", [P, T]); M["OS"] = sb("OS", [P, 4, T]); M["rd"] = sb("rd", [P, T]); M["on"] = sb("on", [P, T])
        PXs = sb("PX", [P, 4, 1024])
        M["PX"] = [PXs[:, n, :] for n in range(4)]
        M["big0"], M["big1"] = (PXs[:, 2 * n:2 * n + 2, :].rearrange("p a c -> p (a c)") for n in range(2))
        M["oh"] = sb("oh", [P, 2048])
        for nm, shape, dt in (("XN", [P, NB, T], F32), ("st4", [P, GB, 6], F32), ("mv4", [P, GB, 2], F32), ("ve4", [P, GB], F32),
                              ("rs4", [P, GB], F32), ("mhalf4", [P, GB], F32), ("XT", [P, 2, 512], F32), ("GW", [P, 2, E0], F32),
                              ("LG", [P, NB, E0], F32), ("SU", [P, 2, HS], F32), ("SD", [P, 4, T], F32), ("RL", [P, 4, 512], F32),
                              ("sc", [P, NB, E0], F32), ("scb", [P, NB, E0], F32), ("lt", [P, 8, 8], F32),
                              ("MV", [P, NB, 8], F32), ("MI", [P, NB, 8], U32), ("bc", [P, E0], F32), ("iota", [P, E0], F32),
                              ("A", [P, NB, E0], F32), ("C", [P, NB, E0], F32), ("pos", [P, NB, E0], F32),
                              ("Ab", [P, NB, E0], BF16), ("Ab2", [P, NB, E0], BF16), ("before32", [P, P], F32),
                              ("before", [P, P], BF16), ("ones", [P, P], BF16), ("SI", [P, NB, K0], U32), ("GI", [P, NB, K0], U32),
                              ("ws", [P, NB], F32), ("wr", [P, NB, K0], F32), ("CW", [P, GB, E1], F32), ("GW1", [P, 2, E1], F32),
                              ("SG", [P, 2, ISH], F32), ("SP", [P, 2, ISH], F32), ("SDn", [P, 3, T], F32),
                              ("EG", [P, E1, 2, I1], F32), ("EP", [P, E1, 2, I1], F32), ("ED", [88, E1, 2, T], F32)):
            M[nm] = sb(nm, shape, dt)
        for nm, n, shape in (("XC", 2, [P, T]), ("rt", 5, [P, P]), ("tk", 6, [P, NB, K0]), 
                             ("XeT", 2, [P, T]), ("EH", 2, [P, P]), ("r1", 4, [P, GB, E1]), ("s1", 3, [P, GB])):
            M[nm] = [sb(f"{nm}{k}", shape) for k in range(n)]
        M["EW"] = [M["RL"][:, k, :] for k in range(4)]
        M["XE"] = [M["OS"][:, k, :] for k in range(4)]
        M["YE"] = [M["QKc"][k // 2][:, k % 2, :] for k in range(4)]
        M["GA"] = [M["oh"][:, T * k:T * k + T] for k in range(8)]
        M["xe_d"] = nc.dram_tensor("xe", [E0 * CAP, T], F32, kind="Internal").ap()
        M["ye_d"] = nc.dram_tensor("ye", [E0 * CAP, T], F32, kind="Internal").ap()
        M["ew_d"] = d["ew"]
        ps = lambda name, w=512: ctx.enter_context(nc.psum_tensor(name, [P, w], F32))
        M["S"] = [ps("S0"), ps("S1")]; M["ST"] = [ps(f"ST{n}", 1024) for n in range(2)]
        M["O"] = ps("O"); M["M1"] = ps("M1")
        ST = M["ST"]
        BK = [M["S"][0][:, :], M["S"][1][:, :]] + [ST[n][:, 512 * k:512 * k + 512] for n in range(2) for k in range(2)] + [M["O"][:, :], M["M1"][:, :]]
        M["ctx_d"] = d["ctx"].rearrange("b c t -> c b t")

        q.phase()
        ld = lambda dst, src, ch="w_w": q.op("sp", f"ld.{len(q.phases[-1]['at'])}", lambda e, i: e.dma_start(dst, src), channel=ch)
        ld(X[:, :, :], d["x"].rearrange("b c t -> c b t"), "w_x")
        M["hbL0"] = sb("hbL0", [16, P]); M["hbL1"] = sb("hbL1", [8, P]); M["rT"] = sb("rT", [16, T])
        for nm in ("Wq", "Wk", "Wv", "Wo", "ident", "hbL0", "hbL1", "perm"):
            ld(M[nm][:, :], d[nm])
        for nm in ("bq", "bk", "bo"):
            ld(M[nm][:, :], d[nm])
        ld(M["bv"][:, :], d["bv"].to_broadcast([P, P]))
        ld(M["graw"][:, :], d["graw"].to_broadcast([P, 5]), "w_g")
        for nm in ("GW", "GW1", "SU", "SD", "lt", "before32", "SG", "SP", "SDn", "EG", "EP", "ED"):
            ld(M[nm][tuple(slice(None) for _ in M[nm].shape)], d[nm], "w_s0" if nm in ("SU", "SD") else "w_f1" if nm in ("SG", "SP", "SDn", "EG", "EP", "ED") else "w_w")
        for nm in ("bc", "iota"):
            ld(M[nm][:, :], d[nm].to_broadcast([P, E0]))
        q.op("dve", "ones", lambda e, i: e.memset(M["ones"][:, :], 1.0))
        q.op("dve", "mhalf4", lambda e, i: e.memset(M["mhalf4"][:, :], -0.5))
        q.op("dve", "before", lambda e, i: e.tensor_copy(M["before"][:, :], M["before32"][:, :]), after=["w_w"])
        q.op("dve", "zero", lambda e, i: e.memset(M["XN"][:, :, :], 0.0))
        for n in range(2):
            q.op("sp", f"z{n}", lambda e, i, n=n: e.dma_start(
                M["xe_d"][2048 * n:2048 * n + 2048, :].rearrange("(p b) t -> p b t", p=P), M["XN"][:, :, :]), after=["zero"], channel="w_z")
        for n in range(2):
            q.op("pool", f"one.QS{n}", lambda e, i, n=n: e.memset(M["QS"][n][:, :, :, :], 1.0))
            q.op("dve", f"one.VA{n}", lambda e, i, n=n: e.memset(M["VA"][n][:, :, :, :], 1.0))
        q.op("dve", "mhalf", lambda e, i: e.memset(M["mhalf"][:, :], -0.5))
        q.op("act", "gates", lambda e, i: e.activation(M["tg"][:, :], M["graw"][:, 0:4], ACT.Tanh), after=["w_g"])
        q.op("dve", "gamma", lambda e, i: e.tensor_tensor(M["tg"][:, 2:3], M["tg"][:, 2:3], M["graw"][:, 4:5], ALU.mult), after=["gates"])
        q.op("dve", "bog", lambda e, i: e.tensor_tensor(M["bog"][:, :], M["bo"][:, :], M["tg"][:, 0:1], ALU.mult), after=["gates", "w_w"])

        q.phase(NB // 2)
        A = Attention("L0", 16, 8)
        for hb in range(2):
            attention_half(q, A, M, hb)

        q.phase(NGRP)
        shared0(q, M, BK)
        q.phase()
        route0(q, M, BK)
        q.phase(E0 // 4)
        experts0(q, M, BK)
        q.phase()
        combine0(q, M)
        for n in range(2):
            q.op("dve", f"one.QS{n}", lambda e, i, n=n: e.memset(M["QS"][n][96:97, :, 1, :], 1.0))
        q.phase(NB // 2)
        A = Attention("L1", 8, 16)
        for hb in range(2):
            attention_half(q, A, M, hb)
        q.phase(NGRP)
        ffn1(q, M, BK)

        q.phase()
        q.op("sp", "store", lambda e, i: e.dma_start(out.rearrange("b c t -> c b t"), X[:, :, :]), channel="st")
        q.emit()


def orders():
    p = np.arange(128)
    cx = 16 * (p % 8) + p // 8
    cq = 8 * (8 * (p // 64) + p % 8) + p % 64 // 8
    cv = 8 * (4 * (p // 32) + p % 4) + p % 32 // 4
    cw = 16 * (2 * (p // 32) + p % 2) + p % 32 // 2
    return cx, cq, cv, cw


def layout(inp):
    a = {k: np.asarray(v) for k, v in inp.items()}
    cx, cq, cv, cw = orders()
    d = {"x": a["x"][:, cx, :], "ctx": a["ctx_2048"][:, cx, :]}
    for n in "qkv":
        d["W" + n] = a["L0_xattn_W" + n][cv if n == "v" else cq][:, cx].T
    d["Wo"] = a["L0_xattn_Wo"][cx][:, cv].T
    for n in "qk":
        d["b" + n] = a["L0_xattn_b" + n][cq].reshape(128, 1)
    d["bv"] = a["L0_xattn_bv"][cv].reshape(1, 128)
    d["perm"] = np.equal(cw[:, None], cx[None, :]).astype(np.float32)
    d["bo"] = a["L0_xattn_bo"][cx].reshape(128, 1)
    d["graw"] = np.stack([a["g_xattn"][0], a["g_ffn"][0], a["g_xattn"][1], a["g_ffn"][1], a["L1_xattn_gamma"]]).reshape(1, 5)
    d["ident"] = np.eye(128, dtype=np.float32)
    for nm, G, R in (("hbL0", 4, 8), ("hbL1", 2, 16)):
        s = d[nm] = np.zeros((4 * G, 128), np.float32)
        for j in range(4):
            for i in range(R):
                for g in range(G):
                    s[G * j + g, 32 * j + G * i + g] = 1
    up, down = a["L0_ffn_up_w"], a["L0_ffn_down_w"]
    d["ew"] = np.concatenate([up.transpose(0, 2, 1)[:, 0:128], up.transpose(0, 2, 1)[:, 128:256], down.transpose(0, 2, 1)], axis=2)
    halves = lambda w: w.T.reshape(2, 128, -1).transpose(1, 0, 2)
    d["GW"], d["GW1"], d["SU"] = halves(a["L0_ffn_gate_w"]), halves(a["L1_ffn_gate_w"]), halves(a["L0_ffn_shared_up_w"])
    d["SG"], d["SP"] = halves(a["L1_ffn_shared_gate"]), halves(a["L1_ffn_shared_up"])
    d["SD"] = a["L0_ffn_shared_down_w"].T.reshape(4, 128, 256).transpose(1, 0, 2)
    d["SDn"] = np.zeros((3, 128, 256), np.float32)
    d["SDn"].reshape(384, 256)[0:352] = a["L1_ffn_shared_down"].T
    d["SDn"] = d["SDn"].transpose(1, 0, 2)
    for nm, w in (("EG", "gate"), ("EP", "up")):
        d[nm] = a["L1_ffn_expert_" + w].transpose(2, 0, 1).reshape(2, 128, 8, 176).transpose(1, 2, 0, 3)
    d["ED"] = a["L1_ffn_expert_down"].transpose(0, 2, 1).reshape(8, 2, 88, 256).transpose(2, 0, 1, 3)
    d["lt"] = np.broadcast_to(np.tril(np.ones((8, 8), np.float32), -1), (128, 8, 8))
    d["iota"] = np.arange(32, dtype=np.float32).reshape(1, 32)
    d["bc"] = a["L0_ffn_bias_corr"].reshape(1, 32)
    d["before32"] = np.less(cx[:, None], cx[None, :]).astype(np.float32)
    return {k: np.ascontiguousarray(v) for k, v in d.items()}


def kernel(**inputs):
    import concourse.bacc as bacc
    from concourse.bass_utils import run_bass_kernel_spmd

    nc = bacc.Bacc("TRN2", target_bir_lowering=False, num_devices=1)
    arrays = {f"in_{name}": array for name, array in layout(inputs).items()}
    args = {name[3:]: nc.dram_tensor(name, a.shape, mybir.dt.from_np(a.dtype), kind="ExternalInput").ap()
            for name, a in arrays.items()}
    out = nc.dram_tensor("out", (NB, C, T), F32, kind="ExternalOutput").ap()
    build(nc, args, out)
    r = run_bass_kernel_spmd(nc, [arrays], core_ids=[0])
    got = r.results[0]["out"]
    cx = orders()[0]
    inverse = [int(np.nonzero(cx == c)[0][0]) for c in range(C)]
    return got[:, inverse, :]
```

```python
from contextlib import ExitStack

import numpy as np
import concourse.bass as bass
from concourse import mybir

F32 = mybir.dt.float32
BF16 = mybir.dt.bfloat16
U32 = mybir.dt.uint32
I32 = mybir.dt.int32
ALU = mybir.AluOpType
ACT = mybir.ActivationFunctionType
AX = mybir.AxisListType
P = 128
ENGINES = ("pe", "dve", "act", "pool", "sp")


class Queue:

    def __init__(self, nc, ctx):
        self.nc, self.ctx = nc, ctx
        self.sem = {}
        self.phases = []
        self.sem["pad"] = ctx.enter_context(nc.semaphore("s_pad"))

    def channel(self, name):
        if name not in self.sem:
            self.sem[name] = self.ctx.enter_context(self.nc.semaphore("s_" + name))
        return name

    def phase(self, n=1):
        self.phases.append(dict(n=n, lags={0}, ops={e: [] for e in ENGINES}, at={}, count={}))

    def op(self, engine, name, fn, after=(), lag=0, channel=None, apart=False):
        ph = self.phases[-1]
        ch = self.channel(channel or engine)
        k = ph["count"].get(ch, 0)
        ph["count"][ch] = k + 1
        ph["lags"].add(lag)
        assert name not in ph["at"], name
        ph["at"][name] = (ch, k)
        ph["ops"][engine].append((name, ch, k, fn, [(a, 0) if isinstance(a, str) else a for a in after], lag, apart))

    def emit(self):
        total = {c: 0 for c in self.sem if c != "pad"}
        step = {c: 1 if c in ENGINES else 16 for c in total}
        plans = []
        for ph in self.phases:
            runs = ph["n"] + max(ph["lags"]) - min(ph["lags"])
            start = dict(total)
            for c, m in ph["count"].items():
                total[c] += m * runs
            plans.append((ph, runs, start, dict(total)))
        programs = {}
        for e in ENGINES:
            programs[e] = self._program(e, plans, step)
        with self.nc.Block() as block:
            for e in ("sp", "pool", "act", "pe", "dve"):
                of_block(block, e)(programs[e])

    def _program(self, e, plans, step):
        q = self

        def program(eng):
            seen = {}

            def wait(sem, value):
                if isinstance(value, int):
                    if value <= 0 or seen.get(sem, 0) >= value:
                        return
                    seen[sem] = value
                eng.wait_ge(q.sem[sem], value)
                if e == "sp" and not isinstance(value, int):
                    eng.sem_inc(q.sem["pad"], 1)

            for n_ph, (ph, runs, start, end) in enumerate(plans):
                if n_ph and ph["ops"][e]:
                    for c, v in start.items():
                        if v and not c.startswith("w_"):
                            wait(c, v * step[c])

                def iteration(r, i):
                    skipped = {}
                    inside = {}

                    def flush(c):
                        if skipped.get(c):
                            base = start[c] + ph["count"][c] * r
                            k0, m = skipped.pop(c)
                            wait(c, (base + k0) * step[c])
                            eng.sem_inc(q.sem[c], m * step[c])

                    issued = set()
                    for name, ch, k, fn, after, lag, apart in ph["ops"][e]:
                        if isinstance(i, int) and not 0 <= i - lag < ph["n"]:
                            k0, m = skipped.get(ch, (k, 0))
                            skipped[ch] = (k0, m + 1)
                            continue
                        for c in list(skipped):
                            flush(c)
                        need = {}
                        for a, d in after:
                            if a.startswith("w_"):
                                need[a] = max(need.get(a, 0), d) if d else end[a] * step[a]
                                continue
                            c, ka = ph["at"][a]
                            off = start[c] + ka + 1 - d * ph["count"][c]
                            need[c] = max(need.get(c, -10**9), off)
                        for c, off in need.items():
                            if c.startswith("w_"):
                                wait(c, off)
                                continue
                            if isinstance(r, int):
                                v = off + ph["count"][c] * r
                                if off + ph["count"][c] * r > start[c]:
                                    wait(c, v * step[c])
                            elif off > inside.get(c, -10**9):
                                inside[c] = off
                                wait(c, (r * ph["count"][c] + off) * step[c])
                        if apart and e != "sp" and not isinstance(r, int) and need:
                            eng.sem_inc(q.sem["pad"], 1)
                        made = fn(eng, i)
                        made.then_inc(q.sem[ch], step[ch])
                    for c in list(skipped):
                        flush(c)

                if not ph["ops"][e]:
                    continue
                lo, hi = min(ph["lags"]), ph["n"] + max(ph["lags"])
                full = (max(ph["lags"]), ph["n"] + min(ph["lags"]))
                if full[0] == lo:
                    full = (lo + 1, full[1])
                for i in range(lo, min(full[0], hi)):
                    iteration(i - lo, i)
                if full[1] > full[0]:
                    with eng.Fori(full[0], full[1]) as i:
                        iteration(i - lo, i)
                    seen.clear()
                for i in range(max(full), hi):
                    iteration(i - lo, i)
            if e == "sp":
                for c, v in plans[-1][3].items():
                    wait(c, v * step[c])

        return program


def of_block(block, engine):
    return {"sp": block.sync, "pool": block.gpsimd, "act": block.scalar, "pe": block.tensor, "dve": block.vector}[engine]



NB, C, T = 16, 128, 256
E0, H0, CAP, K0 = 32, 128, 128, 4
HS = 512
E1, I1, ISH = 8, 176, 352
EPS = 1e-5
STACK = 96
U = 4
TERMS = ((0, 0), (1, 0), (2, 0), (0, 1), (1, 1), (0, 2))


class Attention:
    def __init__(self, name, H, R):
        self.name, self.H, self.R = name, H, R
        self.NQ = H // 4
        self.scale = float(R) ** -0.5

    def heads(self, quad):
        return [self.NQ * c + quad for c in range(4)]


def attention_half(q, A, M, hb):
    R, H, NQ, L0 = A.R, A.H, A.NQ, A.name == "L0"
    skew = {0: 3, 1: 2, 2: 1, 3: 0, 4: -1}
    B = {s: hb + k for s, k in skew.items()}
    lag = {s: -(b // U) for s, b in B.items()}
    n0, n1, n2, n3, n4 = (B[s] % U for s in range(5))
    QS, QKc, QKs, VA, M1, PX = M["QS"], M["QKc"], M["QKs"], M["VA"], M["M1"], M["PX"]
    at = q.phases[-1]["at"]

    def of(kind, stage, batch, end=""):
        return (f"{kind}{batch % U}{end}", -((batch - skew[stage]) // U))

    def x_at(i, batch):
        return M["X"][:, bass.ds(i * U + batch, 1), :][:, 0, :]

    def back(kind, n, per):
        return (f"{kind}{n % (U * per)}", 0 if n >= 0 else 1)

    def score(k):
        h = A.heads(k // 4)[k % 4]
        n = hb * H + k
        for a in range(2):
            q.op("pe", f"s{n}.{a}", lambda e, i, a=a: e.matmul(
                M["S"][n % 2][:, 256 * a:256 * a + 256], QS[n2][0:STACK, h, 0, 128 * a:128 * a + 128],
                QS[n2][0:STACK, h, 1, :], start=True, stop=True), after=[of("sp", 1, B[2]), back("max", n - 2, H)], lag=lag[2])
        q.op("dve", f"max{n}", lambda e, i: e.tensor_reduce(
            M["mx"][n2 % 2][:, :, h], M["S"][n % 2][:, :].rearrange("p (a s) -> p a s", a=2), AX.X, ALU.max, negate=True),
            after=[f"s{n}.1", of("mtT", 2, B[2] - 2, ".1")], lag=lag[2])

    def score_t(m):
        pair = hb * (H // 2) + m
        bank = M["ST"][pair % 2]
        for u in range(2):
            h = A.heads(m // 2)[2 * (m % 2) + u]
            for a in range(2):
                q.op("pe", f"st{pair}.{u}{a}", lambda e, i, a=a, u=u, h=h: e.matmul(
                    bank[:, 512 * u + 256 * a:512 * u + 256 * a + 256], QS[n3][0:STACK + 1, h, 1, 128 * a:128 * a + 128],
                    QS[n3][0:STACK + 1, h, 0, :], start=True, stop=True),
                    after=[of("mrow", 2, B[3]), of("sp", 1, B[3]), back("exp", pair - 2, H // 2)])
        q.op("act", f"exp{pair}", lambda e, i: e.activation(PX[pair % 4][:, :], bank[:, :], ACT.Exp, scale=A.scale),
             after=[f"st{pair}.11", back("pv", hb * NQ + m // 2 - 2, NQ)])

    def values(quad):
        n = hb * NQ + quad
        O = M["O"]
        for a in range(2):
            for u in range(4):
                h = A.heads(quad)[u]
                pair = hb * (H // 2) + 2 * quad + u // 2
                q.op("pe", f"pv{n}" if (a, u) == (1, 3) else f"pv{n}.{a}.{u}", lambda e, i, a=a, u=u, h=h, pair=pair: e.matmul(
                    O[32 * u:32 * u + 32, 256 * (quad % 2):256 * (quad % 2) + 256], VA[n3 % 2][:, a, h, :],
                    PX[pair % 4][:, 512 * (u % 2) + 256 * a:512 * (u % 2) + 256 * a + 256], start=(a == 0), stop=(a == 1)),
                    after=[f"exp{pair}", of("va", 2, B[3]), back("oe", (n - 2) // 2, NQ // 2)])
        if quad % 2 == 1:
            k = n // 2
            q.op("act", f"oe{k}", lambda e, i: e.activation(
                M["OS"][:, quad - 1:quad + 1, :], O[:, :].rearrange("p (g t) -> p g t", g=2), ACT.Copy),
                after=[f"pv{n}", of("num", 3, B[3] - 1), of("den", 3, B[3] - 1)])

    def norm():
        n, g = n0, lag[0]
        Xb = lambda i: x_at(i, B[0])
        q.op("dve", f"bn{n}", lambda e, i: e.bn_stats(M["st6"][n % 2][:, :], Xb(i)), after=["w_x"], lag=g)
        q.op("dve", f"bna{n}", lambda e, i: e.bn_aggr(M["mv"][n % 2][:, :], M["st6"][n % 2][:, :]), after=[f"bn{n}", of("xn", 0, B[0] - 2)], lag=g, apart=True)
        q.op("dve", f"ve{n}", lambda e, i: e.tensor_scalar(M["ve"][n % 2][:, :], M["mv"][n % 2][:, 1:2], EPS, None, ALU.add), after=[f"bna{n}"], lag=g)
        q.op("pool", f"rs{n}", lambda e, i: e.tensor_tensor(M["rs"][n % 2][:, :], M["ve"][n % 2][:, :], M["mhalf"][:, :], ALU.pow),
             after=[f"ve{n}", of("xn", 0, B[0] - 2)], lag=g)
        q.op("dve", f"xn{n}", lambda e, i: e.tensor_scalar(
            M["Xn"][:, :] if L0 else QKc[n % 2][:, 0, :], Xb(i), M["mv"][n % 2][:, 0:1], M["rs"][n % 2][:, 0:1], ALU.subtract, ALU.mult),
            after=[f"rs{n}", of("qp", 0, B[0] - 1) if L0 else of("res2.", 0, B[0] - 2)], lag=g)

    def keys_in():
        n = n0
        q.op("sp", f"ldc{n}", lambda e, i: e.dma_start(
            M["Cb"][n % 2][:, :], M["ctx_d"][:, bass.ds(i * U + B[0], 1), :][:, 0, :]),
             after=[of("vt", 2, B[0] - 2), of("kp" if L0 else "kc", 0, B[0] - 2)], lag=lag[0], channel=f"ldc{n}", apart=True)

    def project():
        n, g = n0, lag[0]
        free = [of("res2.", 0, B[0] - 2)]
        if L0:
            q.op("pe", f"qp{n}", lambda e, i: e.matmul(M1[:, 0:256], M["Wq"][:, :], M["Xn"][:, :], start=True, stop=True),
                 after=[f"xn{n}", "w_w", of("va", 2, B[2])], lag=g)
            q.op("pe", f"kp{n}", lambda e, i: e.matmul(M1[:, 256:512], M["Wk"][:, :], M["Cb"][n % 2][:, :], start=True, stop=True),
                 after=[f"ldc{n}", of("mt", 2, B[2] - 1)], lag=g)
            q.op("act", f"qc{n}", lambda e, i: e.activation(QKc[n % 2][:, 0, :], M1[:, 0:256], ACT.Identity, bias=M["bq"][:, 0:1]),
                 after=[f"kp{n}"] + free, lag=g)
            q.op("act", f"kc{n}", lambda e, i: e.activation(QKc[n % 2][:, 1, :], M1[:, 256:512], ACT.Identity, bias=M["bk"][:, 0:1]),
                 after=[f"kp{n}"] + free, lag=g)
        else:
            q.op("act", f"kc{n}", lambda e, i: e.activation(QKc[n % 2][:, 1, :], M["Cb"][n % 2][:, :], ACT.Copy), after=[f"ldc{n}"] + free, lag=g)
            at[f"qc{n}"] = at[f"xn{n}"]
        part = lambda k: QKs[n % 2][:, k, :, :]
        q.op("pool", f"cut0.{n}", lambda e, i: e.tensor_copy(part(0), QKc[n % 2][:, :, :]),
             after=[f"qc{n}", f"kc{n}", of("sp", 1, B[0] - 2)], lag=g, apart=True)
        q.op("pool", f"res1.{n}", lambda e, i: e.tensor_tensor(QKc[n % 2][:, :, :], QKc[n % 2][:, :, :], part(0), ALU.subtract), after=[f"cut0.{n}"], lag=g)
        q.op("pool", f"cut1.{n}", lambda e, i: e.tensor_copy(part(1), QKc[n % 2][:, :, :]), after=[f"res1.{n}"], lag=g, apart=True)
        q.op("pool", f"res2.{n}", lambda e, i: e.tensor_tensor(part(2), QKc[n % 2][:, :, :], part(1), ALU.subtract), after=[f"cut1.{n}"], lag=g)

    def spread(which):
        n = n1
        for k in range(len(TERMS))[which]:
            a, b = TERMS[k]

            def f(e, i, k=k, x=2 * a, y=2 * b + 1):
                parts = QKs[n % 2][:, :, :, :].rearrange("p k s t -> p (k s) t")
                pair = parts[:, x:y + 1:y - x, :] if y > x else parts[:, x:y - 1 if y else None:y - x, :]
                return e.dma_start(QS[n][R * k:R * k + R, 0:H, :, :], pair)
            q.op("sp", f"sp{n}" if k == len(TERMS) - 1 else f"sp{n}.{k}", f,
                 after=[of("res2.", 0, B[1]), of("st.done", 3, B[1] - U)], lag=lag[1], channel=f"sp{n}")

    def values_in():
        n, g = n2, lag[2]
        for a in range(2):
            if L0:
                f = lambda e, i, a=a: e.matmul(M1[:, 128 * a:128 * a + 128], M["Cb"][n % 2][:, 128 * a:128 * a + 128], M["Wv"][:, :], start=True, stop=True)
            else:
                f = lambda e, i, a=a: e.transpose(M1[:, 128 * a:128 * a + 128], M["Cb"][n % 2][:, 128 * a:128 * a + 128], M["ident"][:, :])
            q.op("pe", f"vt{n}" if a else f"vt{n}.0", f, after=[of("ldc", 0, B[2]), of("yb" if L0 else "x", 4, B[4] - 1), of("mt", 2, B[2] - 1), "w_w"], lag=g)
        for a in range(2):
            def f(e, i, a=a):
                cols = M1[:, 128 * a:128 * a + 128]
                if L0:
                    v = lambda ap: ap.rearrange("p (c r g) -> p c g r", c=4, g=NQ)
                    o = VA[n % 2][:, a, 0:H, 0:32:NQ].rearrange("p (c g) r -> p c g r", g=NQ)
                    return e.tensor_tensor(o, v(cols), v(M["bv"][:, :]), ALU.add)
                return e.tensor_copy(VA[n % 2][:, a, 0:H, 0:32:NQ], cols.rearrange("p (r h) -> p h r", h=H))
            q.op("dve", f"va{n}" if a else f"va{n}.0", f, after=[f"vt{n}", of("pvl", 3, B[2] - 2)], lag=g)

    def maxima():
        n, g = n2, lag[2]
        for a in range(2):
            q.op("pe", f"mtT{n}.{a}", lambda e, i, a=a: e.transpose(
                M1[0:H, 256 + 128 * a:384 + 128 * a], M["mx"][n % 2][:, a, 0:H], M["ident"][:, :]),
                after=[f"max{hb * H + H - 1}", of("yb" if L0 else "x", 4, B[4])] + ([of("kc", 0, B[0])] if L0 else []), lag=g)
        q.op("act", f"mt{n}", lambda e, i: e.activation(M["mxT"][n % 2][0:H, :], M1[0:H, 256:512], ACT.Copy),
             after=[f"mtT{n}.1", of("mrow", 2, B[2] - 2)], lag=g)
        q.op("sp", f"mrow{n}", lambda e, i: e.dma_start(QS[n][STACK:STACK + 1, 0:H, 0, :], M["mxT"][n % 2][0:H, :]),
             after=[f"mt{n}", of("st.done", 3, B[2] - U)], lag=g, channel=f"mrow{n}")

    W = 2 * H

    def heads_out():
        oe = f"oe{(hb * NQ + NQ - 1) // 2}"
        q.op("sp", f"den{hb}", lambda e, i: e.dma_start(M["dn"][:, 0:W], M["OS"][1:98:32, 0:NQ, :]),
             after=[oe, of("rr", 4, B[3] - 1)], channel=f"den{hb}")
        q.op("sp", f"num{hb}", lambda e, i: e.dma_start(M["on"][:, :], M["OS"][0:P:NQ, 0:NQ, :]),
             after=[oe, of("pm", 4, B[3] - 1)], channel=f"num{hb}")

    def residual():
        n, g = n4, lag[4]
        dn, rdn, rd, on = M["dn"], M["rdn"], M["rd"], M["on"]
        q.op("dve", f"rr{n}", lambda e, i: e.reciprocal(rdn[:, 0:W], dn[:, 0:W]), after=[of("den", 3, B[4]), of("rT", 4, B[4] - 1)], lag=g)
        q.op("sp", f"rT{n}", lambda e, i: e.dma_start(M["rT"][0:H, :], rdn[:, 0:W]), after=[f"rr{n}", of("rb", 4, B[4] - 1)], channel=f"rT{n}", lag=g)

    def residual2():
        n, g = n4, lag[4]
        rd, on = M["rd"], M["on"]
        q.op("pe", f"rb{n}", lambda e, i: e.matmul(M1[:, 256:512], M["hb" + A.name][0:H, :], M["rT"][0:H, :], start=True, stop=True),
             after=[f"rT{n}", of("mt", 2, B[2] - 1), "w_w"] + ([of("kc", 0, B[0])] if L0 else []), lag=g)
        q.op("dve", f"on{n}", lambda e, i: e.tensor_tensor(on[:, :], M1[:, 256:512], on[:, :], ALU.mult),
             after=[of("num", 3, B[4]), f"rb{n}"], lag=g)
        q.op("pe", f"pm{n}", lambda e, i: e.matmul(M1[:, 0:256], M["Wo" if L0 else "perm"][:, :], on[:, :], start=True, stop=True),
             after=[f"on{n}", of("va", 2, B[2])] + ([of("qc", 0, B[0])] if L0 else []), lag=g)
        if L0:
            q.op("act", f"yb{n}", lambda e, i: e.activation(rd[:, :], M1[:, 0:256], ACT.Identity, bias=M["bog"][:, 0:1], scale=M["tg"][:, 0:1]),
                 after=[f"pm{n}", of("x", 4, B[4] - 1)], lag=g)
            q.op("dve", f"x{n}", lambda e, i: e.tensor_tensor(x_at(i, B[4]), x_at(i, B[4]), rd[:, :], ALU.add), after=[f"yb{n}"], lag=g)
        else:
            q.op("dve", f"x{n}", lambda e, i: e.scalar_tensor_tensor(
                out=x_at(i, B[4]), in0=M1[:, 0:256], scalar=M["tg"][:, 2:3], in1=x_at(i, B[4]), op0=ALU.mult, op1=ALU.add), after=[f"pm{n}"], lag=g)

    n_pairs, made = H // 2, 0
    norm()
    keys_in()
    for m in range(n_pairs):
        while made < 2 + (H - 2) * (m + 1) // n_pairs and made < H:
            score(made)
            made += 1
        score_t(m)
        if m == 0:
            values_in()
            spread(slice(0, 3))
            residual()
            spread(slice(3, 6))
        if m == 1:
            project()
        if m == n_pairs // 2 + 1:
            residual2()
        if m % 2 == 1 and m >= 3:
            values(m // 2 - 1)
    at[f"st.done{n3}"] = at[f"st{hb * n_pairs + n_pairs - 1}.11"]
    maxima()
    values(NQ - 1)
    at[f"pvl{n3}"] = at[f"pv{hb * NQ + NQ - 1}"]
    heads_out()



GB = 4
NGRP = NB // GB


def layer_norm_batches(q, M, BK, pre):
    Xb = lambda i, b: M["X"][:, bass.ds(i * GB + b, 1), :][:, 0, :]
    Nb = lambda i, b: M["XN"][:, bass.ds(i * GB + b, 1), :][:, 0, :]
    st, mv = M["st4"], M["mv4"]
    for b in range(GB):
        q.op("dve", f"bn{b}", lambda e, i, b=b: e.bn_stats(st[:, b, :], Xb(i, b)), after=[("xn3", 1)])
    for b in range(GB):
        q.op("dve", f"bna{b}", lambda e, i, b=b: e.bn_aggr(mv[:, b, :], st[:, b, :]), after=[f"bn{b}"], apart=True)
    q.op("dve", "ve", lambda e, i: e.tensor_scalar(M["ve4"][:, :], mv[:, :, 1], EPS, None, ALU.add), after=["bna3"])
    q.op("pool", "rs", lambda e, i: e.tensor_tensor(M["rs4"][:, :], M["ve4"][:, :], M["mhalf4"][:, :], ALU.pow), after=["ve", ("xn3", 1)])
    for b in range(GB):
        q.op("dve", f"xn{b}", lambda e, i, b=b: e.tensor_scalar(
            Nb(i, b), Xb(i, b), mv[:, b, 0:1], M["rs4"][:, b:b + 1], ALU.subtract, ALU.mult), after=["rs"] + (["w_z"] if pre == "L0" else []))
    for b in range(GB):
        q.op("act", f"xc{b}", lambda e, i, b=b: e.activation(M["XC"][b % 2][:, :], Nb(i, b), ACT.Copy),
             after=[f"xn{b}", (f"tp{b - 2}.1", 0) if b >= 2 else (f"tp{b + 2}.1", 1)])
        for a in range(2):
            q.op("pe", f"tp{b}.{a}", lambda e, i, b=b, a=a: e.transpose(
                BK[a][:, 128 * b:128 * b + 128], M["XC"][b % 2][:, 128 * a:128 * a + 128], M["ident"][:, :]),
                after=[f"xc{b}", (f"xt{a}", 1), "w_w"])
    q.op("act", "xt0", lambda e, i: e.activation(M["XT"][:, 0, :], BK[0][:, :], ACT.Copy), after=["tp3.0", ("xt.read", 1)])
    q.op("dve", "xt1", lambda e, i: e.tensor_copy(M["XT"][:, 1, :], BK[1][:, :]), after=["tp3.1", ("xt.read", 1)])


def tokens(M, b, a):
    return M["XT"][:, a, 128 * b:128 * b + 128]


def shared0(q, M, BK):
    layer_norm_batches(q, M, BK, "L0")
    at = q.phases[-1]["at"]
    L = BK[2]
    for b in range(GB):
        for a in range(2):
            q.op("pe", f"lg{b}.{a}", lambda e, i, b=b, a=a: e.matmul(
                L[:, E0 * b:E0 * b + E0], tokens(M, b, a), M["GW"][:, a, :], start=(a == 0), stop=(a == 1)),
                after=["xt0", "xt1", ("lgc", 1), "w_w"])
    q.op("dve", "lgc", lambda e, i: e.tensor_copy(
        M["LG"][:, bass.ds(i * GB, GB), :], L[:, 0:GB * E0].rearrange("p (b e) -> p b e", b=GB)), after=["lg3.1"])
    for c in range(4):
        U = BK[3 + c % 2]
        for a in range(2):
            q.op("pe", f"up{c}.{a}", lambda e, i, c=c, a=a, U=U: e.matmul(
                U[:, :], M["SU"][:, a, 128 * c:128 * c + 128], M["XT"][:, a, :], start=(a == 0), stop=(a == 1)),
                after=["xt0", "xt1", (f"relu{c - 2}", 0) if c >= 2 else (f"relu{c + 2}", 1), "w_s0"])
        q.op("act", f"relu{c}", lambda e, i, c=c, U=U: e.activation(M["RL"][:, c, :], U[:, :], ACT.Relu), after=[f"up{c}.1", ("dn3.3", 1)])
        q.op("dve", f"sq{c}", lambda e, i, c=c: e.tensor_tensor(M["RL"][:, c, :], M["RL"][:, c, :], M["RL"][:, c, :], ALU.mult), after=[f"relu{c}"])
    at["xt.read"] = at["up3.1"]
    for b in range(GB):
        D = BK[5 + b % 2]
        for c in range(4):
            q.op("pe", f"dn{b}.{c}", lambda e, i, b=b, c=c, D=D: e.matmul(
                D[:, 0:256], M["RL"][:, c, 128 * b:128 * b + 128], M["SD"][:, c, :], start=(c == 0), stop=(c == 3)),
                after=["sq3", (f"xs{b - 2}", 0) if b >= 2 else (f"xs{b + 2}", 1), "w_s0"])
        X = lambda i, b=b: M["X"][:, bass.ds(i * GB + b, 1), :][:, 0, :]
        q.op("dve", f"xs{b}", lambda e, i, X=X, D=D: e.scalar_tensor_tensor(
            out=X(i), in0=D[:, 0:256], scalar=M["tg"][:, 1:2], in1=X(i), op0=ALU.mult, op1=ALU.add), after=[f"dn{b}.3"])


def chain(q, engine, steps, first=()):
    prev = list(first)
    for name, fn in steps:
        q.op(engine, name, lambda e, i, fn=fn: fn(e), after=prev)
        prev = [name]


def route0(q, M, BK):
    G, K = 8, K0
    LG = M["LG"]
    sc, sb, t = M["sc"], M["scb"], M["rt"]
    flat = lambda ap: ap[:, :, :].rearrange("p b e -> p (b e)")
    q.op("act", "sig", lambda e, i: e.activation(flat(sc), flat(LG), ACT.Sigmoid))
    bias = M["bc"][:, :].unsqueeze(1).to_broadcast([P, NB, E0])
    v4 = sb[:, :, :].rearrange("p b (g m) -> p (b g) m", m=4)
    hi1, lo1, hi2, lo2, gs = (t[k] for k in range(5))
    g3 = lambda ap: ap[:, :].rearrange("p (b g) -> p b g", g=G)
    other = g3(gs).unsqueeze(2).to_broadcast([P, NB, G, G])
    own = g3(gs).unsqueeze(3).to_broadcast([P, NB, G, G])
    lt = M["lt"][:, :, :].unsqueeze(1).to_broadcast([P, NB, G, G])
    big0, big1, oh = M["big0"], M["big1"], M["oh"]
    gg = lambda m: m[:, 0:NB * G * G].rearrange("p (b g h) -> p b g h", g=G, h=G)
    gg3 = lambda m: m[:, 0:NB * G * G].rearrange("p (x h) -> p x h", h=G)
    ke = lambda m: m[:, :].rearrange("p (b k e) -> p b k e", k=K, e=E0)
    TT = lambda o, a, b, op: (lambda e: e.tensor_tensor(o, a, b, op))
    chain(q, "dve", [
        ("bias", TT(sb[:, :, :], sc[:, :, :], bias, ALU.add)),
        ("hi1", TT(hi1[:, :], v4[:, :, 0], v4[:, :, 1], ALU.max)),
        ("lo1", TT(lo1[:, :], v4[:, :, 0], v4[:, :, 1], ALU.min)),
        ("hi2", TT(hi2[:, :], v4[:, :, 2], v4[:, :, 3], ALU.max)),
        ("lo2", TT(lo2[:, :], v4[:, :, 2], v4[:, :, 3], ALU.min)),
        ("lo", TT(lo1[:, :], lo1[:, :], lo2[:, :], ALU.max)),
        ("mid", TT(lo2[:, :], hi1[:, :], hi2[:, :], ALU.min)),
        ("second", TT(lo1[:, :], lo1[:, :], lo2[:, :], ALU.max)),
        ("first", TT(hi1[:, :], hi1[:, :], hi2[:, :], ALU.max)),
        ("gs", TT(gs[:, :], hi1[:, :], lo1[:, :], ALU.add)),
        ("eq", TT(gg(big0), other, own, ALU.is_equal)),
        ("eqlt", TT(gg(big0), gg(big0), lt, ALU.mult)),
        ("gt", TT(gg(big1), other, own, ALU.is_gt)),
        ("ahead", TT(gg(big0), gg(big0), gg(big1), ALU.add)),
        ("rank", lambda e: e.tensor_reduce(hi1[:, :], gg3(big0), AX.X, ALU.add)),
        ("gm", lambda e: e.tensor_scalar(hi1[:, :], hi1[:, :], 4.0, None, ALU.is_lt)),
        ("masked", TT(v4, v4, hi1[:, :].unsqueeze(2).to_broadcast([P, NB * G, 4]), ALU.mult)),
        ("masked0", lambda e: e.tensor_scalar(flat(sb), flat(sb), 0.0, None, ALU.add)),
    ], ["sig", "w_w"])
    for b in range(NB):
        q.op("dve", f"top{b}", lambda e, i, b=b: e.max(M["MV"][:, b, :], sb[:, b, :]), after=["masked0"])
    for b in range(NB):
        q.op("dve", f"idx{b}", lambda e, i, b=b: e.max_index(M["MI"][:, b, :], M["MV"][:, b, :], sb[:, b, :]), after=[f"top{b}"])
    idxf, w, pk, val, f0, f1 = (M["tk"][k] for k in range(6))
    io = M["iota"][:, :].unsqueeze(1).unsqueeze(1).to_broadcast([P, NB, K, E0])
    x4 = lambda m: m[:, :, :].unsqueeze(3).to_broadcast([P, NB, K, E0])
    xe = lambda m: m[:, :, :].unsqueeze(2).to_broadcast([P, NB, K, E0])
    red = lambda o, m: (lambda e: e.tensor_reduce(o[:, :, :], ke(m), AX.X, ALU.add))
    chain(q, "dve", [
        ("idxf", lambda e: e.tensor_copy(idxf[:, :, :], M["MI"][:, :, 0:K])),
        ("oh", TT(ke(oh), x4(idxf), io, ALU.is_equal)),
        ("A", lambda e: e.tensor_reduce(M["A"][:, :, :], oh[:, :].rearrange("p (b k e) -> p b e k", k=K, e=E0), AX.X, ALU.add)),
        ("Ab", lambda e: e.tensor_copy(flat(M["Ab"]), flat(M["A"]))),
        ("C0", lambda e: e.memset(M["C"][:, 0, :], 0.0)),
    ] + [(f"C{b}", TT(M["C"][:, b, :], M["C"][:, b - 1, :], M["A"][:, b - 1, :], ALU.add)) for b in range(1, NB)]
      + [("Cb", lambda e: e.tensor_copy(flat(M["Ab2"]), flat(M["C"])))], [f"idx{NB - 1}", "w_w"])
    q.op("pe", "pos0", lambda e, i: e.matmul(BK[0][:, :], M["before"][:, :], flat(M["Ab"]), start=True, stop=False), after=["Ab", "w_w"])
    q.op("pe", "pos1", lambda e, i: e.matmul(BK[0][:, :], M["ones"][:, :], flat(M["Ab2"]), start=False, stop=True), after=["Cb"])
    pos = M["pos"]
    chain(q, "dve", [
        ("wp", TT(ke(big1), ke(oh), xe(sc), ALU.mult)),
        ("w", red(w, big1)),
        ("posc", lambda e: e.tensor_copy(flat(pos), BK[0][:, :])),
        ("pp", TT(ke(big1), ke(oh), xe(pos), ALU.mult)),
        ("pk", red(pk, big1)),
        ("val", lambda e: e.tensor_scalar(val[:, :, :], pk[:, :, :], float(CAP), None, ALU.is_lt)),
        ("e128", lambda e: e.tensor_scalar(idxf[:, :, :], idxf[:, :, :], float(CAP), None, ALU.mult)),
        ("out", lambda e: e.tensor_scalar(f0[:, :, :], val[:, :, :], -2.0 * E0 * CAP, 2.0 * E0 * CAP, ALU.mult, ALU.add)),
        ("s0", TT(f0[:, :, :], f0[:, :, :], idxf[:, :, :], ALU.add)),
        ("s1", TT(f0[:, :, :], f0[:, :, :], pk[:, :, :], ALU.add)),
        ("si", lambda e: e.tensor_copy(M["SI"][:, :, :], f0[:, :, :])),
        ("g0", lambda e: e.tensor_scalar(f1[:, :, :], pk[:, :, :], float(CAP - 1), None, ALU.min)),
        ("g1", TT(f1[:, :, :], f1[:, :, :], idxf[:, :, :], ALU.add)),
        ("gi", lambda e: e.tensor_copy(M["GI"][:, :, :], f1[:, :, :])),
        ("ws", lambda e: e.tensor_reduce(M["ws"][:, :], w[:, :, :], AX.X, ALU.add)),
        ("we", lambda e: e.tensor_scalar(M["ws"][:, :], M["ws"][:, :], 1e-20, None, ALU.add)),
        ("wr", lambda e: e.reciprocal(M["ws"][:, :], M["ws"][:, :])),
        ("wn", TT(w[:, :, :], w[:, :, :], M["ws"][:, :].unsqueeze(2).to_broadcast([P, NB, K]), ALU.mult)),
        ("wv", TT(w[:, :, :], w[:, :, :], val[:, :, :], ALU.mult)),
        ("wg", lambda e: e.tensor_scalar(M["wr"][:, :, :], w[:, :, :], M["tg"][:, 1:2], 2.5, ALU.mult, ALU.mult)),
    ], ["Cb", "pos1"])
    for b in range(NB):
        for k in range(K):
            q.op("pool", f"sc{b}.{k}", lambda e, i, b=b, k=k: e.indirect_dma_start(
                out=M["xe_d"], out_offset=bass.IndirectOffsetOnAxis(ap=M["SI"][:, b, k:k + 1], axis=0),
                in_=M["XN"][:, b, :], in_offset=None, bounds_check=E0 * CAP - 1, oob_is_err=False),
                after=["si", "w_z"], channel=f"scat{(b * K + k) % 8}")


def experts0(q, M, BK):
    U = 4
    at = q.phases[-1]["at"]
    for u in range(U):
        def w(e, i, u=u):
            return e.dma_start(M["EW"][u][:, :], M["ew_d"][bass.ds(i * U + u + U, 1), :, :].rearrange("o p c -> (o p) c"))
        def x(e, i, u=u):
            return e.dma_start(M["XE"][u][:, :], M["xe_d"][bass.ds((i * U + u + U) * CAP, CAP), :])
        q.op("sp", f"ldx{u}", x, after=[(f"et{u}.1", 0)], lag=-1, channel=f"ldx{u}", apart=True)
        q.op("sp", f"ldw{u}", w, after=[(f"ed{u}", 0)], lag=-1, channel=f"ldw{u}", apart=True)
        q.op("sp", f"sty{u}", lambda e, i, u=u: e.dma_start(M["ye_d"][bass.ds((i * U + u) * CAP, CAP), :], M["YE"][u][:, :]),
             after=[f"ey{u}"], channel=f"sty{u}", apart=True)
    for u in range(U):
        v = u % 2
        for a in range(2):
            q.op("pe", f"et{u}.{a}", lambda e, i, u=u, a=a, v=v: e.transpose(
                BK[v][:, 128 * a:128 * a + 128], M["XE"][u][:, 128 * a:128 * a + 128], M["ident"][:, :]),
                after=[(f"ldx{u}", 1), (f"ex{u - 2}", 0) if u >= 2 else (f"ex{u + 2}", 1)])
        q.op("act", f"ex{u}", lambda e, i, v=v: e.activation(M["XeT"][v][:, :], BK[v][:, 0:256], ACT.Copy),
             after=[f"et{u}.1", (f"eu{u - 2}.1", 0) if u >= 2 else (f"eu{u + 2}.1", 1)])
        for a in range(2):
            q.op("pe", f"eu{u}.{a}", lambda e, i, u=u, a=a, v=v: e.matmul(
                BK[2 + v][:, 0:128], M["EW"][u][:, 128 * a:128 * a + 128], M["XeT"][v][:, 128 * a:128 * a + 128],
                start=(a == 0), stop=(a == 1)),
                after=[f"ex{u}", (f"ldw{u}", 1), (f"er{u - 2}", 0) if u >= 2 else (f"er{u + 2}", 1)])
        q.op("act", f"er{u}", lambda e, i, v=v: e.activation(M["EH"][v][:, :], BK[2 + v][:, 0:128], ACT.Relu),
             after=[f"eu{u}.1", (f"ed{u - 2}", 0) if u >= 2 else (f"ed{u + 2}", 1)])
        q.op("dve", f"es{u}", lambda e, i, v=v: e.tensor_tensor(M["EH"][v][:, :], M["EH"][v][:, :], M["EH"][v][:, :], ALU.mult), after=[f"er{u}"])
        q.op("pe", f"ed{u}", lambda e, i, u=u, v=v: e.matmul(
            BK[4 + v][:, 0:256], M["EH"][v][:, :], M["EW"][u][:, 256:512], start=True, stop=True),
            after=[f"es{u}", (f"ey{u - 2}", 0) if u >= 2 else (f"ey{u + 2}", 1)])
        q.op("dve", f"ey{u}", lambda e, i, u=u, v=v: e.tensor_copy(M["YE"][u][:, :], BK[4 + v][:, 0:256]), after=[f"ed{u}", (f"sty{u}", 1)])


def combine0(q, M):
    D = 4
    for b in range(NB):
        for k in range(K0):
            n = b * K0 + k
            q.op("pool", f"ga{n}", lambda e, i, b=b, k=k, n=n: e.indirect_dma_start(
                out=M["GA"][n % 8][:, :], out_offset=None, in_=M["ye_d"],
                in_offset=bass.IndirectOffsetOnAxis(ap=M["GI"][:, b, k:k + 1], axis=0), bounds_check=E0 * CAP - 1, oob_is_err=False),
                after=[f"ca{n - 8}"] if n >= 8 else [], channel=f"scat{n % 8}")
            q.op("dve", f"ca{n}", lambda e, i, b=b, k=k, n=n: e.scalar_tensor_tensor(
                out=M["X"][:, b, :], in0=M["GA"][n % 8][:, :], scalar=M["wr"][:, b, k:k + 1], in1=M["X"][:, b, :],
                op0=ALU.mult, op1=ALU.add), after=[f"ga{n}"] + ([f"ca{n - 1}"] if k else []))


def ffn1(q, M, BK):
    layer_norm_batches(q, M, BK, "L1")
    at = q.phases[-1]["at"]
    L = BK[2]
    for b in range(GB):
        for a in range(2):
            q.op("pe", f"lg{b}.{a}", lambda e, i, b=b, a=a: e.matmul(
                L[:, E1 * b:E1 * b + E1], tokens(M, b, a), M["GW1"][:, a, :], start=(a == 0), stop=(a == 1)),
                after=["xt0", "xt1", ("fx34", 1), "w_w"])
    r = M["r1"]
    s = M["s1"]
    lc, p, m0, m1 = r[0], r[1], r[2], r[3]
    bc = lambda m: m[:, :].unsqueeze(2).to_broadcast([P, GB, E1])
    other = lambda m: m[:, :, :].unsqueeze(2).to_broadcast([P, GB, E1, E1])
    own = lambda m: m[:, :, :].unsqueeze(3).to_broadcast([P, GB, E1, E1])
    lt = M["lt"][:, :, :].unsqueeze(1).to_broadcast([P, GB, E1, E1])
    W = GB * E1 * E1
    gg = lambda m: m[:, 0:W].rearrange("p (b g h) -> p b g h", g=E1, h=E1)
    gg3 = lambda m: m[:, 0:W].rearrange("p (x h) -> p x h", h=E1)
    fl = lambda m: m[:, :, :].rearrange("p b e -> p (b e)")
    q.op("dve", "lc", lambda e, i: e.tensor_copy(fl(lc), L[:, 0:GB * E1]), after=["lg3.1"])
    q.op("dve", "mx", lambda e, i: e.tensor_reduce(s[0][:, :], lc[:, :, :], AX.X, ALU.max), after=["lc"])
    q.op("dve", "sm", lambda e, i: e.tensor_tensor(lc[:, :, :], lc[:, :, :], bc(s[0]), ALU.subtract), after=["mx"])
    q.op("act", "ex", lambda e, i: e.activation(fl(p), fl(lc), ACT.Exp), after=["sm", ("wc", 1)])
    steps = [
        ("su", lambda e: e.tensor_reduce(s[1][:, :], p[:, :, :], AX.X, ALU.add)),
        ("ri", lambda e: e.reciprocal(s[1][:, :], s[1][:, :])),
        ("pr", lambda e: e.tensor_tensor(p[:, :, :], p[:, :, :], bc(s[1]), ALU.mult)),
        ("eq", lambda e: e.tensor_tensor(gg(M["big0"]), other(p), own(p), ALU.is_equal)),
        ("el", lambda e: e.tensor_tensor(gg(M["big0"]), gg(M["big0"]), lt, ALU.mult)),
        ("gt", lambda e: e.tensor_tensor(gg(M["big1"]), other(p), own(p), ALU.is_gt)),
        ("ah", lambda e: e.tensor_tensor(gg(M["big0"]), gg(M["big0"]), gg(M["big1"]), ALU.add)),
        ("rk", lambda e: e.tensor_reduce(fl(m0), gg3(M["big0"]), AX.X, ALU.add)),
        ("se", lambda e: e.tensor_scalar(fl(m0), fl(m0), 2.0, None, ALU.is_lt)),
        ("ps", lambda e: e.tensor_tensor(m1[:, :, :], m0[:, :, :], p[:, :, :], ALU.mult)),
        ("sw", lambda e: e.tensor_reduce(s[2][:, :], m1[:, :, :], AX.X, ALU.add)),
        ("sa", lambda e: e.tensor_scalar(s[2][:, :], s[2][:, :], 1e-20, None, ALU.add)),
        ("sr", lambda e: e.reciprocal(s[2][:, :], s[2][:, :])),
        ("wn", lambda e: e.tensor_tensor(m1[:, :, :], m1[:, :, :], bc(s[2]), ALU.mult)),
        ("wc", lambda e: e.tensor_scalar(M["CW"][:, :, :], m1[:, :, :], M["tg"][:, 3:4], None, ALU.mult)),
    ]
    prev = ["ex"]
    for name, fn in steps:
        q.op("dve", name, lambda e, i, fn=fn: fn(e), after=prev + ([("lastx", 1)] if name == "wc" else []))
        prev = [name]
    work = [("S", 0, [(0, 128), (128, 128), (256, 96)])] + [("E", x, [(0, 88), (88, 88)]) for x in range(E1)]
    n_chunks = sum(len(c) for _, _, c in work)

    def back(kind, n, depth):
        return (f"{kind}{n - depth}", 0) if n >= depth else (f"{kind}{max(m for m in range(n_chunks) if m % depth == n)}", 1)

    n = ndn = 0
    for kind, x, chunks in work:
        first = n
        for lo, size in chunks:
            slot = n % 4
            for w, bk in (("g", 3), ("u", 4)):
                for a in range(2):
                    src = M["SG" if w == "g" else "SP"][:, a, lo:lo + size] if kind == "S" else M["EG" if w == "g" else "EP"][:, x, a, lo:lo + size]
                    q.op("pe", f"{w}{n}.{a}", lambda e, i, src=src, a=a, bk=bk, size=size, n=n: e.matmul(
                        BK[bk + 2 * (n % 2)][0:size, :], src, M["XT"][:, a, :], start=(a == 0), stop=(a == 1)),
                        after=["xt0", "xt1", back("hu", n, 2), "w_f1"])
            q.op("act", f"si{n}", lambda e, i, n=n, size=size, slot=slot: e.activation(
                M["RL"][0:size, slot, :], BK[3 + 2 * (n % 2)][0:size, :], ACT.Silu), after=[f"g{n}.1", back("dr", n, 4)])
            q.op("dve", f"hu{n}", lambda e, i, n=n, size=size, slot=slot: e.tensor_tensor(
                M["RL"][0:size, slot, :], BK[4 + 2 * (n % 2)][0:size, :], M["RL"][0:size, slot, :], ALU.mult), after=[f"si{n}", f"u{n}.1"])
            n += 1
        for b in range(GB):
            D = BK[7 if ndn % 2 else 2]
            for k, (lo, size) in enumerate(chunks):
                slot = (first + k) % 4
                src = M["SDn"][0:size, k, :] if kind == "S" else M["ED"][0:size, x, k, :]
                q.op("pe", f"fd{ndn}.{k}", lambda e, i, D=D, slot=slot, size=size, b=b, src=src, k=k, chunks=chunks: e.matmul(
                    D[:, 0:256], M["RL"][0:size, slot, 128 * b:128 * b + 128], src, start=(k == 0), stop=(k == len(chunks) - 1)),
                    after=[f"hu{first + len(chunks) - 1}", "lc", (f"fx{ndn - 2}", 0) if ndn >= 2 else (f"fx{34 + ndn}", 1), "w_f1"])
            sc = M["tg"][:, 3:4] if kind == "S" else M["CW"][:, b, x:x + 1]
            X = lambda i, b=b: M["X"][:, bass.ds(i * GB + b, 1), :][:, 0, :]
            q.op("dve", f"fx{ndn}", lambda e, i, D=D, sc=sc, X=X: e.scalar_tensor_tensor(
                out=X(i), in0=D[:, 0:256], scalar=sc, in1=X(i), op0=ALU.mult, op1=ALU.add),
                after=[f"fd{ndn}.{len(chunks) - 1}", "wc"] + ([f"fx{ndn - 4}"] if ndn >= 4 else []))
            for k in range(len(chunks)):
                if b == GB - 1:
                    at[f"dr{first + k}"] = at[f"fd{ndn}.{len(chunks) - 1}"]
            ndn += 1
    at["xt.read"] = at[f"u{n - 1}.1"]
    at["lastx"] = at[f"fx{ndn - 1}"]




def build(nc, d, out):
    ctx = ExitStack()
    with ctx:
        sb = lambda name, shape, dt=F32: ctx.enter_context(nc.sbuf_tensor(name, shape, dt))
        q = Queue(nc, ctx)
        for e in ENGINES[:4]:
            q.channel(e)
        M = {}
        X = M["X"] = sb("X", [P, NB, T])
        for nm in ("Wq", "Wk", "Wv", "Wo"):
            M[nm] = sb(nm, [P, P])
        for nm in ("bq", "bk", "bo"):
            M[nm] = sb(nm, [P, 1])
        M["bv"] = sb("bv", [P, P])
        M["ident"] = sb("ident", [P, P]); M["perm"] = sb("perm", [P, P])
        M["dn"] = sb("dn", [P, 32]); M["rdn"] = sb("rdn", [P, 32]); M["bog"] = sb("bog", [P, 1])
        M["tg"] = sb("tg", [P, 4]); M["graw"] = sb("graw", [P, 5])
        M["mhalf"] = sb("mhalf", [P, 1])
        for nm, shape, dt in (
                              ("VA", [P, 2, 16, 32], F32), ("QKc", [P, 2, T], F32), ("QKs", [P, 3, 2, T], BF16),
                               ("Cb", [P, T], F32), ("st6", [P, 6], F32), ("mv", [P, 2], F32),
                              ("ve", [P, 1], F32), ("rs", [P, 1], F32), ("mx", [P, 2, 16], F32), ("mxT", [16, T], BF16)):
            M[nm] = [sb(f"{nm}{n}", shape, dt) for n in range(2)]
        M["Xn"] = sb("Xn", [P, T]); M["OS"] = sb("OS", [P, 4, T]); M["rd"] = sb("rd", [P, T]); M["on"] = sb("on", [P, T])
        PXs = sb("PX", [P, 4, 1024])
        M["PX"] = [PXs[:, n, :] for n in range(4)]
        M["big0"], M["big1"] = (PXs[:, 2 * n:2 * n + 2, :].rearrange("p a c -> p (a c)") for n in range(2))
        M["QS"] = [sb(f"QS{n}", [P, 16, 2, T], BF16)[:, :, :, :] for n in range(2)]
        spare = sb("spare", [P, 8192])
        M["XN"], M["oh"] = spare[:, 0:4096].rearrange("p (b t) -> p b t", b=NB), spare[:, 4096:6144]
        for k, nm in enumerate(("sc", "scb", "A", "C")):
            M[nm] = spare[:, 6144 + 512 * k:6656 + 512 * k].rearrange("p (b e) -> p b e", b=NB)
        for nm, shape, dt in (("st4", [P, GB, 6], F32), ("mv4", [P, GB, 2], F32), ("ve4", [P, GB], F32),
                              ("rs4", [P, GB], F32), ("mhalf4", [P, GB], F32), ("XT", [P, 2, 512], F32), ("GW", [P, 2, E0], F32),
                              ("LG", [P, NB, E0], F32), ("SU", [P, 2, HS], F32), ("SD", [P, 4, T], F32), ("RL", [P, 4, 512], F32),
                              ("lt", [P, 8, 8], F32),
                              ("MV", [P, NB, 8], F32), ("MI", [P, NB, 8], U32), ("bc", [P, E0], F32), ("iota", [P, E0], F32),
                              
                              ("Ab", [P, NB, E0], BF16), ("Ab2", [P, NB, E0], BF16), 
                              ("before", [P, P], BF16), ("ones", [P, P], BF16), ("SI", [P, NB, K0], U32), ("GI", [P, NB, K0], U32),
                              ("ws", [P, NB], F32), ("wr", [P, NB, K0], F32), ("CW", [P, GB, E1], F32), ("GW1", [P, 2, E1], F32),
                              ("SG", [P, 2, ISH], F32), ("SP", [P, 2, ISH], F32), ("SDn", [P, 3, T], F32),
                              ("EG", [P, E1, 2, I1], F32), ("EP", [P, E1, 2, I1], F32), ("ED", [88, E1, 2, T], F32)):
            M[nm] = sb(nm, shape, dt)
        for nm, n, shape in (("tk", 6, [P, NB, K0]), 
                             ("EH", 2, [P, P]), ("r1", 4, [P, GB, E1]), ("s1", 3, [P, GB])):
            M[nm] = [sb(f"{nm}{k}", shape) for k in range(n)]
        M["QS"] += [spare[:, 4096 * n:4096 * n + 4096].bitcast(BF16).rearrange("p (g s t) -> p g s t", g=16, s=2)
                    for n in range(2)]
        M["XC"] = [M["Xn"], M["rd"]]
        M["XeT"] = M["Cb"]
        M["pos"] = M["RL"][:, 2, :].rearrange("p (b e) -> p b e", b=NB)
        M["before32"] = M["on"][:, 0:P]
        M["rt"] = [M["RL"][:, k % 4, P * (k // 4):P * (k // 4) + P] for k in range(5)]
        M["EW"] = [M["RL"][:, k, :] for k in range(4)]
        M["XE"] = [M["OS"][:, k, :] for k in range(4)]
        M["YE"] = [M["QKc"][k // 2][:, k % 2, :] for k in range(4)]
        M["GA"] = [M["oh"][:, T * k:T * k + T] for k in range(8)]
        M["xe_d"] = nc.dram_tensor("xe", [E0 * CAP, T], F32, kind="Internal").ap()
        M["ye_d"] = nc.dram_tensor("ye", [E0 * CAP, T], F32, kind="Internal").ap()
        M["ew_d"] = d["ew"]
        ps = lambda name, w=512: ctx.enter_context(nc.psum_tensor(name, [P, w], F32))
        M["S"] = [ps("S0"), ps("S1")]; M["ST"] = [ps(f"ST{n}", 1024) for n in range(2)]
        M["O"] = ps("O"); M["M1"] = ps("M1")
        ST = M["ST"]
        BK = [M["S"][0][:, :], M["S"][1][:, :]] + [ST[n][:, 512 * k:512 * k + 512] for n in range(2) for k in range(2)] + [M["O"][:, :], M["M1"][:, :]]
        M["ctx_d"] = d["ctx"].rearrange("b c t -> c b t")

        q.phase()
        ld = lambda dst, src, ch="w_w": q.op("sp", f"ld.{len(q.phases[-1]['at'])}", lambda e, i: e.dma_start(dst, src), channel=ch)
        ld(X[:, :, :], d["x"].rearrange("b c t -> c b t"), "w_x")
        M["hbL0"] = sb("hbL0", [16, P]); M["hbL1"] = sb("hbL1", [8, P]); M["rT"] = sb("rT", [16, T])
        for nm in ("Wq", "Wk", "Wv", "Wo", "ident", "hbL0", "hbL1", "perm"):
            ld(M[nm][:, :], d[nm])
        for nm in ("bq", "bk", "bo"):
            ld(M[nm][:, :], d[nm])
        ld(M["bv"][:, :], d["bv"].to_broadcast([P, P]))
        ld(M["graw"][:, :], d["graw"].to_broadcast([P, 5]), "w_g")
        for nm in ("GW", "GW1", "SU", "SD", "lt", "before32", "SG", "SP", "SDn", "EG", "EP", "ED"):
            ld(M[nm][tuple(slice(None) for _ in M[nm].shape)], d[nm], "w_s0" if nm in ("SU", "SD") else "w_f1" if nm in ("SG", "SP", "SDn", "EG", "EP", "ED") else "w_w")
        for nm in ("bc", "iota"):
            ld(M[nm][:, :], d[nm].to_broadcast([P, E0]))
        q.op("dve", "ones", lambda e, i: e.memset(M["ones"][:, :], 1.0))
        q.op("dve", "mhalf4", lambda e, i: e.memset(M["mhalf4"][:, :], -0.5))
        q.op("dve", "before", lambda e, i: e.tensor_copy(M["before"][:, :], M["before32"][:, :]), after=["w_w"])
        q.op("dve", "zero", lambda e, i: e.memset(M["LG"][:, :, :], 0.0))
        q.op("sp", "z", lambda e, i: e.dma_start(
            M["xe_d"].rearrange("(p b c) t -> p b (c t)", p=P, c=2),
            M["LG"][:, :, :].rearrange("p b e -> p (b e)").unsqueeze(1).to_broadcast([P, 16, 512])), after=["zero"], channel="w_z")
        for n in range(U):
            q.op("dve" if n % 2 else "pool", f"one.QS{n}", lambda e, i, n=n: e.memset(M["QS"][n][:, :, :, :], 0.0))
            q.op("dve", f"row.QS{n}", lambda e, i, n=n: e.memset(M["QS"][n][STACK:STACK + 1, :, 1, :], 1.0), after=[f"one.QS{n}"])
        for n in range(2):
            q.op("dve", f"one.VA{n}", lambda e, i, n=n: e.memset(M["VA"][n][:, :, :, :], 1.0))
        q.op("dve", "mhalf", lambda e, i: e.memset(M["mhalf"][:, :], -0.5))
        q.op("act", "gates", lambda e, i: e.activation(M["tg"][:, :], M["graw"][:, 0:4], ACT.Tanh), after=["w_g"])
        q.op("dve", "gamma", lambda e, i: e.tensor_tensor(M["tg"][:, 2:3], M["tg"][:, 2:3], M["graw"][:, 4:5], ALU.mult), after=["gates"])
        q.op("dve", "bog", lambda e, i: e.tensor_tensor(M["bog"][:, :], M["bo"][:, :], M["tg"][:, 0:1], ALU.mult), after=["gates", "w_w"])

        q.phase(NB // U)
        A = Attention("L0", 16, 8)
        for hb in range(U):
            attention_half(q, A, M, hb)

        q.phase(NGRP)
        shared0(q, M, BK)
        q.phase()
        route0(q, M, BK)
        q.phase(E0 // 4)
        experts0(q, M, BK)
        q.phase()
        combine0(q, M)
        for n in (2, 3):
            q.op("dve", f"one.QS{n}", lambda e, i, n=n: e.memset(M["QS"][n][STACK:STACK + 1, :, 1, :], 1.0), after=[f"ca{NB * K0 - 1}"])
        q.phase(NB // U)
        A = Attention("L1", 8, 16)
        for hb in range(U):
            attention_half(q, A, M, hb)
        q.phase(NGRP)
        ffn1(q, M, BK)

        q.phase()
        q.op("sp", "store", lambda e, i: e.dma_start(out.rearrange("b c t -> c b t"), X[:, :, :]), channel="st")
        q.emit()


def orders():
    p = np.arange(128)
    cx = 16 * (p % 8) + p // 8
    cq = 8 * (p % 16) + p // 16
    cv = 8 * (4 * (p // 32) + p % 4) + p % 32 // 4
    cw = 16 * (2 * (p // 32) + p % 2) + p % 32 // 2
    return cx, cq, cv, cw


def layout(inp):
    a = {k: np.asarray(v) for k, v in inp.items()}
    cx, cq, cv, cw = orders()
    d = {"x": a["x"][:, cx, :], "ctx": a["ctx_2048"][:, cx, :]}
    for n in "qkv":
        d["W" + n] = a["L0_xattn_W" + n][cv if n == "v" else cq][:, cx].T
    d["Wo"] = a["L0_xattn_Wo"][cx][:, cv].T
    for n in "qk":
        d["b" + n] = a["L0_xattn_b" + n][cq].reshape(128, 1)
    d["bv"] = a["L0_xattn_bv"][cv].reshape(1, 128)
    d["perm"] = np.equal(cw[:, None], cx[None, :]).astype(np.float32)
    d["bo"] = a["L0_xattn_bo"][cx].reshape(128, 1)
    d["graw"] = np.stack([a["g_xattn"][0], a["g_ffn"][0], a["g_xattn"][1], a["g_ffn"][1], a["L1_xattn_gamma"]]).reshape(1, 5)
    d["ident"] = np.eye(128, dtype=np.float32)
    for nm, G, R in (("hbL0", 4, 8), ("hbL1", 2, 16)):
        s = d[nm] = np.zeros((4 * G, 128), np.float32)
        for j in range(4):
            for i in range(R):
                for g in range(G):
                    s[G * j + g, 32 * j + G * i + g] = 1
    up, down = a["L0_ffn_up_w"], a["L0_ffn_down_w"]
    d["ew"] = np.concatenate([up.transpose(0, 2, 1)[:, 0:128], up.transpose(0, 2, 1)[:, 128:256], down.transpose(0, 2, 1)], axis=2)
    halves = lambda w: w.T.reshape(2, 128, -1).transpose(1, 0, 2)
    d["GW"], d["GW1"], d["SU"] = halves(a["L0_ffn_gate_w"]), halves(a["L1_ffn_gate_w"]), halves(a["L0_ffn_shared_up_w"])
    d["SG"], d["SP"] = halves(a["L1_ffn_shared_gate"]), halves(a["L1_ffn_shared_up"])
    d["SD"] = a["L0_ffn_shared_down_w"].T.reshape(4, 128, 256).transpose(1, 0, 2)
    d["SDn"] = np.zeros((3, 128, 256), np.float32)
    d["SDn"].reshape(384, 256)[0:352] = a["L1_ffn_shared_down"].T
    d["SDn"] = d["SDn"].transpose(1, 0, 2)
    for nm, w in (("EG", "gate"), ("EP", "up")):
        d[nm] = a["L1_ffn_expert_" + w].transpose(2, 0, 1).reshape(2, 128, 8, 176).transpose(1, 2, 0, 3)
    d["ED"] = a["L1_ffn_expert_down"].transpose(0, 2, 1).reshape(8, 2, 88, 256).transpose(2, 0, 1, 3)
    d["lt"] = np.broadcast_to(np.tril(np.ones((8, 8), np.float32), -1), (128, 8, 8))
    d["iota"] = np.arange(32, dtype=np.float32).reshape(1, 32)
    d["bc"] = a["L0_ffn_bias_corr"].reshape(1, 32)
    d["before32"] = np.less(cx[:, None], cx[None, :]).astype(np.float32)
    return {k: np.ascontiguousarray(v) for k, v in d.items()}


def kernel(**inputs):
    import concourse.bacc as bacc
    from concourse.bass_utils import run_bass_kernel_spmd

    nc = bacc.Bacc("TRN2", target_bir_lowering=False, num_devices=1)
    arrays = {f"in_{name}": array for name, array in layout(inputs).items()}
    args = {name[3:]: nc.dram_tensor(name, a.shape, mybir.dt.from_np(a.dtype), kind="ExternalInput").ap()
            for name, a in arrays.items()}
    out = nc.dram_tensor("out", (NB, C, T), F32, kind="ExternalOutput").ap()
    build(nc, args, out)
    r = run_bass_kernel_spmd(nc, [arrays], core_ids=[0])
    got = r.results[0]["out"]
    cx = orders()[0]
    inverse = [int(np.nonzero(cx == c)[0][0]) for c in range(C)]
    return got[:, inverse, :]
```

```python
from contextlib import ExitStack

import numpy as np
import concourse.bass as bass
from concourse import mybir

F32 = mybir.dt.float32
BF16 = mybir.dt.bfloat16
U32 = mybir.dt.uint32
I32 = mybir.dt.int32
ALU = mybir.AluOpType
ACT = mybir.ActivationFunctionType
AX = mybir.AxisListType
P = 128
ENGINES = ("pe", "dve", "act", "pool", "sp")


class Queue:

    def __init__(self, nc, ctx):
        self.nc, self.ctx = nc, ctx
        self.sem = {}
        self.phases = []
        self.sem["pad"] = ctx.enter_context(nc.semaphore("s_pad"))

    def channel(self, name):
        if name not in self.sem:
            self.sem[name] = self.ctx.enter_context(self.nc.semaphore("s_" + name))
        return name

    def phase(self, n=1):
        self.phases.append(dict(n=n, lags={0}, ops={e: [] for e in ENGINES}, at={}, count={}))

    def op(self, engine, name, fn, after=(), lag=0, channel=None, apart=False):
        ph = self.phases[-1]
        ch = self.channel(channel or engine)
        k = ph["count"].get(ch, 0)
        ph["count"][ch] = k + 1
        ph["lags"].add(lag)
        assert name not in ph["at"], name
        ph["at"][name] = (ch, k)
        ph["ops"][engine].append((name, ch, k, fn, [(a, 0) if isinstance(a, str) else a for a in after], lag, apart))

    def emit(self):
        total = {c: 0 for c in self.sem if c != "pad"}
        step = {c: 1 if c in ENGINES else 16 for c in total}
        plans = []
        for ph in self.phases:
            runs = ph["n"] + max(ph["lags"]) - min(ph["lags"])
            start = dict(total)
            for c, m in ph["count"].items():
                total[c] += m * (ph["n"] if c.startswith("soft") else runs)
            plans.append((ph, runs, start, dict(total)))
        programs = {}
        for e in ENGINES:
            programs[e] = self._program(e, plans, step)
        with self.nc.Block() as block:
            for e in ("sp", "pool", "act", "pe", "dve"):
                of_block(block, e)(programs[e])

    def _program(self, e, plans, step):
        q = self

        def program(eng):
            seen = {}

            def wait(sem, value):
                if isinstance(value, int):
                    if value <= 0 or seen.get(sem, 0) >= value:
                        return
                    seen[sem] = value
                eng.wait_ge(q.sem[sem], value)
                if e == "sp" and not isinstance(value, int):
                    eng.sem_inc(q.sem["pad"], 1)

            for n_ph, (ph, runs, start, end) in enumerate(plans):
                if n_ph and ph["ops"][e]:
                    for c, v in start.items():
                        if v and not c.startswith("w_"):
                            wait(c, v * step[c])

                def iteration(r, i):
                    skipped = {}
                    inside = {}

                    def flush(c):
                        if skipped.get(c):
                            base = start[c] + ph["count"][c] * r
                            k0, m = skipped.pop(c)
                            wait(c, (base + k0) * step[c])
                            eng.sem_inc(q.sem[c], m * step[c])

                    issued = set()
                    for name, ch, k, fn, after, lag, apart in ph["ops"][e]:
                        if isinstance(i, int) and not 0 <= i - lag < ph["n"]:
                            if ch.startswith("soft"):
                                assert lag == min(ph["lags"])
                                continue
                            k0, m = skipped.get(ch, (k, 0))
                            skipped[ch] = (k0, m + 1)
                            continue
                        for c in list(skipped):
                            flush(c)
                        need = {}
                        for a, d in after:
                            if a.startswith("w_"):
                                if not (d and isinstance(i, int) and i < 0):
                                    need[a] = end[a] * step[a]
                                continue
                            c, ka = ph["at"][a]
                            off = start[c] + ka + 1 - d * ph["count"][c]
                            need[c] = max(need.get(c, -10**9), off)
                        for c, off in need.items():
                            if c.startswith("w_"):
                                wait(c, off)
                                continue
                            if isinstance(r, int):
                                v = off + ph["count"][c] * r
                                if c.startswith("soft"):
                                    v = min(v, start[c] + ph["count"][c] * ph["n"])
                                if off + ph["count"][c] * r > start[c]:
                                    wait(c, v * step[c])
                            elif off > inside.get(c, -10**9):
                                inside[c] = off
                                wait(c, (r * ph["count"][c] + off) * step[c])
                        if apart and e != "sp" and not isinstance(r, int) and need:
                            eng.sem_inc(q.sem["pad"], 1)
                        made = fn(eng, i)
                        made.then_inc(q.sem[ch], step[ch])
                    for c in list(skipped):
                        flush(c)

                if not ph["ops"][e]:
                    continue
                lo, hi = min(ph["lags"]), ph["n"] + max(ph["lags"])
                full = (max(ph["lags"]), ph["n"] + min(ph["lags"]))
                if full[0] == lo:
                    full = (lo + 1, full[1])
                for i in range(lo, min(full[0], hi)):
                    iteration(i - lo, i)
                if full[1] > full[0]:
                    with eng.Fori(full[0], full[1]) as i:
                        iteration(i - lo, i)
                    seen.clear()
                for i in range(max(full), hi):
                    iteration(i - lo, i)
            if e == "sp":
                for c, v in plans[-1][3].items():
                    wait(c, v * step[c])

        return program


def of_block(block, engine):
    return {"sp": block.sync, "pool": block.gpsimd, "act": block.scalar, "pe": block.tensor, "dve": block.vector}[engine]



NB, C, T = 16, 128, 256
E0, H0, CAP, K0 = 32, 128, 128, 4
HS = 512
E1, I1, ISH = 8, 176, 352
EPS = 1e-5
STACK = 96
U = 4
TERMS = ((0, 0), (1, 0), (2, 0), (0, 1), (1, 1), (0, 2))


class Attention:
    def __init__(self, name, H, R):
        self.name, self.H, self.R = name, H, R
        self.NQ = H // 4
        self.scale = float(R) ** -0.5


def attention_step(q, A, M, hb):
    R, H, NQ, L0 = A.R, A.H, A.NQ, A.name == "L0"
    skew = {0: 3, 1: 2, 2: 1, 3: 0, 4: -1, 5: -2, 6: 4}
    B = {s: hb + k for s, k in skew.items()}
    lag = {s: -(b // U) for s, b in B.items()}
    n0, n1, n2, n3, n4, n5, n6 = (B[s] % U for s in range(7))
    QS, QKc, QKs, VA, M1, PX = M["QS"], M["QKc"], M["QKs"], M["VA"], M["M1"], M["PX"]
    at = q.phases[-1]["at"]

    def of(kind, stage, batch, end=""):
        return (f"{kind}{batch % U}{end}", -((batch - skew[stage]) // U))

    def x_at(i, batch):
        return M["X"][:, bass.ds(i * U + batch, 1), :][:, 0, :]

    def back(kind, n, per):
        return (f"{kind}{n % (U * per)}", 0 if n >= 0 else 1)

    readers = [("mt", 3, ".1"), ("va", 2, ""), ("kc", 0, ""), ("mt", 2, ".0"), ("on", 5, ""), ("yb" if L0 else "x", 5, "")]
    if not L0:
        readers.pop(2)

    def bank_free(reader):
        p = readers.index(reader)
        return [of(k, s, B[s] - (n >= p), end) for n, (k, s, end) in enumerate(readers)]

    def pv(batch, quad):
        batch, quad = batch + quad // NQ, quad % NQ
        return of("pv", 4 if quad == NQ - 1 else 3, batch, f".{quad}")

    def score(k):
        n = hb * H + k
        for a in range(2):
            q.op("pe", f"s{n}.{a}", lambda e, i, a=a: e.matmul(
                M["S"][n % 2][:, 256 * a:256 * a + 256], QS[n2][0:STACK, k, 0, 128 * a:128 * a + 128],
                QS[n2][0:STACK, k, 1, :], start=True, stop=True), after=[of("sp", 1, B[2]), of("max", 2, B[2] - (k < 2), f".{(k - 2) % H}")], lag=lag[2])
        q.op("dve", f"max{n2}.{k}", lambda e, i: e.tensor_reduce(
            M["mx"][n2 % 2][:, :, k], M["S"][n % 2][:, :].rearrange("p (a s) -> p a s", a=2), AX.X, ALU.max, negate=True),
            after=[f"s{n}.1", of("mtT", 3, B[2] - 2, ".1.1")], lag=lag[2])

    def score_t(m, u):
        pair = hb * (H // 2) + m
        bank = M["ST"][pair % 2]
        for a in range(2):
            q.op("pe", f"st{pair}.{u}{a}", lambda e, i, a=a: e.matmul(
                bank[:, 512 * u + 256 * a:512 * u + 256 * a + 256], QS[n3][0:STACK + 1, 2 * m + u, 1, 128 * a:128 * a + 128],
                QS[n3][0:STACK + 1, 2 * m + u, 0, :], start=True, stop=True),
                after=[of("mrow", 3, B[3], ".1") if 2 * m >= H // 2 else of("mrow", 2, B[3], ".0"), of("sp", 1, B[3]), back("exp", pair - 2, H // 2)])
        if u == 1:
            q.op("act", f"exp{pair}", lambda e, i: e.activation(PX[pair % 4][:, :], bank[:, :], ACT.Exp, scale=A.scale),
                 after=[f"st{pair}.11", pv(B[3], m // 2 - 2)])

    def values(quad):
        O = M["O"]
        stage = 4 if quad == NQ - 1 else 3
        n = B[stage] % U
        for a in range(2):
            for u in range(4):
                pair = n * (H // 2) + 2 * quad + u // 2
                exp = (f"exp{pair}", -(B[stage] // U))
                q.op("pe", f"pv{n}.{quad}" if (a, u) == (1, 3) else f"pv{n}.{quad}.{a}.{u}", lambda e, i, a=a, u=u, pair=pair: e.matmul(
                    O[32 * u:32 * u + 32, 256 * (quad % 2):256 * (quad % 2) + 256], VA[n % 2][:, a, 4 * quad + u, :],
                    PX[pair % 4][:, 512 * (u % 2) + 256 * a:512 * (u % 2) + 256 * a + 256], start=(a == 0), stop=(a == 1)),
                    after=[exp, of("va", 2, B[stage]), oe(B[stage], quad // 2 - 1)], lag=lag[stage])
        if quad % 2 == 1:
            q.op("act", f"oe{n}.{quad // 2}", lambda e, i: e.activation(
                M["OS"][:, quad - 1:quad + 1, :], O[:, :].rearrange("p (g t) -> p g t", g=2), ACT.Copy),
                after=[f"pv{n}.{quad}", of("num", 4, B[stage] - 1), of("den", 4, B[stage] - 1)], lag=lag[stage])

    def oe(batch, k):
        batch, k = batch + k // (NQ // 2), k % (NQ // 2)
        return of("oe", 4 if k == NQ // 2 - 1 else 3, batch, f".{k}")

    def norm():
        n, g = n0, lag[0]
        Xb = lambda i: x_at(i, B[0])
        q.op("dve", f"bn{n}", lambda e, i: e.bn_stats(M["st6"][n % 2][:, :], Xb(i)), 
             after=["w_x"] + [("w_x2", 1)] * (lag[0] < 0) + ([] if L0 else [of("ca", 6, B[0], ".3")]), lag=g, apart=True)
        q.op("dve", f"bna{n}", lambda e, i: e.bn_aggr(M["mv"][n % 2][:, :], M["st6"][n % 2][:, :]), after=[f"bn{n}", of("xn", 0, B[0] - 2)], lag=g, apart=True)
        q.op("dve", f"ve{n}", lambda e, i: e.tensor_scalar(M["ve"][n % 2][:, :], M["mv"][n % 2][:, 1:2], EPS, None, ALU.add), after=[f"bna{n}"], lag=g)
        q.op("pool", f"rs{n}", lambda e, i: e.tensor_tensor(M["rs"][n % 2][:, :], M["ve"][n % 2][:, :], M["mhalf"][:, :], ALU.pow),
             after=[f"ve{n}", of("xn", 0, B[0] - 2)], lag=g)

    def norm2():
        n, g = n0, lag[0]
        Xb = lambda i: x_at(i, B[0])
        q.op("dve", f"xn{n}", lambda e, i: e.tensor_scalar(
            M["Xn"][:, :] if L0 else QKc[n % 2][:, 0, :], Xb(i), M["mv"][n % 2][:, 0:1], M["rs"][n % 2][:, 0:1], ALU.subtract, ALU.mult),
            after=[f"rs{n}", of("qp", 0, B[0] - 1) if L0 else of("res2.", 0, B[0] - 2)], lag=g)

    def keys_in():
        n = n0
        q.op("sp", f"ldc{n}", lambda e, i: e.dma_start(
            M["Cb"][n][:, :], M["ctx_d"][:, bass.ds(i * U + B[0], 1), :][:, 0, :]),
             after=[of("vt", 2, B[0] - U), of("kp" if L0 else "kc", 0, B[0] - U)], lag=lag[0], channel=f"ldc{n}", apart=True)

    def project():
        n, g = n0, lag[0]
        free = [of("res2.", 0, B[0] - 2)]
        if L0:
            q.op("pe", f"qp{n}", lambda e, i: e.matmul(M1[:, 0:256], M["Wq"][:, :], M["Xn"][:, :], start=True, stop=True),
                 after=[f"xn{n}", "w_w"] + bank_free(("kc", 0, "")), lag=g)
            q.op("pe", f"kp{n}", lambda e, i: e.matmul(M1[:, 256:512], M["Wk"][:, :], M["Cb"][n][:, :], start=True, stop=True),
                 after=[f"ldc{n}"], lag=g)
            q.op("act", f"qc{n}", lambda e, i: e.activation(QKc[n % 2][:, 0, :], M1[:, 0:256], ACT.Identity, bias=M["bq"][:, 0:1]),
                 after=[f"kp{n}"] + free, lag=g)
            q.op("act", f"kc{n}", lambda e, i: e.activation(QKc[n % 2][:, 1, :], M1[:, 256:512], ACT.Identity, bias=M["bk"][:, 0:1]),
                 after=[f"kp{n}"] + free, lag=g)
        else:
            q.op("act", f"kc{n}", lambda e, i: e.activation(QKc[n % 2][:, 1, :], M["Cb"][n][:, :], ACT.Copy), after=[f"ldc{n}"] + free, lag=g)
            at[f"qc{n}"] = at[f"xn{n}"]
        q.op("act", f"cut0.{n}", lambda e, i: cut(e, 0), after=[f"qc{n}", f"kc{n}", of("sp", 1, B[0] - 2)], lag=g, apart=True)
        q.op("pool", f"res1.{n}", lambda e, i: e.tensor_tensor(QKc[n % 2][:, :, :], QKc[n % 2][:, :, :], part(0), ALU.subtract), after=[f"cut0.{n}"], lag=g)

    part = lambda k: QKs[n0 % 2][:, k, :, :]

    def cut(e, k):
        return e.activation(part(k), QKc[n0 % 2][:, :, :], ACT.Copy)

    def project2():
        n, g = n0, lag[0]
        q.op("act", f"cut1.{n}", lambda e, i: cut(e, 1), after=[f"res1.{n}"], lag=g, apart=True)
        q.op("pool", f"res2.{n}", lambda e, i: e.tensor_tensor(part(2), QKc[n % 2][:, :, :], part(1), ALU.subtract), after=[f"cut1.{n}"], lag=g)

    def gather():
        n, g = n6, lag[6]
        row = lambda m, i: m[:, bass.ds(i * U + B[6], 1), :][:, 0, :]
        q.op("dve", f"gic{n}", lambda e, i: e.tensor_copy(M["GIf"][n % 2][:, :], row(M["GI"], i)), after=[of("ga", 6, B[6] - 2, ".3")], lag=g)
        q.op("dve", f"wrc{n}", lambda e, i: e.tensor_copy(M["wrf"][n % 2][:, :], row(M["wr"], i)), after=[of("ca", 6, B[6] - 2, ".3")], lag=g)
        for k in range(K0):
            q.op("pool", f"ga{n}.{k}", lambda e, i, k=k: e.indirect_dma_start(
                out=M["GA"][K0 * (n % 2) + k], out_offset=None, in_=M["ye_d"],
                in_offset=bass.IndirectOffsetOnAxis(ap=M["GIf"][n % 2][:, k:k + 1], axis=0), bounds_check=E0 * CAP - 1, oob_is_err=False),
                after=[f"gic{n}", of("ca", 6, B[6] - 2, f".{k}")], lag=g, channel=f"soft{n}.{k}", apart=True)

    def combine():
        n, g = n6, lag[6]
        for k in range(K0):
            q.op("dve", f"ca{n}.{k}", lambda e, i, k=k: e.scalar_tensor_tensor(
                out=x_at(i, B[6]), in0=M["GA"][K0 * (n % 2) + k], scalar=M["wrf"][n % 2][:, k:k + 1], in1=x_at(i, B[6]),
                op0=ALU.mult, op1=ALU.add), after=[f"ga{n}.{k}", f"wrc{n}"] + ([f"ca{n}.{k - 1}"] if k else []), lag=g)

    def spread(which):
        n = n1
        for k in range(len(TERMS))[which]:
            a, b = TERMS[k]

            def f(e, i, k=k, x=2 * a, y=2 * b + 1):
                parts = QKs[n % 2][:, :, :, :].rearrange("p k s t -> p (k s) t")
                pair = parts[:, x:y + 1:y - x, :] if y > x else parts[:, x:y - 1 if y else None:y - x, :]
                return e.dma_start(QS[n][R * k:R * k + R, 0:H, :, :], pair)
            q.op("sp", f"sp{n}" if k == len(TERMS) - 1 else f"sp{n}.{k}", f,
                 after=[of("res2.", 0, B[1]), of("st.done", 3, B[1] - U)], lag=lag[1], channel=f"sp{n}")

    def values_in():
        n, g = n2, lag[2]
        for a in range(2):
            if L0:
                f = lambda e, i, a=a: e.matmul(M1[:, 128 * a:128 * a + 128], M["Cb"][n][:, 128 * a:128 * a + 128], M["Wv"][:, :], start=True, stop=True)
            else:
                f = lambda e, i, a=a: e.transpose(M1[:, 128 * a:128 * a + 128], M["Cb"][n][:, 128 * a:128 * a + 128], M["ident"][:, :])
            q.op("pe", f"vt{n}" if a else f"vt{n}.0", f, after=[of("ldc", 0, B[2]), "w_w"] + bank_free(("va", 2, "")), lag=g)
        for a in range(2):
            def f(e, i, a=a):
                cols = M1[:, 128 * a:128 * a + 128]
                if L0:
                    v = lambda ap: ap.rearrange("p (c r g) -> p c g r", c=4, g=NQ)
                    o = VA[n % 2][:, a, 0:H, 0:32:NQ].rearrange("p (g c) r -> p c g r", c=4)
                    return e.tensor_tensor(o, v(cols), v(M["bv"][:, :]), ALU.add)
                return e.activation(VA[n % 2][:, a, 0:H, 0:32:NQ], cols.rearrange("p (r k) -> p k r", k=H), ACT.Copy)
            q.op("dve" if L0 else "act", f"va{n}" if a else f"va{n}.0", f, after=[f"vt{n}", pv(B[2] - 2, NQ - 1)], lag=g)

    def maxima(part):
        stage = 2 + part
        n, g = B[stage] % U, lag[stage]
        hh = H // 2
        for a in range(2):
            q.op("pe", f"mtT{n}.{part}.{a}", lambda e, i, a=a: e.transpose(
                M1[0:hh, 256 + 128 * a:384 + 128 * a], M["mx"][n % 2][:, a, hh * part:hh * part + hh], M["ident"][:, :]),
                after=[of("max", 2, B[stage], f".{hh * part + hh - 1}")] + bank_free(("mt", stage, f".{part}")), lag=g)
        q.op("act", f"mt{n}.{part}", lambda e, i: e.activation(M["mxT"][n % 2][0:hh, part, :], M1[0:hh, 256:512], ACT.Copy),
             after=[f"mtT{n}.{part}.1", of("mrow", stage, B[stage] - 2, f".{part}")], lag=g)
        q.op("sp", f"mrow{n}.{part}", lambda e, i: e.dma_start(
            QS[n][STACK:STACK + 1, hh * part:hh * part + hh, 0, :], M["mxT"][n % 2][0:hh, part, :]),
             after=[f"mt{n}.{part}", of("st.done", 3, B[stage] - U)], lag=g, channel=f"mrow{n}.{part}")

    W = 2 * H

    def heads_out():
        n, g = n4, lag[4]
        q.op("sp", f"den{n}", lambda e, i: e.dma_start(M["dn"][:, 0:W], M["OS"][1:98:32, 0:NQ, :]),
             after=[oe(B[4], NQ // 2 - 1), of("rr", 5, B[4] - 1)], channel=f"den{n}", lag=g)
        q.op("sp", f"num{n}", lambda e, i: e.dma_start(M["on"][n % 2][:, :], M["OS"][0:P:NQ, 0:NQ, :]),
             after=[oe(B[4], NQ // 2 - 1), of("pm", 5, B[4] - 2)], channel=f"num{n}", lag=g)

    def reciprocals():
        n, g = n5, lag[5]
        dn, rdn = M["dn"], M["rdn"]
        q.op("dve", f"rr{n}", lambda e, i: e.reciprocal(rdn[:, 0:W], dn[:, 0:W]), after=[of("den", 4, B[5]), of("rT", 5, B[5] - 1)], lag=g)
        q.op("sp", f"rT{n}", lambda e, i: e.dma_start(M["rT"][n % 2][0:H, :], rdn[:, 0:W]), after=[f"rr{n}", of("rb", 5, B[5] - 2)], channel=f"rT{n}", lag=g)

    def divide():
        n, g = n5, lag[5]
        on = M["on"][n % 2]
        q.op("pe", f"rb{n}", lambda e, i: e.matmul(M1[:, 256:512], M["hb" + A.name][0:H, :], M["rT"][n % 2][0:H, :], start=True, stop=True),
             after=[f"rT{n}", "w_w"] + bank_free(("on", 5, "")), lag=g)
        q.op("dve", f"on{n}", lambda e, i: e.tensor_tensor(on[:, :], M1[:, 256:512], on[:, :], ALU.mult),
             after=[of("num", 4, B[5]), f"rb{n}"], lag=g)

    def residual():
        n, g = n5, lag[5]
        rd, on = M["rd"], M["on"][n % 2]
        q.op("pe", f"pm{n}", lambda e, i: e.matmul(M1[:, 0:256], M["Wo" if L0 else "perm"][:, :], on[:, :], start=True, stop=True),
             after=[f"on{n}"] + bank_free(readers[-1]), lag=g)
        if L0:
            q.op("act", f"yb{n}", lambda e, i: e.activation(rd[:, :], M1[:, 0:256], ACT.Identity, bias=M["bog"][:, 0:1], scale=M["tg"][:, 0:1]),
                 after=[f"pm{n}", of("x", 5, B[5] - 1)], lag=g)
            q.op("dve", f"x{n}", lambda e, i: e.tensor_tensor(x_at(i, B[5]), x_at(i, B[5]), rd[:, :], ALU.add), after=[f"yb{n}"], lag=g)
        else:
            q.op("dve", f"x{n}", lambda e, i: e.scalar_tensor_tensor(
                out=x_at(i, B[5]), in0=M1[:, 0:256], scalar=M["tg"][:, 2:3], in1=x_at(i, B[5]), op0=ALU.mult, op1=ALU.add), after=[f"pm{n}"], lag=g)

    n_pairs = H // 2
    if not L0:
        norm()
        gather()
    keys_in()
    for m in range(n_pairs):
        for u in range(2):
            score(2 * m + u)
            score_t(m, u)
            place = 2 * m + u if n_pairs == 4 else m if u else None
            if place == 0:
                maxima(1)
                if L0:
                    norm()
                reciprocals()
                spread(slice(0, 2 if L0 else 6))
            if place == 1:
                values(NQ - 1)
                norm2()
                heads_out()
                spread(slice(2, 4) if L0 else slice(0))
            if place == 2:
                values_in()
                spread(slice(4, 6) if L0 else slice(0))
            if place == (3 if L0 else 1):
                project()
            if place == 4:
                maxima(0)
                project2()
            if place == 5:
                divide()
            if place == 6:
                residual()
        if m % 2 == 1 and m >= 3:
            values(m // 2 - 1)
    at[f"st.done{n3}"] = at[f"st{hb * n_pairs + n_pairs - 1}.11"]
    if not L0:
        combine()



GB = 4
NGRP = NB // GB


def layer_norm_batches(q, M, BK, pre):
    Xb = lambda i, b: M["X"][:, bass.ds((i + 1) * GB + b, 1), :][:, 0, :]
    Nb = lambda i, b: M["XN"][:, bass.ds((i + 1) * GB + b, 1), :][:, 0, :]
    st, mv = M["st4"], M["mv4"]
    op = lambda *args, **kw: q.op(*args, lag=-1, **kw)
    for b in range(GB):
        op("dve", f"bn{b}", lambda e, i, b=b: e.bn_stats(st[:, b, :], Xb(i, b)), after=[("xn3", 1)])
    for b in range(GB):
        op("dve", f"bna{b}", lambda e, i, b=b: e.bn_aggr(mv[:, b, :], st[:, b, :]), after=[f"bn{b}"], apart=True)
    op("dve", "ve", lambda e, i: e.tensor_scalar(M["ve4"][:, :], mv[:, :, 1], EPS, None, ALU.add), after=["bna3"])
    op("pool", "rs", lambda e, i: e.tensor_tensor(M["rs4"][:, :], M["ve4"][:, :], M["mhalf4"][:, :], ALU.pow), after=["ve", ("xn3", 1)])
    for b in range(GB):
        op("dve", f"xn{b}", lambda e, i, b=b: e.tensor_scalar(
            Nb(i, b), Xb(i, b), mv[:, b, 0:1], M["rs4"][:, b:b + 1], ALU.subtract, ALU.mult), after=["rs"] + (["w_z"] if pre == "L0" else []))


def transposes(q, M, BK):
    normed = "xn0" in q.phases[-1]["at"]
    Nb = lambda i, b: M["XN"][:, bass.ds((i + 1) * GB + b, 1), :][:, 0, :]
    op = lambda *args, **kw: q.op(*args, lag=-1, **kw)
    for b in range(GB):
        op("act", f"xc{b}", lambda e, i, b=b: e.activation(M["XC"][b % 2][:, :], Nb(i, b), ACT.Copy),
           after=[f"xn{b}"] * normed + [(f"tp{b - 2}.1", 0) if b >= 2 else (f"tp{b + 2}.1", 1)])
        for a in range(2):
            op("pe", f"tp{b}.{a}", lambda e, i, b=b, a=a: e.transpose(
                BK[a][:, 128 * b:128 * b + 128], M["XC"][b % 2][:, 128 * a:128 * a + 128], M["ident"][:, :]),
                after=[f"xc{b}", f"xt{a}"])


def tokens_in(q, M, BK):
    q.op("act", "xt0", lambda e, i: e.activation(M["XT"][:, 0, :], BK[0][:, :], ACT.Copy), after=[("tp3.0", 1), ("xt.read", 1)])
    q.op("dve", "xt1", lambda e, i: e.tensor_copy(M["XT"][:, 1, :], BK[1][:, :]), after=[("tp3.1", 1), ("xt.read", 1)])


def tokens(M, b, a):
    return M["XT"][:, a, 128 * b:128 * b + 128]


def logits0(q, M, BK):
    tokens_in(q, M, BK)
    at = q.phases[-1]["at"]
    L = BK[2]
    for b in range(GB):
        for a in range(2):
            q.op("pe", f"lg{b}.{a}", lambda e, i, b=b, a=a: e.matmul(
                L[:, E0 * b:E0 * b + E0], tokens(M, b, a), M["GW"][:, a, :], start=(a == 0), stop=(a == 1)),
                after=["xt0", "xt1", ("lgc", 1), "w_f0"])
    at["xt.read"] = at["lg3.1"]
    layer_norm_batches(q, M, BK, "L0")
    q.op("dve", "lgc", lambda e, i: e.tensor_copy(
        M["LG"][:, bass.ds(i * GB, GB), :], L[:, 0:GB * E0].rearrange("p (b e) -> p b e", b=GB)), after=["lg3.1"])
    transposes(q, M, BK)


def shared0(q, M, BK):
    tokens_in(q, M, BK)
    at = q.phases[-1]["at"]
    for c in range(4):
        U = BK[3 + c % 2]
        for a in range(2):
            q.op("pe", f"up{c}.{a}", lambda e, i, c=c, a=a, U=U: e.matmul(
                U[:, :], M["SU"][:, a, 128 * c:128 * c + 128], M["XT"][:, a, :], start=(a == 0), stop=(a == 1)),
                after=["xt0", "xt1", (f"relu{c - 2}", 0) if c >= 2 else (f"relu{c + 2}", 1), "w_s0"])
        q.op("act", f"relu{c}", lambda e, i, c=c, U=U: e.activation(M["RL"][:, c, :], U[:, :], ACT.Relu), after=[f"up{c}.1", ("dn3.3", 1)])
        q.op("dve", f"sq{c}", lambda e, i, c=c: e.tensor_tensor(M["RL"][:, c, :], M["RL"][:, c, :], M["RL"][:, c, :], ALU.mult), after=[f"relu{c}"])
    at["xt.read"] = at["up3.1"]
    transposes(q, M, BK)
    for b in range(GB):
        D = BK[5 + b % 2]
        for c in range(4):
            q.op("pe", f"dn{b}.{c}", lambda e, i, b=b, c=c, D=D: e.matmul(
                D[:, 0:256], M["RL"][:, c, 128 * b:128 * b + 128], M["SD"][:, c, :], start=(c == 0), stop=(c == 3)),
                after=["sq3", (f"xs{b - 2}", 0) if b >= 2 else (f"xs{b + 2}", 1), "w_s0"])
        X = lambda i, b=b: M["X"][:, bass.ds(i * GB + b, 1), :][:, 0, :]
        q.op("dve", f"xs{b}", lambda e, i, X=X, D=D: e.scalar_tensor_tensor(
            out=X(i), in0=D[:, 0:256], scalar=M["tg"][:, 1:2], in1=X(i), op0=ALU.mult, op1=ALU.add), after=[f"dn{b}.3"])


def chain(q, engine, steps, first=()):
    prev = list(first)
    for name, fn in steps:
        q.op(engine, name, lambda e, i, fn=fn: fn(e), after=prev)
        prev = [name]


def route0(q, M, BK):
    G, K = 8, K0
    LG = M["LG"]
    sc, sb, t = M["sc"], M["scb"], M["rt"]
    flat = lambda ap: ap[:, :, :].rearrange("p b e -> p (b e)")
    q.op("act", "sig", lambda e, i: e.activation(flat(sc), flat(LG), ACT.Sigmoid))
    bias = M["bc"][:, :].unsqueeze(1).to_broadcast([P, NB, E0])
    v4 = sb[:, :, :].rearrange("p b (g m) -> p (b g) m", m=4)
    hi1, lo1, hi2, lo2, gs = (t[k] for k in range(5))
    g3 = lambda ap: ap[:, :].rearrange("p (b g) -> p b g", g=G)
    other = g3(gs).unsqueeze(2).to_broadcast([P, NB, G, G])
    own = g3(gs).unsqueeze(3).to_broadcast([P, NB, G, G])
    lt = M["lt"][:, :, :].unsqueeze(1).to_broadcast([P, NB, G, G])
    big0, big1, oh = M["big0"], M["big1"], M["oh"]
    gg = lambda m: m[:, 0:NB * G * G].rearrange("p (b g h) -> p b g h", g=G, h=G)
    gg3 = lambda m: m[:, 0:NB * G * G].rearrange("p (x h) -> p x h", h=G)
    ke = lambda m: m[:, :].rearrange("p (b k e) -> p b k e", k=K, e=E0)
    TT = lambda o, a, b, op: (lambda e: e.tensor_tensor(o, a, b, op))
    chain(q, "dve", [
        ("bias", TT(sb[:, :, :], sc[:, :, :], bias, ALU.add)),
        ("hi1", TT(hi1[:, :], v4[:, :, 0], v4[:, :, 1], ALU.max)),
        ("lo1", TT(lo1[:, :], v4[:, :, 0], v4[:, :, 1], ALU.min)),
        ("hi2", TT(hi2[:, :], v4[:, :, 2], v4[:, :, 3], ALU.max)),
        ("lo2", TT(lo2[:, :], v4[:, :, 2], v4[:, :, 3], ALU.min)),
        ("lo", TT(lo1[:, :], lo1[:, :], lo2[:, :], ALU.max)),
        ("mid", TT(lo2[:, :], hi1[:, :], hi2[:, :], ALU.min)),
        ("second", TT(lo1[:, :], lo1[:, :], lo2[:, :], ALU.max)),
        ("first", TT(hi1[:, :], hi1[:, :], hi2[:, :], ALU.max)),
        ("gs", TT(gs[:, :], hi1[:, :], lo1[:, :], ALU.add)),
        ("eq", TT(gg(big0), other, own, ALU.is_equal)),
        ("eqlt", TT(gg(big0), gg(big0), lt, ALU.mult)),
        ("gt", TT(gg(big1), other, own, ALU.is_gt)),
        ("ahead", TT(gg(big0), gg(big0), gg(big1), ALU.add)),
        ("rank", lambda e: e.tensor_reduce(hi1[:, :], gg3(big0), AX.X, ALU.add)),
        ("gm", lambda e: e.tensor_scalar(hi1[:, :], hi1[:, :], 4.0, None, ALU.is_lt)),
        ("masked", TT(v4, v4, hi1[:, :].unsqueeze(2).to_broadcast([P, NB * G, 4]), ALU.mult)),
        ("masked0", lambda e: e.tensor_scalar(flat(sb), flat(sb), 0.0, None, ALU.add)),
    ], ["sig", "w_f0"])
    for b in range(NB):
        q.op("dve", f"top{b}", lambda e, i, b=b: e.max(M["MV"][:, b, :], sb[:, b, :]), after=["masked0"])
    for b in range(NB):
        q.op("dve", f"idx{b}", lambda e, i, b=b: e.max_index(M["MI"][:, b, :], M["MV"][:, b, :], sb[:, b, :]), after=[f"top{b}"])
    idxf, w, pk, val, f0, f1 = (M["tk"][k] for k in range(6))
    io = M["iota"][:, :].unsqueeze(1).unsqueeze(1).to_broadcast([P, NB, K, E0])
    x4 = lambda m: m[:, :, :].unsqueeze(3).to_broadcast([P, NB, K, E0])
    xe = lambda m: m[:, :, :].unsqueeze(2).to_broadcast([P, NB, K, E0])
    red = lambda o, m: (lambda e: e.tensor_reduce(o[:, :, :], ke(m), AX.X, ALU.add))
    chain(q, "dve", [
        ("idxf", lambda e: e.tensor_copy(idxf[:, :, :], M["MI"][:, :, 0:K])),
        ("oh", TT(ke(oh), x4(idxf), io, ALU.is_equal)),
        ("A", lambda e: e.tensor_reduce(M["A"][:, :, :], oh[:, :].rearrange("p (b k e) -> p b e k", k=K, e=E0), AX.X, ALU.add)),
        ("C0", lambda e: e.memset(M["C"][:, 0, :], 0.0)),
    ] + [(f"C{b}", TT(M["C"][:, b, :], M["C"][:, b - 1, :], M["A"][:, b - 1, :], ALU.add)) for b in range(1, NB)], [f"idx{NB - 1}", "w_f0"])
    q.op("pe", "pos0", lambda e, i: e.matmul(BK[0][:, :], M["before"][:, :], flat(M["A"]), start=True, stop=False), after=["A", "w_f0"])
    q.op("pe", "pos1", lambda e, i: e.matmul(BK[0][:, :], M["ones"][:, :], flat(M["C"]), start=False, stop=True), after=[f"C{NB - 1}"])
    pos = M["pos"]
    chain(q, "dve", [
        ("posc", lambda e: e.tensor_copy(flat(pos), BK[0][:, :])),
        ("pp", TT(ke(big1), ke(oh), xe(pos), ALU.mult)),
        ("pk", red(pk, big1)),
        ("val", lambda e: e.tensor_scalar(val[:, :, :], pk[:, :, :], float(CAP), None, ALU.is_lt)),
        ("e128", lambda e: e.tensor_scalar(idxf[:, :, :], idxf[:, :, :], float(CAP), None, ALU.mult)),
        ("out", lambda e: e.tensor_scalar(f0[:, :, :], val[:, :, :], -2.0 * E0 * CAP, 2.0 * E0 * CAP, ALU.mult, ALU.add)),
        ("s0", TT(f0[:, :, :], f0[:, :, :], idxf[:, :, :], ALU.add)),
        ("s1", TT(f0[:, :, :], f0[:, :, :], pk[:, :, :], ALU.add)),
        ("si", lambda e: e.tensor_copy(M["SI"][:, :, :], f0[:, :, :])),
        ("wp", TT(ke(big1), ke(oh), xe(sc), ALU.mult)),
        ("w", red(w, big1)),
        ("g0", lambda e: e.tensor_scalar(f1[:, :, :], pk[:, :, :], float(CAP - 1), None, ALU.min)),
        ("g1", TT(f1[:, :, :], f1[:, :, :], idxf[:, :, :], ALU.add)),
        ("gi", lambda e: e.tensor_copy(M["GI"][:, :, :], f1[:, :, :])),
        ("ws", lambda e: e.tensor_reduce(M["ws"][:, :], w[:, :, :], AX.X, ALU.add)),
        ("we", lambda e: e.tensor_scalar(M["ws"][:, :], M["ws"][:, :], 1e-20, None, ALU.add)),
        ("wr", lambda e: e.reciprocal(M["ws"][:, :], M["ws"][:, :])),
        ("wn", TT(w[:, :, :], w[:, :, :], M["ws"][:, :].unsqueeze(2).to_broadcast([P, NB, K]), ALU.mult)),
        ("wv", TT(w[:, :, :], w[:, :, :], val[:, :, :], ALU.mult)),
        ("wg", lambda e: e.tensor_scalar(M["wr"][:, :, :], w[:, :, :], M["tg"][:, 1:2], 2.5, ALU.mult, ALU.mult)),
    ], [f"C{NB - 1}", "pos1"])
    for b in range(NB):
        for k in range(K):
            q.op("pool", f"sc{b}.{k}", lambda e, i, b=b, k=k: e.indirect_dma_start(
                out=M["xe_d"], out_offset=bass.IndirectOffsetOnAxis(ap=M["SI"][:, b, k:k + 1], axis=0),
                in_=M["XN"][:, b, :], in_offset=None, bounds_check=E0 * CAP - 1, oob_is_err=False),
                after=["si", "w_z"], channel="w_scat")


def experts0(q, M, BK):
    U = 4
    at = q.phases[-1]["at"]
    for u in range(U):
        def w(e, i, u=u):
            return e.dma_start(M["EW"][u][:, :], M["ew_d"][bass.ds(i * U + u + U, 1), :, :].rearrange("o p c -> (o p) c"))
        def x(e, i, u=u):
            return e.dma_start(M["XE"][u][:, :], M["xe_d"][bass.ds((i * U + u + U) * CAP, CAP), :])
        q.op("sp", f"ldx{u}", x, after=[(f"et{u}.1", 0), "w_scat"], lag=-1, channel=f"ldx{u}", apart=True)
        q.op("sp", f"ldw{u}", w, after=[(f"ed{u}", 0)], lag=-1, channel=f"ldw{u}", apart=True)
        q.op("sp", f"sty{u}", lambda e, i, u=u: e.dma_start(M["ye_d"][bass.ds((i * U + u) * CAP, CAP), :], M["YE"][u][:, :]),
             after=[f"ey{u}"], channel=f"sty{u}", apart=True)
    def tokens_of(u):
        v = u % 2
        for a in range(2):
            q.op("pe", f"et{u}.{a}", lambda e, i, u=u, a=a, v=v: e.transpose(
                BK[v][:, 128 * a:128 * a + 128], M["XE"][u][:, 128 * a:128 * a + 128], M["ident"][:, :]),
                after=[(f"ldx{u}", 1), (f"ex{u - 2}", 0) if u >= 2 else (f"ex{u + 2}", 1)])
        q.op("act", f"ex{u}", lambda e, i, v=v: e.activation(M["XeT"][v][:, :], BK[v][:, 0:256], ACT.Copy),
             after=[f"et{u}.1", (f"eu{u - 2}.1", 0) if u >= 2 else (f"eu{u + 2}.1", 1)])

    def up(u):
        v = u % 2
        for a in range(2):
            q.op("pe", f"eu{u}.{a}", lambda e, i, u=u, a=a, v=v: e.matmul(
                BK[2 + v][:, 0:128], M["EW"][u][:, 128 * a:128 * a + 128], M["XeT"][v][:, 128 * a:128 * a + 128],
                start=(a == 0), stop=(a == 1)),
                after=[f"ex{u}", (f"ldw{u}", 1), (f"er{u - 2}", 0) if u >= 2 else (f"er{u + 2}", 1)])
        q.op("act", f"er{u}", lambda e, i, v=v: e.activation(M["EH"][v][:, :], BK[2 + v][:, 0:128], ACT.Relu),
             after=[f"eu{u}.1", (f"ed{u - 2}", 0) if u >= 2 else (f"ed{u + 2}", 1)])
        q.op("dve", f"es{u}", lambda e, i, v=v: e.tensor_tensor(M["EH"][v][:, :], M["EH"][v][:, :], M["EH"][v][:, :], ALU.mult), after=[f"er{u}"])

    def down(u):
        v = u % 2
        q.op("pe", f"ed{u}", lambda e, i, u=u, v=v: e.matmul(
            BK[4 + v][:, 0:256], M["EH"][v][:, :], M["EW"][u][:, 256:512], start=True, stop=True),
            after=[f"es{u}", (f"ey{u - 2}", 0) if u >= 2 else (f"ey{u + 2}", 1)])
        q.op("dve", f"ey{u}", lambda e, i, u=u, v=v: e.tensor_copy(M["YE"][u][:, :], BK[4 + v][:, 0:256]), after=[f"ed{u}", (f"sty{u}", 1)])

    for u in range(U + 2):
        if u < U:
            tokens_of(u)
        if 0 <= u - 1 < U:
            up(u - 1)
        if u >= 2:
            down(u - 2)


def ffn1(q, M, BK, out):
    tokens_in(q, M, BK)
    at = q.phases[-1]["at"]
    L = BK[2]
    for b in range(GB):
        for a in range(2):
            q.op("pe", f"lg{b}.{a}", lambda e, i, b=b, a=a: e.matmul(
                L[:, E1 * b:E1 * b + E1], tokens(M, b, a), M["GW1"][:, a, :], start=(a == 0), stop=(a == 1)),
                after=["xt0", "xt1", ("fx34", 1), "w_f0"])
    r = M["r1"]
    s = M["s1"]
    lc, p, m0, m1 = r[0], r[1], r[2], r[3]
    bc = lambda m: m[:, :].unsqueeze(2).to_broadcast([P, GB, E1])
    other = lambda m: m[:, :, :].unsqueeze(2).to_broadcast([P, GB, E1, E1])
    own = lambda m: m[:, :, :].unsqueeze(3).to_broadcast([P, GB, E1, E1])
    lt = M["lt"][:, :, :].unsqueeze(1).to_broadcast([P, GB, E1, E1])
    W = GB * E1 * E1
    gg = lambda m: m[:, 0:W].rearrange("p (b g h) -> p b g h", g=E1, h=E1)
    gg3 = lambda m: m[:, 0:W].rearrange("p (x h) -> p x h", h=E1)
    fl = lambda m: m[:, :, :].rearrange("p b e -> p (b e)")
    chain_steps = []

    def weights(count):
        for _ in range(min(count, len(chain_steps))):
            chain_steps.pop(0)()

    chain_steps.append(lambda: q.op("dve", "lc", lambda e, i: e.tensor_copy(fl(lc), L[:, 0:GB * E1]), after=["lg3.1"]))
    chain_steps.append(lambda: q.op("dve", "mx", lambda e, i: e.tensor_reduce(s[0][:, :], lc[:, :, :], AX.X, ALU.max), after=["lc"]))
    chain_steps.append(lambda: q.op("dve", "sm", lambda e, i: e.tensor_tensor(lc[:, :, :], lc[:, :, :], bc(s[0]), ALU.subtract), after=["mx"]))
    chain_steps.append(lambda: q.op("act", "ex", lambda e, i: e.activation(fl(p), fl(lc), ACT.Exp), after=["sm", ("wc", 1)]))
    steps = [
        ("su", lambda e: e.tensor_reduce(s[1][:, :], p[:, :, :], AX.X, ALU.add)),
        ("ri", lambda e: e.reciprocal(s[1][:, :], s[1][:, :])),
        ("pr", lambda e: e.tensor_tensor(p[:, :, :], p[:, :, :], bc(s[1]), ALU.mult)),
        ("eq", lambda e: e.tensor_tensor(gg(M["big0"]), other(p), own(p), ALU.is_equal)),
        ("el", lambda e: e.tensor_tensor(gg(M["big0"]), gg(M["big0"]), lt, ALU.mult)),
        ("gt", lambda e: e.tensor_tensor(gg(M["big1"]), other(p), own(p), ALU.is_gt)),
        ("ah", lambda e: e.tensor_tensor(gg(M["big0"]), gg(M["big0"]), gg(M["big1"]), ALU.add)),
        ("rk", lambda e: e.tensor_reduce(fl(m0), gg3(M["big0"]), AX.X, ALU.add)),
        ("se", lambda e: e.tensor_scalar(fl(m0), fl(m0), 2.0, None, ALU.is_lt)),
        ("ps", lambda e: e.tensor_tensor(m1[:, :, :], m0[:, :, :], p[:, :, :], ALU.mult)),
        ("sw", lambda e: e.tensor_reduce(s[2][:, :], m1[:, :, :], AX.X, ALU.add)),
        ("sa", lambda e: e.tensor_scalar(s[2][:, :], s[2][:, :], 1e-20, None, ALU.add)),
        ("sr", lambda e: e.reciprocal(s[2][:, :], s[2][:, :])),
        ("wn", lambda e: e.tensor_tensor(m1[:, :, :], m1[:, :, :], bc(s[2]), ALU.mult)),
        ("wc", lambda e: e.tensor_scalar(M["CW"][:, :, :], m1[:, :, :], M["tg"][:, 3:4], None, ALU.mult)),
    ]
    prev = ["ex"]
    for name, fn in steps:
        chain_steps.append(lambda name=name, fn=fn, prev=prev: q.op(
            "dve", name, lambda e, i: fn(e), after=prev + ([("lastx", 1)] if name == "wc" else [])))
        prev = [name]
    work = [("S", 0, [(0, 128), (128, 128), (256, 96)])] + [("E", x, [(0, 128), (256, 112)]) for x in range(E1)]
    n_chunks = sum(len(c) for _, _, c in work)
    firsts = [sum(len(c) for _, _, c in work[:k]) for k in range(len(work))]

    def back(kind, n, depth):
        return (f"{kind}{n - depth}", 0) if n >= depth else (f"{kind}{max(m for m in range(n_chunks) if m % depth == n)}", 1)

    def rows_of(kind, k, size):
        return slice(64, 112) if (kind, k) == ("E", 1) else slice(0, size)

    def hidden(item):
        kind, x, chunks = work[item]
        for k, (lo, size) in enumerate(chunks):
            n = firsts[item] + k
            slot, gate, up = n % 4, BK[3 + 2 * (n % 2)], BK[4 + 2 * (n % 2)]
            joint = (kind, k) == ("E", 1)
            for w in "g" if joint else "gu":
                for a in range(2):
                    if kind == "S":
                        src = M["SG" if w == "g" else "SP"][:, a, lo:lo + size]
                    else:
                        c0 = lo + (128 if w == "u" else 0)
                        src = M["EGU"][:, x, a, c0:c0 + size]
                    q.op("pe", f"{w}{n}.{a}", lambda e, i, src=src, a=a, bank=gate if w == "g" else up, size=size: e.matmul(
                        bank[0:size, :], src, M["XT"][:, a, :], start=(a == 0), stop=(a == 1)),
                        after=["xt0", "xt1", back("hu", n, 2), "w_f1"])
            h = M["RL"][rows_of(kind, k, size), slot, :]
            q.op("act", f"si{n}", lambda e, i, h=h, gate=gate, m=48 if joint else size: e.activation(h, gate[0:m, :], ACT.Silu),
                 after=[f"g{n}.1", back("dr", n, 4)])
            u = gate[64:112, :] if joint else up[0:size, :]
            q.op("dve", f"hu{n}", lambda e, i, h=h, u=u: e.tensor_tensor(h, u, h, ALU.mult),
                 after=[f"si{n}", f"g{n}.1" if joint else f"u{n}.1"])
            weights(2)
        at["xt.read"] = at[f"g{n}.1"] if joint else at[f"u{n}.1"]

    def down(item):
        kind, x, chunks = work[item]
        for b in range(GB):
            nd = item * GB + b
            D = BK[7 if nd % 2 else 2]
            for k, (lo, size) in enumerate(chunks):
                slot = (firsts[item] + k) % 4
                rows = rows_of(kind, k, size)
                src = M["SDn"][rows, k, :] if kind == "S" else M["ED"][rows, x, k, :]
                q.op("pe", f"fd{nd}.{k}", lambda e, i, D=D, slot=slot, rows=rows, b=b, src=src, k=k, last=len(chunks) - 1: e.matmul(
                    D[:, 0:256], M["RL"][rows, slot, 128 * b:128 * b + 128], src, start=(k == 0), stop=(k == last)),
                    after=[f"hu{firsts[item] + len(chunks) - 1}", "lc", (f"fx{nd - 2}", 0) if nd >= 2 else (f"fx{GB * len(work) - 2 + nd}", 1), "w_f1"])
            sc = M["tg"][:, 3:4] if kind == "S" else M["CW"][:, b, x:x + 1]
            X = lambda i, b=b: M["X"][:, bass.ds(i * GB + b, 1), :][:, 0, :]
            q.op("dve", f"fx{nd}", lambda e, i, D=D, sc=sc, X=X: e.scalar_tensor_tensor(
                out=X(i), in0=D[:, 0:256], scalar=sc, in1=X(i), op0=ALU.mult, op1=ALU.add),
                after=[f"fd{nd}.{len(chunks) - 1}"] + (["wc"] if kind == "E" else []) + ([f"fx{nd - 4}"] if nd >= 4 else []))
            weights(2)
        for k in range(len(chunks)):
            at[f"dr{firsts[item] + k}"] = at[f"fd{nd}.{len(chunks) - 1}"]

    hidden(0)
    for item in range(1, len(work)):
        if len(work[item - 1][2]) + len(work[item][2]) > 4:
            down(item - 1)
            hidden(item)
        else:
            hidden(item)
            down(item - 1)
        if item == 4:
            layer_norm_batches(q, M, BK, "L1")
        if item == 6:
            transposes(q, M, BK)
    down(len(work) - 1)
    at["lastx"] = at[f"fx{GB * len(work) - 1}"]
    q.op("sp", "store", lambda e, i: e.dma_start(out[:, bass.ds(i * GB, GB), :], M["X"][:, bass.ds(i * GB, GB), :]),
         after=["lastx"], channel="st", apart=True)




def build(nc, d, out):
    ctx = ExitStack()
    with ctx:
        sb = lambda name, shape, dt=F32: ctx.enter_context(nc.sbuf_tensor(name, shape, dt))
        q = Queue(nc, ctx)
        for e in ENGINES[:4]:
            q.channel(e)
        M = {}
        X = M["X"] = sb("X", [P, NB, T])
        for nm in ("Wq", "Wk", "Wv", "Wo"):
            M[nm] = sb(nm, [P, P])
        for nm in ("bq", "bk", "bo"):
            M[nm] = sb(nm, [P, 1])
        M["bv"] = sb("bv", [P, P])
        M["ident"] = sb("ident", [P, P]); M["perm"] = sb("perm", [P, P])
        M["dn"] = sb("dn", [P, 32]); M["rdn"] = sb("rdn", [P, 32]); M["bog"] = sb("bog", [P, 1])
        M["tg"] = sb("tg", [P, 4]); M["graw"] = sb("graw", [P, 5])
        M["mhalf"] = sb("mhalf", [P, 1])
        for nm, shape, dt in (("VA", [P, 2, 16, 32], F32), ("QKc", [P, 2, T], F32), ("QKs", [P, 3, 2, T], BF16),
                               ("st6", [P, 6], F32), ("mv", [P, 2], F32),
                              ("ve", [P, 1], F32), ("rs", [P, 1], F32), ("mx", [P, 2, 16], F32), ("mxT", [8, 2, T], BF16)):
            M[nm] = [sb(f"{nm}{n}", shape, dt) for n in range(2)]
        M["Cb"] = [sb(f"Cb{n}", [P, T]) for n in range(U)]
        M["Xn"] = sb("Xn", [P, T]); M["OS"] = sb("OS", [P, 4, T]); M["rd"] = sb("rd", [P, T]); M["on"] = [sb(f"on{n}", [P, T]) for n in range(2)]
        PXs = sb("PX", [P, 4, 1024])
        M["PX"] = [PXs[:, n, :] for n in range(4)]
        M["big0"], M["big1"] = (PXs[:, 2 * n:2 * n + 2, :].rearrange("p a c -> p (a c)") for n in range(2))
        M["QS"] = [sb(f"QS{n}", [P, 16, 2, T], BF16)[:, :, :, :] for n in range(2)]
        spare = sb("spare", [P, 8192])
        M["XN"], M["oh"] = spare[:, 0:4096].rearrange("p (b t) -> p b t", b=NB), spare[:, 4096:6144]
        for k, nm in enumerate(("sc", "scb", "A", "C")):
            M[nm] = spare[:, 6144 + 512 * k:6656 + 512 * k].rearrange("p (b e) -> p b e", b=NB)
        for nm, shape, dt in (("st4", [P, GB, 6], F32), ("mv4", [P, GB, 2], F32), ("ve4", [P, GB], F32),
                              ("rs4", [P, GB], F32), ("mhalf4", [P, GB], F32), ("XT", [P, 2, 512], F32), ("GW", [P, 2, E0], F32),
                              ("SU", [P, 2, HS], F32), ("SD", [P, 4, T], F32), ("RL", [P, 4, 512], F32),
                              ("lt", [P, 8, 8], F32),
                              ("bc", [P, E0], F32), ("iota", [P, E0], F32),
                              ("before", [P, P], F32), ("ones", [P, P], F32), ("SI", [P, NB, K0], U32), ("GI", [P, NB, K0], U32),
                              ("GIf0", [P, K0], U32), ("GIf1", [P, K0], U32), ("wrf0", [P, K0], F32), ("wrf1", [P, K0], F32), ("ws", [P, NB], F32), ("wr", [P, NB, K0], F32), ("CW", [P, GB, E1], F32), ("GW1", [P, 2, E1], F32),
                              ("SG", [P, 2, ISH], F32), ("SP", [P, 2, ISH], F32), ("SDn", [P, 3, T], F32),
                              ("EGU", [P, E1, 2, 368], F32), ("ED", [P, E1, 2, T], F32)):
            M[nm] = sb(nm, shape, dt)
        for nm, n, shape in (("r1", 4, [P, GB, E1]), ("s1", 3, [P, GB])):
            M[nm] = [sb(f"{nm}{k}", shape) for k in range(n)]
        M["QS"] += [spare[:, 4096 * n:4096 * n + 4096].bitcast(BF16).rearrange("p (g s t) -> p g s t", g=16, s=2)
                    for n in range(2)]
        M["XC"] = [M["Xn"], M["rd"]]
        M["LG"] = PXs[:, 3, 0:512].rearrange("p (b e) -> p b e", b=NB)
        for nm in ("GIf", "wrf"):
            M[nm] = [M[nm + "0"], M[nm + "1"]]
        M["XeT"] = M["Cb"]
        M["EH"] = [M["on"][k][:, 0:P] for k in range(2)]
        M["MV"] = M["RL"][:, 1, 128:256].rearrange("p (b e) -> p b e", b=NB)
        M["MI"] = M["RL"][:, 1, 256:384].bitcast(U32).rearrange("p (b e) -> p b e", b=NB)
        M["tk"] = [M["RL"][:, 3, 128 + 64 * k:192 + 64 * k].rearrange("p (b e) -> p b e", b=NB) for k in range(6)]
        M["pos"] = M["RL"][:, 2, :].rearrange("p (b e) -> p b e", b=NB)
        M["rt"] = [M["RL"][:, k % 4, P * (k // 4):P * (k // 4) + P] for k in range(5)]
        M["EW"] = [M["RL"][:, k, :] for k in range(4)]
        M["XE"] = [M["OS"][:, k, :] for k in range(4)]
        M["YE"] = [M["QKc"][k // 2][:, k % 2, :] for k in range(4)]
        M["GA"] = [M["SD"][:, k, :] for k in range(4)] + [M["SU"][:, k // 2, T * (k % 2):T * (k % 2) + T] for k in range(4)]
        M["xe_d"] = nc.dram_tensor("xe", [E0 * CAP, T], F32, kind="Internal").ap()
        M["ye_d"] = nc.dram_tensor("ye", [E0 * CAP, T], F32, kind="Internal").ap()
        M["ew_d"] = d["ew"]
        ps = lambda name, w=512: ctx.enter_context(nc.psum_tensor(name, [P, w], F32))
        M["S"] = [ps("S0"), ps("S1")]; M["ST"] = [ps(f"ST{n}", 1024) for n in range(2)]
        M["O"] = ps("O"); M["M1"] = ps("M1")
        ST = M["ST"]
        BK = [M["S"][0][:, :], M["S"][1][:, :]] + [ST[n][:, 512 * k:512 * k + 512] for n in range(2) for k in range(2)] + [M["O"][:, :], M["M1"][:, :]]
        M["ctx_d"] = d["ctx"].rearrange("b c t -> c b t")

        q.phase()
        def ld(dst, src, ch="w_w", engine="sp"):
            q.op(engine, f"ld.{len(q.phases[-1]['at'])}", lambda e, i: e.dma_start(dst, src), channel=ch)

        M["hbL0"] = sb("hbL0", [16, P]); M["hbL1"] = sb("hbL1", [8, P]); M["rT"] = [sb(f"rT{n}", [16, T]) for n in range(2)]
        x_in = d["x"].rearrange("b c t -> c b t")
        ld(X[:, 0:U, :], x_in[:, 0:U, :], "w_x")
        ld(M["graw"][:, :], d["graw"].to_broadcast([P, 5]), "w_g")
        for nm in ("Wq", "Wk", "bq", "bk", "Wv", "ident"):
            ld(M[nm][:, :], d[nm])
        ld(M["bv"][:, :], d["bv"].to_broadcast([P, P]))
        for nm in ("hbL0", "Wo", "bo", "hbL1", "perm"):
            ld(M[nm][:, :], d[nm])
        ld(X[:, U:NB, :], x_in[:, U:NB, :], "w_x2", "act")
        ones2 = float(np.array([0x3F803F80], np.uint32).view(np.float32)[0])
        for n in range(U):
            q.op("pool", f"zero.QS{n}", lambda e, i, n=n: e.memset(M["QS"][n].rearrange("p h s t -> p (h s t)").bitcast(F32), 0.0))
        for n in range(2):
            q.op("dve", f"one.VA{n}", lambda e, i, n=n: e.memset(M["VA"][n][:, :, :, :], 1.0))
        for n in range(U):
            q.op("dve", f"one.QS{n}", lambda e, i, n=n: e.memset(M["QS"][n][STACK:STACK + 1, :, 1, :].bitcast(F32), ones2), after=[f"zero.QS{n}"])
        everything = lambda m: m[tuple(slice(None) for _ in m.shape)]
        for nm, ch in (("GW", "w_f0"), ("SU", "w_s0"), ("SD", "w_s0"), ("lt", "w_f0"), ("before", "w_f0"), ("GW1", "w_f0")):
            ld(everything(M[nm]), d[nm], ch, "act")
        for nm in ("bc", "iota"):
            ld(M[nm][:, :], d[nm].to_broadcast([P, E0]), "w_f0", "act")
        q.op("dve", "ones", lambda e, i: e.memset(M["ones"][:, :], 1.0))
        q.op("dve", "mhalf4", lambda e, i: e.memset(M["mhalf4"][:, :], -0.5))
        q.op("dve", "mhalf", lambda e, i: e.memset(M["mhalf"][:, :], -0.5))
        q.op("act", "gates", lambda e, i: e.activation(M["tg"][:, :], M["graw"][:, 0:4], ACT.Tanh), after=["w_g"])
        q.op("dve", "gamma", lambda e, i: e.tensor_tensor(M["tg"][:, 2:3], M["tg"][:, 2:3], M["graw"][:, 4:5], ALU.mult), after=["gates"])
        q.op("dve", "bog", lambda e, i: e.tensor_tensor(M["bog"][:, :], M["bo"][:, :], M["tg"][:, 0:1], ALU.mult), after=["gates", "w_w"])

        q.phase(NB // U)
        A = Attention("L0", 16, 8)
        for hb in range(U):
            attention_step(q, A, M, hb)

        q.phase()
        q.op("dve", "zero", lambda e, i: e.memset(M["OS"][:, 0:2, :], 0.0))
        q.op("sp", "z", lambda e, i: e.dma_start(
            M["xe_d"].rearrange("(p b c) t -> p b (c t)", p=P, c=2),
            M["OS"][:, 0:2, :].rearrange("p a t -> p (a t)").unsqueeze(1).to_broadcast([P, 16, 512])), after=["zero"], channel="w_z")
        q.phase(NGRP)
        logits0(q, M, BK)
        q.phase()
        route0(q, M, BK)
        for nm in ("SG", "SP", "SDn", "EGU", "ED"):
            ld(everything(M[nm]), d[nm], "w_f1")
        q.phase(NGRP)
        shared0(q, M, BK)
        q.phase(E0 // 4)
        experts0(q, M, BK)
        q.phase()
        for n in (2, 3):
            q.op("dve", f"one.QS{n}", lambda e, i, n=n: e.memset(M["QS"][n][STACK:STACK + 1, :, 1, :], 1.0))
        q.phase(NB // U)
        A = Attention("L1", 8, 16)
        for hb in range(U):
            attention_step(q, A, M, hb)
        q.phase(NGRP)
        ffn1(q, M, BK, out.rearrange("b c t -> c b t"))

        q.emit()


def orders():
    p = np.arange(128)
    head = lambda k, NQ: NQ * (k % 4) + k // 4
    cx = 16 * head(p % 8, 2) + p // 8
    cq = 8 * head(p % 16, 4) + p // 16
    cv = 8 * (4 * (p // 32) + p % 4) + p % 32 // 4
    cw = 16 * (2 * (p // 32) + p % 2) + p % 32 // 2
    return cx, cq, cv, cw


def layout(inp):
    a = {k: np.asarray(v) for k, v in inp.items()}
    cx, cq, cv, cw = orders()
    d = {"x": a["x"][:, cx, :], "ctx": a["ctx_2048"][:, cx, :]}
    for n in "qkv":
        d["W" + n] = a["L0_xattn_W" + n][cv if n == "v" else cq][:, cx].T
    d["Wo"] = a["L0_xattn_Wo"][cx][:, cv].T
    for n in "qk":
        d["b" + n] = a["L0_xattn_b" + n][cq].reshape(128, 1)
    d["bv"] = a["L0_xattn_bv"][cv].reshape(1, 128)
    d["perm"] = np.equal(cw[:, None], cx[None, :]).astype(np.float32)
    d["bo"] = a["L0_xattn_bo"][cx].reshape(128, 1)
    d["graw"] = np.stack([a["g_xattn"][0], a["g_ffn"][0], a["g_xattn"][1], a["g_ffn"][1], a["L1_xattn_gamma"]]).reshape(1, 5)
    d["ident"] = np.eye(128, dtype=np.float32)
    for nm, G, R in (("hbL0", 4, 8), ("hbL1", 2, 16)):
        s = d[nm] = np.zeros((4 * G, 128), np.float32)
        for j in range(4):
            for i in range(R):
                for g in range(G):
                    s[G * j + g, 32 * j + G * i + g] = 1
    up, down = a["L0_ffn_up_w"], a["L0_ffn_down_w"]
    d["ew"] = np.concatenate([up.transpose(0, 2, 1)[:, 0:128], up.transpose(0, 2, 1)[:, 128:256], down.transpose(0, 2, 1)], axis=2)
    halves = lambda w: w.T.reshape(2, 128, -1).transpose(1, 0, 2)
    d["GW"], d["GW1"], d["SU"] = halves(a["L0_ffn_gate_w"]), halves(a["L1_ffn_gate_w"]), halves(a["L0_ffn_shared_up_w"])
    d["SG"], d["SP"] = halves(a["L1_ffn_shared_gate"]), halves(a["L1_ffn_shared_up"])
    d["SD"] = a["L0_ffn_shared_down_w"].T.reshape(4, 128, 256).transpose(1, 0, 2)
    d["SDn"] = np.zeros((3, 128, 256), np.float32)
    d["SDn"].reshape(384, 256)[0:352] = a["L1_ffn_shared_down"].T
    d["SDn"] = d["SDn"].transpose(1, 0, 2)
    g, u = (a["L1_ffn_expert_" + w].transpose(2, 0, 1).reshape(2, 128, 8, 176).transpose(1, 2, 0, 3) for w in ("gate", "up"))
    d["EGU"] = np.concatenate([g[..., 0:128], u[..., 0:128], g[..., 128:176], np.zeros((128, 8, 2, 16), np.float32), u[..., 128:176]], axis=3)
    down = a["L1_ffn_expert_down"].transpose(2, 0, 1)
    d["ED"] = np.zeros((128, 8, 2, 256), np.float32)
    d["ED"][:, :, 0] = down[0:128]
    d["ED"][64:112, :, 1] = down[128:176]
    d["lt"] = np.broadcast_to(np.tril(np.ones((8, 8), np.float32), -1), (128, 8, 8))
    d["iota"] = np.arange(32, dtype=np.float32).reshape(1, 32)
    d["bc"] = a["L0_ffn_bias_corr"].reshape(1, 32)
    d["before"] = np.less(cx[:, None], cx[None, :]).astype(np.float32)
    return {k: np.ascontiguousarray(v) for k, v in d.items()}


def kernel(**inputs):
    import concourse.bacc as bacc
    from concourse.bass_utils import run_bass_kernel_spmd

    nc = bacc.Bacc("TRN2", target_bir_lowering=False, num_devices=1)
    arrays = {f"in_{name}": array for name, array in layout(inputs).items()}
    args = {name[3:]: nc.dram_tensor(name, a.shape, mybir.dt.from_np(a.dtype), kind="ExternalInput").ap()
            for name, a in arrays.items()}
    out = nc.dram_tensor("out", (NB, C, T), F32, kind="ExternalOutput").ap()
    build(nc, args, out)
    r = run_bass_kernel_spmd(nc, [arrays], core_ids=[0])
    got = r.results[0]["out"]
    cx = orders()[0]
    inverse = [int(np.nonzero(cx == c)[0][0]) for c in range(C)]
    return got[:, inverse, :]
```
